# Optimizing a Trainium2 kernel written in Bass

```python
import numpy as np
import jax
import jax.numpy as jnp

def _softmax(x, axis=-1):
    return jax.nn.softmax(x, axis=axis)

def _gelu(x):
    return jax.nn.gelu(x, approximate=True)

def _silu(x):
    return jax.nn.silu(x)

def _sigmoid(x):
    return jax.nn.sigmoid(x)

def _layernorm(x, axis=-1, eps=1e-05):
    m = jnp.mean(x, axis=axis, keepdims=True)
    v = jnp.var(x, axis=axis, keepdims=True)
    return (x - m) / jnp.sqrt(v + eps)

def _scatter_add(tgt, idx, src, axis=0):
    return tgt.at[idx].add(src)

def _segment_sum(src, seg, n):
    return jax.ops.segment_sum(src, seg, n)
kernel_name = 'mk_gps_d1_gnn_r8_5402db'

def setup_inputs(seed: int=0):
    np.random.seed(seed)
    _w = jnp.asarray

    def _rec_inputs():
        import jax
        import jax.numpy as jnp
        _gk = jax.random.key(seed)
        x = -6.415e-05 + 1 * jax.random.normal(jax.random.fold_in(_gk, 1), (1250, 512), jnp.float32)
        src = jax.random.randint(jax.random.fold_in(_gk, 2), (20000,), 0, 1250, jnp.int32)
        dst = jnp.minimum((1250 * jax.random.uniform(jax.random.fold_in(_gk, 3), (20000,)) ** 2.0).astype(jnp.int32), 9999)
        _o = jnp.argsort(dst, stable=True)
        src = src[_o]
        dst = dst[_o]
        edge_attr_4 = 0.000126197 + 0.999763 * jax.random.normal(jax.random.fold_in(_gk, 11), (20000, 4), jnp.float32)
        return (x, src, dst, edge_attr_4)
    x, src, dst, edge_attr_4 = _rec_inputs()

    def _L0_gnn_setup():
        import jax, jax.numpy as jnp
        import numpy as np
        N = 2500
        E = 40000
        IN = 512
        H = 4
        C = 128
        ED = 4
        NEG_SLOPE = 0.2
        BN_EPS = 1e-05

        def _edge_gat(x, edge_index, edge_attr, W, W_edge, att_src, att_dst, att_edge, bias, gamma, beta):
            n = x.shape[0]
            loop = jnp.arange(n, dtype=edge_index.dtype)
            src = jnp.concatenate([edge_index[0], loop])
            dst = jnp.concatenate([edge_index[1], loop])
            ea = jnp.concatenate([edge_attr, jnp.broadcast_to(edge_attr.mean(0), (n, edge_attr.shape[1]))], 0)
            h = (x @ W).reshape(n, H, C)
            a_src = (h * att_src[None]).sum(-1)
            a_dst = (h * att_dst[None]).sum(-1)
            e = (ea @ W_edge).reshape(-1, H, C)
            a_edge = (e * att_edge[None]).sum(-1)
            alpha = a_src[src] + a_dst[dst] + a_edge
            alpha = jax.nn.leaky_relu(alpha, NEG_SLOPE)
            amax = jax.lax.stop_gradient(jax.ops.segment_max(alpha, dst, num_segments=n))
            ex = jnp.exp(alpha - amax[dst])
            denom = jax.ops.segment_sum(ex, dst, num_segments=n)
            att = ex / (denom[dst] + 1e-16)
            msg = h[src] * att[:, :, None]
            out = jax.ops.segment_sum(msg, dst, num_segments=n).reshape(n, H * C) + bias
            mu = out.mean(0)
            var = out.var(0)
            return (out - mu) / jnp.sqrt(var + BN_EPS) * gamma + beta
        key = jax.random.key(seed)
        ks = jax.random.split(key, 10)
        x = jax.random.normal(ks[0], (N, IN), dtype=jnp.float32)
        edge_index = jax.random.randint(ks[1], (2, E), 0, N, dtype=jnp.int64)
        edge_attr = jax.random.normal(ks[2], (E, ED), dtype=jnp.float32)
        W = jax.random.normal(ks[3], (IN, H * C), dtype=jnp.float32) / np.sqrt(IN)
        W_edge = jax.random.normal(ks[4], (ED, H * C), dtype=jnp.float32) / np.sqrt(ED)
        att_src = jax.random.normal(ks[5], (H, C), dtype=jnp.float32) / np.sqrt(C)
        att_dst = jax.random.normal(ks[6], (H, C), dtype=jnp.float32) / np.sqrt(C)
        att_edge = jax.random.normal(ks[7], (H, C), dtype=jnp.float32) / np.sqrt(C)
        bias = jnp.zeros((H * C,), dtype=jnp.float32)
        gamma = jnp.ones((H * C,), dtype=jnp.float32)
        beta = jnp.zeros((H * C,), dtype=jnp.float32)
        return {'x': x, 'edge_index': edge_index, 'edge_attr': edge_attr, 'W': W, 'W_edge': W_edge, 'att_src': att_src, 'att_dst': att_dst, 'att_edge': att_edge, 'bias': bias, 'gamma': gamma, 'beta': beta}
    _L0_gnn_all = _L0_gnn_setup()
    _L0_gnn_in = {k: v for k, v in _L0_gnn_all.items() if k in ('W', 'W_edge', 'att_src', 'att_dst', 'att_edge', 'bias', 'gamma', 'beta')}
    del _L0_gnn_all

    def _L0_mix_setup():
        import jax, jax.numpy as jnp
        import numpy as np
        D_MODEL = 512
        N_HEADS = 8
        D_HEAD = D_MODEL // N_HEADS
        EPS = 1e-06

        def _split_heads(t, B, S):
            return t.reshape(B, S, N_HEADS, D_HEAD).transpose(0, 2, 1, 3)

        def _reference_tuple_inner(x, Wq, bq, Wk, bk, Wv, bv, Wo, bo):
            B, S, _ = x.shape
            q = _split_heads(x @ Wq.T + bq, B, S)
            k = _split_heads(x @ Wk.T + bk, B, S)
            v = _split_heads(x @ Wv.T + bv, B, S)
            q = jax.nn.relu(q)
            k = jax.nn.relu(k)
            k_sum = k.sum(axis=-1, keepdims=True)
            attn = jnp.einsum('bhnd,bhmd->bhnm', q, k) / (k_sum + EPS)
            attn = jax.nn.softmax(attn, axis=-1)
            out = jnp.einsum('bhnm,bhmd->bhnd', attn, v)
            out = out.transpose(0, 2, 1, 3).reshape(B, S, D_MODEL)
            return (out @ Wo.T + bo, attn)
        key = jax.random.key(seed)
        ks = jax.random.split(key, 9)
        B, S = (2, 256)
        scale = 0.02
        x = jax.random.normal(ks[0], (B, S, D_MODEL), dtype=jnp.float32)
        Wq = jax.random.normal(ks[1], (D_MODEL, D_MODEL), dtype=jnp.float32) * scale
        Wk = jax.random.normal(ks[2], (D_MODEL, D_MODEL), dtype=jnp.float32) * scale
        Wv = jax.random.normal(ks[3], (D_MODEL, D_MODEL), dtype=jnp.float32) * scale
        Wo = jax.random.normal(ks[4], (D_MODEL, D_MODEL), dtype=jnp.float32) * scale
        bq = jax.random.normal(ks[5], (D_MODEL,), dtype=jnp.float32) * scale
        bk = jax.random.normal(ks[6], (D_MODEL,), dtype=jnp.float32) * scale
        bv = jax.random.normal(ks[7], (D_MODEL,), dtype=jnp.float32) * scale
        bo = jax.random.normal(ks[8], (D_MODEL,), dtype=jnp.float32) * scale
        return {'x': x, 'Wq': Wq, 'bq': bq, 'Wk': Wk, 'bk': bk, 'Wv': Wv, 'bv': bv, 'Wo': Wo, 'bo': bo}
    _L0_mix_all = _L0_mix_setup()
    _L0_mix_in = {k: v for k, v in _L0_mix_all.items() if k in ('Wq', 'bq', 'Wk', 'bk', 'Wv', 'bv', 'Wo', 'bo')}
    del _L0_mix_all

    def _L0_ffn_setup():
        import jax, jax.numpy as jnp
        import numpy as np
        D_IN, D_HID, E, K = (512, 256, 10, 2)
        KS = (9, 1)

        def conv1d_same(x, w, b):
            y = jax.lax.conv_general_dilated(x, w, window_strides=(1,), padding='SAME', dimension_numbers=('NCH', 'OIH', 'NCH'))
            return y + b[None, :, None]
        key = jax.random.key(seed)
        ks = jax.random.split(key, 16)
        s = 0.02
        B, T = (2, 256)
        return {'x': jax.random.normal(ks[0], (B, T, D_IN), jnp.float32), 'rc_w1': jax.random.normal(ks[1], (D_IN, D_IN, 3), jnp.float32) * s, 'rc_b1': jnp.zeros((D_IN,), jnp.float32), 'rc_w2': jax.random.normal(ks[2], (E, D_IN, 3), jnp.float32) * s, 'rc_b2': jnp.zeros((E,), jnp.float32), 'sh_w1': jax.random.normal(ks[3], (D_HID, D_IN, KS[0]), jnp.float32) * s, 'sh_b1': jnp.zeros((D_HID,), jnp.float32), 'sh_w2': jax.random.normal(ks[4], (D_IN, D_HID, KS[1]), jnp.float32) * s, 'sh_b2': jnp.zeros((D_IN,), jnp.float32), 'e_w1': jax.random.normal(ks[5], (E, D_IN, D_HID), jnp.float32) * s, 'e_b1': jnp.zeros((E, D_HID), jnp.float32), 'e_w2': jax.random.normal(ks[6], (E, D_HID, D_IN), jnp.float32) * s, 'e_b2': jnp.zeros((E, D_IN), jnp.float32), 'ln_g': jnp.ones((D_IN,), jnp.float32), 'ln_b': jnp.zeros((D_IN,), jnp.float32)}
    _L0_ffn_all = _L0_ffn_setup()
    _L0_ffn_in = {k: v for k, v in _L0_ffn_all.items() if k in ('rc_w1', 'rc_b1', 'rc_w2', 'rc_b2', 'sh_w1', 'sh_b1', 'sh_w2', 'sh_b2', 'e_w1', 'e_b1', 'e_w2', 'e_b2', 'ln_g', 'ln_b')}
    del _L0_ffn_all
    return {'x': x, 'src': src, 'dst': dst, 'edge_attr_4': edge_attr_4, 'L0_gnn_W': _L0_gnn_in['W'], 'L0_gnn_W_edge': _L0_gnn_in['W_edge'], 'L0_gnn_att_src': _L0_gnn_in['att_src'], 'L0_gnn_att_dst': _L0_gnn_in['att_dst'], 'L0_gnn_att_edge': _L0_gnn_in['att_edge'], 'L0_gnn_bias': _L0_gnn_in['bias'], 'L0_gnn_gamma': _L0_gnn_in['gamma'], 'L0_gnn_beta': _L0_gnn_in['beta'], 'L0_mix_Wq': _L0_mix_in['Wq'], 'L0_mix_bq': _L0_mix_in['bq'], 'L0_mix_Wk': _L0_mix_in['Wk'], 'L0_mix_bk': _L0_mix_in['bk'], 'L0_mix_Wv': _L0_mix_in['Wv'], 'L0_mix_bv': _L0_mix_in['bv'], 'L0_mix_Wo': _L0_mix_in['Wo'], 'L0_mix_bo': _L0_mix_in['bo'], 'L0_ffn_rc_w1': _L0_ffn_in['rc_w1'], 'L0_ffn_rc_b1': _L0_ffn_in['rc_b1'], 'L0_ffn_rc_w2': _L0_ffn_in['rc_w2'], 'L0_ffn_rc_b2': _L0_ffn_in['rc_b2'], 'L0_ffn_sh_w1': _L0_ffn_in['sh_w1'], 'L0_ffn_sh_b1': _L0_ffn_in['sh_b1'], 'L0_ffn_sh_w2': _L0_ffn_in['sh_w2'], 'L0_ffn_sh_b2': _L0_ffn_in['sh_b2'], 'L0_ffn_e_w1': _L0_ffn_in['e_w1'], 'L0_ffn_e_b1': _L0_ffn_in['e_b1'], 'L0_ffn_e_w2': _L0_ffn_in['e_w2'], 'L0_ffn_e_b2': _L0_ffn_in['e_b2'], 'L0_ffn_ln_g': _L0_ffn_in['ln_g'], 'L0_ffn_ln_b': _L0_ffn_in['ln_b']}

def reference(x, src, dst, edge_attr_4, L0_gnn_W, L0_gnn_W_edge, L0_gnn_att_src, L0_gnn_att_dst, L0_gnn_att_edge, L0_gnn_bias, L0_gnn_gamma, L0_gnn_beta, L0_mix_Wq, L0_mix_bq, L0_mix_Wk, L0_mix_bk, L0_mix_Wv, L0_mix_bv, L0_mix_Wo, L0_mix_bo, L0_ffn_rc_w1, L0_ffn_rc_b1, L0_ffn_rc_w2, L0_ffn_rc_b2, L0_ffn_sh_w1, L0_ffn_sh_b1, L0_ffn_sh_w2, L0_ffn_sh_b2, L0_ffn_e_w1, L0_ffn_e_b1, L0_ffn_e_w2, L0_ffn_e_b2, L0_ffn_ln_g, L0_ffn_ln_b):
    import jax
    import jax.numpy as jnp

    def _L0_gnn_ref(x, edge_index, edge_attr, W, W_edge, att_src, att_dst, att_edge, bias, gamma, beta):
        import jax, jax.numpy as jnp
        import numpy as np
        N = 2500
        E = 40000
        IN = 512
        H = 4
        C = 128
        ED = 4
        NEG_SLOPE = 0.2
        BN_EPS = 1e-05

        def _edge_gat(x, edge_index, edge_attr, W, W_edge, att_src, att_dst, att_edge, bias, gamma, beta):
            n = x.shape[0]
            loop = jnp.arange(n, dtype=edge_index.dtype)
            src = jnp.concatenate([edge_index[0], loop])
            dst = jnp.concatenate([edge_index[1], loop])
            ea = jnp.concatenate([edge_attr, jnp.broadcast_to(edge_attr.mean(0), (n, edge_attr.shape[1]))], 0)
            h = (x @ W).reshape(n, H, C)
            a_src = (h * att_src[None]).sum(-1)
            a_dst = (h * att_dst[None]).sum(-1)
            e = (ea @ W_edge).reshape(-1, H, C)
            a_edge = (e * att_edge[None]).sum(-1)
            alpha = a_src[src] + a_dst[dst] + a_edge
            alpha = jax.nn.leaky_relu(alpha, NEG_SLOPE)
            amax = jax.lax.stop_gradient(jax.ops.segment_max(alpha, dst, num_segments=n))
            ex = jnp.exp(alpha - amax[dst])
            denom = jax.ops.segment_sum(ex, dst, num_segments=n)
            att = ex / (denom[dst] + 1e-16)
            msg = h[src] * att[:, :, None]
            out = jax.ops.segment_sum(msg, dst, num_segments=n).reshape(n, H * C) + bias
            mu = out.mean(0)
            var = out.var(0)
            return (out - mu) / jnp.sqrt(var + BN_EPS) * gamma + beta
        return _edge_gat(x, edge_index, edge_attr, W, W_edge, att_src, att_dst, att_edge, bias, gamma, beta)

    def _L0_mix_ref(x, Wq, bq, Wk, bk, Wv, bv, Wo, bo):
        import jax, jax.numpy as jnp
        import numpy as np
        D_MODEL = 512
        N_HEADS = 8
        D_HEAD = D_MODEL // N_HEADS
        EPS = 1e-06

        def _split_heads(t, B, S):
            return t.reshape(B, S, N_HEADS, D_HEAD).transpose(0, 2, 1, 3)

        def _reference_tuple_inner(x, Wq, bq, Wk, bk, Wv, bv, Wo, bo):
            B, S, _ = x.shape
            q = _split_heads(x @ Wq.T + bq, B, S)
            k = _split_heads(x @ Wk.T + bk, B, S)
            v = _split_heads(x @ Wv.T + bv, B, S)
            q = jax.nn.relu(q)
            k = jax.nn.relu(k)
            k_sum = k.sum(axis=-1, keepdims=True)
            attn = jnp.einsum('bhnd,bhmd->bhnm', q, k) / (k_sum + EPS)
            attn = jax.nn.softmax(attn, axis=-1)
            out = jnp.einsum('bhnm,bhmd->bhnd', attn, v)
            out = out.transpose(0, 2, 1, 3).reshape(B, S, D_MODEL)
            return (out @ Wo.T + bo, attn)
        return _reference_tuple_inner(x, Wq, bq, Wk, bk, Wv, bv, Wo, bo)[0]

    def _L0_ffn_ref(x, rc_w1, rc_b1, rc_w2, rc_b2, sh_w1, sh_b1, sh_w2, sh_b2, e_w1, e_b1, e_w2, e_b2, ln_g, ln_b):
        import jax, jax.numpy as jnp
        import numpy as np
        D_IN, D_HID, E, K = (512, 256, 10, 2)
        KS = (9, 1)

        def conv1d_same(x, w, b):
            y = jax.lax.conv_general_dilated(x, w, window_strides=(1,), padding='SAME', dimension_numbers=('NCH', 'OIH', 'NCH'))
            return y + b[None, :, None]
        B, T, d = x.shape
        residual = x
        xt = jnp.transpose(x, (0, 2, 1))
        rc = conv1d_same(xt, rc_w1, rc_b1)
        rc = jax.nn.gelu(rc, approximate=False)
        rc = conv1d_same(rc, rc_w2, rc_b2)
        logits = jnp.transpose(rc, (0, 2, 1)).reshape(-1, E)
        vals, idx = jax.lax.top_k(logits, K)
        gv = jax.nn.softmax(vals, axis=-1)
        N = logits.shape[0]
        gates = jnp.zeros((N, E), x.dtype).at[jnp.arange(N)[:, None], idx].set(gv)
        x2 = x.reshape(-1, d)
        h = jnp.einsum('nd,edh->enh', x2, e_w1) + e_b1[:, None, :]
        h = jax.nn.elu(h)
        eo = jnp.einsum('enh,ehd->end', h, e_w2) + e_b2[:, None, :]
        y = jnp.einsum('end,ne->nd', eo, gates).reshape(B, T, d)
        sh = conv1d_same(xt, sh_w1, sh_b1)
        sh = jax.nn.silu(sh)
        sh = conv1d_same(sh, sh_w2, sh_b2)
        sh = jnp.transpose(sh, (0, 2, 1))
        z = residual + y + sh
        mu = jnp.mean(z, axis=-1, keepdims=True)
        var = jnp.mean(jnp.square(z - mu), axis=-1, keepdims=True)
        return (z - mu) * jax.lax.rsqrt(var + 1e-05) * ln_g + ln_b
    edge_index = jnp.stack([src, dst])
    xn = _layernorm(x, axis=-1)
    x = x + _L0_gnn_ref(xn, edge_index, edge_attr_4, L0_gnn_W, L0_gnn_W_edge, L0_gnn_att_src, L0_gnn_att_dst, L0_gnn_att_edge, L0_gnn_bias, L0_gnn_gamma, L0_gnn_beta) + _L0_mix_ref(xn[None], L0_mix_Wq, L0_mix_bq, L0_mix_Wk, L0_mix_bk, L0_mix_Wv, L0_mix_bv, L0_mix_Wo, L0_mix_bo)[0]
    x = x + _L0_ffn_ref(_layernorm(x, axis=-1)[None], L0_ffn_rc_w1, L0_ffn_rc_b1, L0_ffn_rc_w2, L0_ffn_rc_b2, L0_ffn_sh_w1, L0_ffn_sh_b1, L0_ffn_sh_w2, L0_ffn_sh_b2, L0_ffn_e_w1, L0_ffn_e_b1, L0_ffn_e_w2, L0_ffn_e_b2, L0_ffn_ln_g, L0_ffn_ln_b)[0]
    return x

_drawn_inputs = setup_inputs


def setup_inputs(seed=0):
    import zlib

    import numpy as np

    out = dict(_drawn_inputs(seed))
    spreads = {'L0_gnn_bias': (0.0, 2.0),
     'L0_gnn_gamma': (1.0, 0.2),
     'L0_gnn_beta': (0.0, 0.1),
     'L0_ffn_rc_b1': (0.0, 0.397),
     'L0_ffn_rc_b2': (0.0, 0.367),
     'L0_ffn_sh_b1': (0.0, 0.8),
     'L0_ffn_sh_b2': (0.0, 0.1),
     'L0_ffn_e_b1': (0.0, 0.8),
     'L0_ffn_e_b2': (0.0, 0.279),
     'L0_ffn_ln_g': (1.0, 0.2),
     'L0_ffn_ln_b': (0.0, 0.1)}
    factors = {'L0_mix_Wq': 8.0,
     'L0_mix_bq': 34.925,
     'L0_mix_Wk': 8.0,
     'L0_mix_bk': 32.038,
     'L0_mix_Wv': 8.0,
     'L0_mix_bv': 7.963,
     'L0_mix_Wo': 6.987,
     'L0_mix_bo': 3.884}
    for name, (base, spread) in spreads.items():
        noise = np.random.default_rng([zlib.crc32(name.encode()), seed]).standard_normal(out[name].shape)
        drawn = base * np.exp(spread * noise) if base else spread * noise
        out[name] = jnp.asarray(drawn.astype(out[name].dtype))
    for name, factor in factors.items():
        out[name] = (out[name] * factor).astype(out[name].dtype)
    return out
```

```python
from contextlib import ExitStack

import concourse.bass as bass
from concourse import mybir

F32 = mybir.dt.float32
F32R = mybir.dt.float32r
I32 = mybir.dt.int32
ALU = mybir.AluOpType
ACT = mybir.ActivationFunctionType
AX = mybir.AxisListType

P = 128
N = 1250
D = 512
KT = D // P
NT = -(-N // P)
NP = NT * P
LAST = N - (NT - 1) * P
SPANS = [(0, 512), (512, 512), (1024, N - 1024)]
FULL_SPANS = [(0, 512), (512, 512), (1024, NP - 1024)]

E = 20000
EC = -(-E // P)
CH = EC + NT + 1
assert CH % 4 == 0
GH, GC = 4, 128
SLOPE = 0.2
BN_EPS = LN_EPS = 1e-5
MH, MD = 8, 64
MIX_EPS = 1e-6
XE, HID = 10, 256
HT = HID // P
RC_TAPS, SH_TAPS = 3, 9
PAD = SH_TAPS // 2
NEG = -3.0e38
SKIP = 1.0e6


class Steps:

    def __init__(self, eng, sem):
        self.eng, self.sem, self.done = eng, sem, 0

    def __call__(self, ins):
        self.done = self.done + 1
        ins.then_inc(self.sem, 1)
        self.eng.wait_ge(self.sem, self.done)


def rows(t):
    return P if t < NT - 1 else LAST


def layer(nc, a, out):
    ctx = ExitStack()

    def dram(name, shape, dt=F32):
        return nc.dram_tensor(name, shape, dt).ap()

    feature_table = dram("feature_table", [NP, D])
    source_table = dram("source_table", [NP, GH])
    target_table = dram("target_table", [NP, 2 * GH])
    max_table = dram("max_table", [NP * CH, GH])
    SLOTS = 4
    sums_table = [dram(f"sums_table{k}", [NP, D + GH]) for k in range(SLOTS)]

    with ctx:
        def keep(name, shape, dt=F32):
            return ctx.enter_context(nc.sbuf_tensor(name, shape, dt))

        ident = keep("ident", [P, P])
        ones = keep("ones", [P, P])
        x1 = keep("x1", [P, NT, D])
        a_dst = keep("a_dst", [P, NT, GH])
        eps_ln = keep("eps_ln", [P, 1])

        mix = ExitStack()
        ctx.enter_context(mix)

        def mkeep(name, shape, dt=F32):
            return mix.enter_context(nc.sbuf_tensor(name, shape, dt))

        q_t = mkeep("q_t", [P, KT, NP])
        k_t = mkeep("k_t", [P, KT, NP])
        v_tok = mkeep("v_tok", [P, NT, D])
        with ExitStack() as s:
            def sb(name, shape, dt=F32):
                return s.enter_context(nc.sbuf_tensor(name, shape, dt))

            def sem(name):
                return s.enter_context(nc.semaphore(name))

            xn_t = sb("xn_t", [P, KT, NP])
            w_gat = sb("w_gat", [P, KT, D])
            w_att = sb("w_att", [P, KT, 2 * GH])
            att = sb("att", [P, 2, D])
            w_q = sb("w_q", [P, KT, D])
            w_k = sb("w_k", [P, KT, D])
            w_v = sb("w_v", [P, KT, D])
            b_qk = sb("b_qk", [P, 2, KT])
            b_v = sb("b_v", [P, D])
            xn = sb("xn", [P, 2, D])
            junk = sb("junk", [P, GC])
            stats = sb("stats", [P, 6])
            mv = sb("mv", [P, NT, 2])
            std = sb("std", [P, NT])
            rstd = sb("rstd", [P, NT])
            row = sb("row", [P, 2, D + GH])
            ksum = sb("ksum", [P, 2, 512])
            pair_ones = sb("pair_ones", [P, P])
            ps = [s.enter_context(nc.psum_tensor(f"ps{b}", [P, 512], F32)) for b in range(8)]
            s_x = sem("x_loaded")
            s_const = sem("constants_ready")
            s_zero = sem("x_padded")
            s_w = sem("weights_loaded")
            s_wq = sem("qkv_weights_loaded")
            s_stat = sem("variance_ready")
            s_std = sem("deviation_ready")
            s_xn = sem("xn_ready")
            s_tr = sem("xn_transposed")
            s_xt = sem("xn_t_ready")
            s_watt = sem("w_att_ready")
            s_h = sem("h_ready")
            s_row_h = sem("h_row_features_ready")
            s_row_a = sem("h_row_logits_ready")
            s_tab = [sem(f"h_row_{b}_stored") for b in range(2)]
            s_qk = sem("qk_ready")
            s_qk_out = sem("qk_copied")
            s_v = sem("v_ready")
            s_v_out = sem("v_copied")
            s_ks = sem("ksum_ready")
            s_ks_out = sem("q_scaled")
            s_d = sem("dve_steps")
            s_p = sem("pool_steps")

            with nc.Block() as block:
                @block.sync
                def _(sp):
                    sp.dma_start(x1[:, 0:NT - 1, :], a["x"][0:(NT - 1) * P, :].rearrange("(t p) d -> p t d", p=P)).then_inc(s_x, 16)
                    sp.wait_ge(s_zero, 1)
                    sp.dma_start(x1[0:LAST, NT - 1, :], a["x"][(NT - 1) * P:N, :]).then_inc(s_x, 16)
                    sp.dma_start(w_gat[:], a["gat_w"].rearrange("(k p) o -> p k o", p=P)).then_inc(s_w, 16)
                    sp.dma_start(att[:, 0, :], a["att_src"].rearrange("h c -> (h c)").partition_broadcast(P)).then_inc(s_w, 16)
                    sp.dma_start(att[:, 1, :], a["att_dst"].rearrange("h c -> (h c)").partition_broadcast(P)).then_inc(s_w, 16)
                    for w, name in ((w_q, "wq_t"), (w_k, "wk_t"), (w_v, "wv_t")):
                        sp.dma_start(w[:], a[name].rearrange("(k p) o -> p k o", p=P)).then_inc(s_wq, 16)
                    with nc.allow_non_contiguous_dma(reason="biases of 512 numbers, one for a partition"):
                        sp.dma_start(b_qk[:, 0, :], a["bq"].rearrange("(k p) -> p k", p=P)).then_inc(s_wq, 16)
                        sp.dma_start(b_qk[:, 1, :], a["bk"].rearrange("(k p) -> p k", p=P)).then_inc(s_wq, 16)
                    sp.dma_start(b_v[:], a["bv"].partition_broadcast(P)).then_inc(s_wq, 16)
                    for t in range(NT):
                        sp.wait_ge(s_row_h, t + 1)
                        sp.dma_start(feature_table[t * P:(t + 1) * P, :], row[:, t % 2, 0:D]).then_inc(s_tab[t % 2], 16)
                        sp.wait_ge(s_row_a, t + 1)
                        sp.dma_start(source_table[t * P:(t + 1) * P, :], row[:, t % 2, D:D + GH]).then_inc(s_tab[t % 2], 16)
                    for b in range(2):
                        sp.wait_ge(s_tab[b], 32 * NT // 2)

                @block.gpsimd
                def _(pool):
                    step = Steps(pool, s_p)
                    pool.memset(x1[:, NT - 1, :], 0.0).then_inc(s_zero, 1)
                    pool.memset(eps_ln[:], LN_EPS).then_inc(s_const, 1)
                    step(pool.memset(ones[:], 1.0))
                    step(pool.memset(ident[:], 0.0))
                    step(pool.memset(pair_ones[:], 0.0))
                    step(pool.memset(pair_ones[0:MD, 0:MD], 1.0))
                    step(pool.memset(pair_ones[MD:P, MD:P], 1.0))
                    pool.affine_select(out=ident[:], in_=ident[:], compare_op=ALU.not_equal, fill=1.0, base=0,
                                       pattern=[[-1, P]], channel_multiplier=1).then_inc(s_const, 1)

                @block.vector
                def _(dve):
                    step = Steps(dve, s_d)
                    dve.wait_ge(s_x, 32)
                    for t in range(NT):
                        step(dve.bn_stats(stats[:], x1[:, t, :]))
                        ins = dve.bn_aggr(mv[:, t, :], stats[:])
                        if t == NT - 1:
                            ins.then_inc(s_stat, 1)
                        else:
                            step(ins)
                    dve.wait_ge(s_w, 48)
                    for k in range(KT):
                        for j in range(2):
                            for h in range(GH):
                                cols = slice(h * GC, (h + 1) * GC)
                                step(dve.tensor_tensor_reduce(out=junk[:], in0=w_gat[:, k, cols], in1=att[:, j, cols],
                                                              scale=1.0, scalar=0.0, op0=ALU.mult, op1=ALU.add,
                                                              accum_out=w_att[:, k, j * GH + h:j * GH + h + 1]))
                    dve.wait_ge(s_std, 1)
                    step(dve.reciprocal(rstd[:], std[:]))
                    for t in range(NT):
                        if t >= 2:
                            dve.wait_ge(s_tr, t - 1)
                        dve.tensor_scalar(xn[:, t % 2, :], x1[:, t, :], mv[:, t, 0:1], rstd[:, t:t + 1],
                                          ALU.subtract, ALU.mult).then_inc(s_xn, 1)
                        if t >= 1:
                            dve.wait_ge(s_tr, t)
                            dve.tensor_copy(xn_t[:, :, (t - 1) * P:t * P],
                                            ps[(t - 1) % 2][:].rearrange("p (k n) -> p k n", k=KT)).then_inc(s_xt, 1)
                    dve.wait_ge(s_tr, NT)
                    dve.tensor_copy(xn_t[:, :, (NT - 1) * P:NT * P],
                                    ps[(NT - 1) % 2][:].rearrange("p (k n) -> p k n", k=KT)).then_inc(s_xt, 1)
                    for t in range(NT):
                        dve.wait_ge(s_h, t + 1)
                        if t >= 2:
                            dve.wait_ge(s_tab[t % 2], 32 * (t // 2))
                        dve.tensor_copy(a_dst[:, t, :], ps[4 + t % 2][:, GH:2 * GH])
                        dve.tensor_copy(row[:, t % 2, D:D + GH], ps[4 + t % 2][:, 0:GH]).then_inc(s_row_a, 1)
                    for t in range(NT):
                        dve.wait_ge(s_v, t + 1)
                        dve.tensor_tensor(v_tok[:, t, :], ps[6 + t % 2][:], b_v[:], ALU.add).then_inc(s_v_out, 1)
                    for m in range(KT):
                        for j, (at, n) in enumerate(FULL_SPANS):
                            i = m * len(SPANS) + j
                            dve.wait_ge(s_ks, i + 1)
                            step(dve.tensor_scalar(ksum[:, i % 2, 0:n], ps[4 + i % 2][:, 0:n], MIX_EPS, None, ALU.add))
                            step(dve.reciprocal(ksum[:, i % 2, 0:n], ksum[:, i % 2, 0:n]))
                            dve.tensor_tensor(q_t[:, m, at:at + n], q_t[:, m, at:at + n], ksum[:, i % 2, 0:n],
                                              ALU.mult).then_inc(s_ks_out, 1)

                @block.scalar
                def _(act):
                    act.wait_ge(s_stat, 1)
                    act.wait_ge(s_const, 2)
                    act.activation(std[:], mv[:, :, 1], ACT.Sqrt, bias=eps_ln[:]).then_inc(s_std, 1)
                    for t in range(NT):
                        act.wait_ge(s_h, t + 1)
                        if t >= 2:
                            act.wait_ge(s_tab[t % 2], 32 * (t // 2))
                        act.copy(row[:, t % 2, 0:D], ps[2 + t % 2][:]).then_inc(s_row_h, 1)
                    act.wait_ge(s_wq, 96)
                    i = 0
                    for j, dst in enumerate((q_t, k_t)):
                        for m in range(KT):
                            for at, n in FULL_SPANS:
                                act.wait_ge(s_qk, i + 1)
                                act.activation(dst[:, m, at:at + n], ps[i % 2][:, 0:n], ACT.Relu,
                                               bias=b_qk[:, j, m:m + 1]).then_inc(s_qk_out, 1)
                                i += 1

                @block.tensor
                def _(pe):
                    pe.wait_ge(s_const, 2)
                    for t in range(NT):
                        pe.wait_ge(s_xn, t + 1)
                        if t >= 2:
                            pe.wait_ge(s_xt, t - 1)
                        for k in range(KT):
                            ins = pe.transpose(ps[t % 2][:, k * P:(k + 1) * P], xn[:, t % 2, k * P:(k + 1) * P], ident[:])
                        ins.then_inc(s_tr, 1)
                    pe.wait_ge(s_xt, NT)
                    pe.wait_ge(s_d, 2 * NT - 1 + 2 * GH * KT)
                    for t in range(NT):
                        if t >= 2:
                            pe.wait_ge(s_row_h, t - 1)
                            pe.wait_ge(s_row_a, t - 1)
                        for k in range(KT):
                            pe.matmul(ps[2 + t % 2][:], xn_t[:, k, t * P:(t + 1) * P], w_gat[:, k, :],
                                      start=(k == 0), stop=(k == KT - 1))
                        for k in range(KT):
                            ins = pe.matmul(ps[4 + t % 2][:, 0:2 * GH], xn_t[:, k, t * P:(t + 1) * P], w_att[:, k, :],
                                            start=(k == 0), stop=(k == KT - 1))
                        ins.then_inc(s_h, 1)
                    pe.wait_ge(s_wq, 96)
                    for t in range(NT):
                        if t >= 2:
                            pe.wait_ge(s_v_out, t - 1)
                        for k in range(KT):
                            ins = pe.matmul(ps[6 + t % 2][:], xn_t[:, k, t * P:(t + 1) * P], w_v[:, k, :],
                                            start=(k == 0), stop=(k == KT - 1))
                        ins.then_inc(s_v, 1)
                    i = 0
                    for w in (w_q, w_k):
                        for m in range(KT):
                            for at, n in FULL_SPANS:
                                if i >= 2:
                                    pe.wait_ge(s_qk_out, i - 1)
                                for k in range(KT):
                                    ins = pe.matmul(ps[i % 2][:, 0:n], w[:, k, m * P:(m + 1) * P], xn_t[:, k, at:at + n],
                                                    start=(k == 0), stop=(k == KT - 1))
                                ins.then_inc(s_qk, 1)
                                i += 1
                    pe.wait_ge(s_qk_out, i)
                    pe.wait_ge(s_row_a, NT)
                    for m in range(KT):
                        for j, (at, n) in enumerate(FULL_SPANS):
                            i = m * len(SPANS) + j
                            if i >= 2:
                                pe.wait_ge(s_ks_out, i - 1)
                            pe.matmul(ps[4 + i % 2][:, 0:n], pair_ones[:], k_t[:, m, at:at + n],
                                      start=True, stop=True).then_inc(s_ks, 1)

        att_out = mkeep("att_out", [P, KT, NP])
        with ExitStack() as s:
            def sb(name, shape, dt=F32):
                return s.enter_context(nc.sbuf_tensor(name, shape, dt))

            def sem(name):
                return s.enter_context(nc.semaphore(name))

            q_now = [sb(f"q_now{b}", [MD + 1, NP]) for b in range(2)]
            k_now = [sb(f"k_now{b}", [MD + 1, N]) for b in range(2)]
            v_now = [sb(f"v_now{b}", [P, NT, 2 * MD]) for b in range(2)]
            q_round = sb("q_round", [MD, NP], F32R)
            k_round = sb("k_round", [MD, N], F32R)
            prob = sb("prob", [P, 2, 512])
            neg_max = [sb(f"neg_max{b}", [P, NT]) for b in range(2)]
            raw = sb("raw", [P, NP])
            inv = sb("inv", [MD, NP])
            logits_nm = s.enter_context(nc.psum_tensor("logits_nm", [P, 3 * 512], F32))
            logits_mn = [s.enter_context(nc.psum_tensor(f"logits_mn{b}", [P, 512], F32)) for b in range(2)]
            summed = s.enter_context(nc.psum_tensor("summed", [P, 3 * 512], F32))
            s_one = sem("constant_columns_ready")
            s_stage = [sem(f"head_{b}_staged") for b in range(2)]
            s_round = sem("qk_rounded")
            s_nm = sem("logits_nm_ready")
            s_max = sem("tile_max_ready")
            s_row = sem("max_row_ready")
            s_rowc = sem("max_row_copied")
            s_mn = sem("logits_mn_ready")
            s_pr = sem("prob_ready")
            s_pv = sem("prob_used")
            s_raw = sem("sums_copied")
            s_inv = sem("inverse_ready")
            s_att = sem("head_done")
            UNITS = [(m, j) for m in range(NT) for j in range(3)]
            NU = len(UNITS)
            MAX_AFTER = [1, 4, 7, 10, 13, 16, 19, 21, 23, 25]
            ROW_AFTER = 28

            with nc.Block() as block:
                def heads(eng, body):
                    with eng.Fori(0, MH // 2 - 1) as u:
                        for b in range(2):
                            body(u * 2 + b, b, True)
                    for b in range(2):
                        body(MH - 2 + b, b, b == 0)

                @block.sync
                def _(sp):
                    def stage(b, m):
                        lo = b * MD
                        sp.dma_start(q_now[b][0:MD, :], q_t[lo:lo + MD, bass.ds(m, 1), :]).then_inc(s_stage[b], 16)
                        sp.dma_start(k_now[b][0:MD, :], k_t[lo:lo + MD, bass.ds(m, 1), 0:N]).then_inc(s_stage[b], 16)
                        sp.dma_start(v_now[b][:, :, 0:MD], v_tok[:, :, bass.ds((m * 2 + b) * MD, MD)]).then_inc(s_stage[b], 16)

                    for b in range(2):
                        stage(b, 0)
                    with sp.Fori(1, MH // 2) as m:
                        for b in range(2):
                            sp.wait_ge(s_raw, m * 2 + (b - 1))
                            stage(b, m)

                @block.tensor
                def _(pe):
                    def tile_logits(t, h):
                        pe.wait_ge(s_max, h * NT + t)
                        for at, n in SPANS:
                            ins = pe.matmul(logits_nm[:, at:at + n], q_round[:, t * P:(t + 1) * P], k_round[:, at:at + n],
                                            start=True, stop=True)
                        ins.then_inc(s_nm, 1)

                    def max_row(h, b):
                        pe.wait_ge(s_max, (h + 1) * NT)
                        for t in range(NT):
                            ins = pe.matmul(logits_nm[0:1, t * P:(t + 1) * P], neg_max[b][:, t:t + 1], ident[:],
                                            start=True, stop=True)
                        ins.then_inc(s_row, 1)

                    def score(h, b, u):
                        m, j = UNITS[u]
                        at, n = FULL_SPANS[j]
                        i = h * NU + u
                        if u > 1:
                            pe.wait_ge(s_pr, i - 1)
                        pe.matmul(logits_mn[u % 2][0:rows(m), 0:n], k_now[b][:, m * P:m * P + rows(m)], q_now[b][:, at:at + n],
                                  start=True, stop=True).then_inc(s_mn, 1)

                    def product(h, b, u):
                        m, j = UNITS[u]
                        at, n = FULL_SPANS[j]
                        pe.wait_ge(s_pr, h * NU + u + 1)
                        pe.matmul(summed[:, at:at + n], v_now[b][0:rows(m), m, :], prob[0:rows(m), u % 2, 0:n],
                                  start=(m == 0), stop=(m == NT - 1)).then_inc(s_pv, 1)

                    def head(h, b, more):
                        pe.wait_ge(s_rowc, h + 1)
                        score(h, b, 0)
                        pe.wait_ge(s_raw, h)
                        if more:
                            pe.wait_ge(s_round, 2 * h + 4)
                        for u in range(NU):
                            if u + 1 < NU:
                                score(h, b, u + 1)
                            if more and u == ROW_AFTER:
                                max_row(h + 1, 1 - b)
                            product(h, b, u)
                            if more and u in MAX_AFTER:
                                tile_logits(MAX_AFTER.index(u), h + 1)

                    pe.wait_ge(s_one, 4)
                    pe.wait_ge(s_stage[0], 48)
                    pe.wait_ge(s_round, 2)
                    for t in range(NT):
                        tile_logits(t, 0)
                    max_row(0, 0)
                    heads(pe, head)

                @block.vector
                def _(dve):
                    def maxima(h, b, turn):
                        dve.wait_ge(s_stage[b], turn * 48 + 48)
                        if not (isinstance(h, int) and h == 0):
                            dve.wait_ge(s_nm, h * NT)
                        dve.tensor_copy(q_round[:], q_now[b][0:MD, :]).then_inc(s_round, 1)
                        dve.tensor_copy(k_round[:], k_now[b][0:MD, :]).then_inc(s_round, 1)
                        for t in range(NT):
                            dve.wait_ge(s_nm, h * NT + t + 1)
                            dve.tensor_reduce(neg_max[b][:, t:t + 1], logits_nm[:, 0:N], AX.X, ALU.max,
                                              negate=True).then_inc(s_max, 1)

                    def finish(h, b, m):
                        dve.wait_ge(s_raw, h + 1)
                        dve.reciprocal(inv[:], raw[MD:P, :]).then_inc(s_inv, 1)
                        dve.wait_ge(s_inv, h + 1)
                        dve.tensor_tensor(att_out[b * MD:(b + 1) * MD, bass.ds(m, 1), :], raw[0:MD, :], inv[:],
                                          ALU.mult).then_inc(s_att, 1)

                    for b in range(2):
                        dve.memset(k_now[b][MD:MD + 1, :], 1.0).then_inc(s_one, 1)
                        dve.memset(v_now[b][:, :, MD:2 * MD], 1.0).then_inc(s_one, 1)
                    maxima(0, 0, 0)
                    with dve.Fori(0, MH // 2 - 1) as u:
                        maxima(u * 2 + 1, 1, u)
                        finish(u * 2, 0, u)
                        maxima(u * 2 + 2, 0, u + 1)
                        finish(u * 2 + 1, 1, u)
                    maxima(MH - 1, 1, MH // 2 - 1)
                    finish(MH - 2, 0, MH // 2 - 1)
                    finish(MH - 1, 1, MH // 2 - 1)

                @block.scalar
                def _(act):
                    def row(h, b):
                        act.wait_ge(s_row, h + 1)
                        act.copy(q_now[b][MD:MD + 1, :], logits_nm[0:1, 0:NP]).then_inc(s_rowc, 1)

                    def head(h, b, more):
                        for u in range(NU):
                            m, j = UNITS[u]
                            n = FULL_SPANS[j][1]
                            if u > 1:
                                act.wait_ge(s_pv, h * NU + u - 1)
                            act.wait_ge(s_mn, h * NU + u + 1)
                            act.activation(prob[0:rows(m), u % 2, 0:n], logits_mn[u % 2][0:rows(m), 0:n], ACT.Exp).then_inc(s_pr, 1)
                        if more:
                            row(h + 1, 1 - b)
                        act.wait_ge(s_att, h)
                        act.wait_ge(s_pv, h * NU + NU)
                        act.copy(raw[:], summed[:, 0:NP]).then_inc(s_raw, 1)

                    row(0, 0)
                    heads(act, head)

        with ExitStack() as s:
            def sb(name, shape, dt=F32):
                return s.enter_context(nc.sbuf_tensor(name, shape, dt))

            def sem(name):
                return s.enter_context(nc.semaphore(name))

            w_o = sb("w_o", [P, KT, D])
            b_o = sb("b_o", [P, D])
            ps = [s.enter_context(nc.psum_tensor(f"mo{b}", [P, 512], F32)) for b in range(2)]
            s_w = sem("wo_loaded")
            s_m = sem("mixed")
            s_x = sem("mix_added")
            s_b = sem("bias_added")
            with nc.Block() as block:
                @block.sync
                def _(sp):
                    sp.dma_start(w_o[:], a["wo_t"].rearrange("(k p) o -> p k o", p=P)).then_inc(s_w, 16)
                    sp.dma_start(b_o[:], a["bo"].partition_broadcast(P)).then_inc(s_w, 16)

                @block.tensor
                def _(pe):
                    pe.wait_ge(s_w, 32)
                    for t in range(NT):
                        if t >= 2:
                            pe.wait_ge(s_x, t - 1)
                        for k in range(KT):
                            ins = pe.matmul(ps[t % 2][:], att_out[:, k, t * P:(t + 1) * P], w_o[:, k, :],
                                            start=(k == 0), stop=(k == KT - 1))
                        ins.then_inc(s_m, 1)

                @block.vector
                def _(dve):
                    dve.wait_ge(s_w, 32)
                    for t in range(NT):
                        dve.tensor_tensor(x1[:, t, :], x1[:, t, :], b_o[:], ALU.add).then_inc(s_b, 1)
                    for t in range(NT):
                        dve.wait_ge(s_b, t + 1)
                        dve.wait_ge(s_m, t + 1)
                        dve.tensor_tensor(x1[:, t, :], x1[:, t, :], ps[t % 2][:], ALU.add).then_inc(s_x, 1)
        mix.close()

        gat = ExitStack()
        ctx.enter_context(gat)

        def gkeep(name, shape, dt=F32):
            return gat.enter_context(nc.sbuf_tensor(name, shape, dt))

        src_i = gkeep("src_i", [P, CH], I32)
        dst_i = gkeep("dst_i", [P, CH], I32)
        dst_row = gkeep("dst_row", [P, CH * P], I32)
        dst_f = gkeep("dst_f", [P, CH])
        logit = gkeep("logit", [P, CH, GH])
        row_idx = gkeep("row_idx", [P, CH], I32)

        with ExitStack() as s:
            def sb(name, shape, dt=F32):
                return s.enter_context(nc.sbuf_tensor(name, shape, dt))

            def sem(name):
                return s.enter_context(nc.semaphore(name))

            SL = 4
            attr = sb("attr", [P, EC, 4])
            w_edge = sb("w_edge", [P, 4, D])
            att_edge = sb("att_edge", [P, D])
            v_edge = sb("v_edge", [P, 4, GH])
            mean = sb("mean", [P, 4])
            key = sb("key", [P, CH])
            key_i = sb("key_i", [P, CH], I32)
            chunk_i = sb("chunk_i", [P, CH], I32)
            before = sb("before", [P, P])
            low = sb("low", [P, 2240])
            src_now = [sb(f"src_now{k}", [P, 1], I32) for k in range(SL)]
            source_now = [sb(f"source_now{k}", [P, GH]) for k in range(SL)]
            logit_now = [sb(f"logit_now{k}", [P, GH]) for k in range(SL)]
            other = [sb(f"other{k}", [P, P]) for k in range(SL)]
            earlier = [sb(f"earlier{k}", [P, 1]) for k in range(SL)]
            scratch_f = [sb(f"scratch_f{k}", [P, P]) for k in range(SL)]
            scratch_m = [sb(f"scratch_m{k}", [P, GH, P]) for k in range(SL)]
            max_now = [sb(f"max_now{k}", [P, GH]) for k in range(SL)]
            key_now = [sb(f"key_now{k}", [P, 1], I32) for k in range(SL)]
            spread = [s.enter_context(nc.psum_tensor(f"spread{k}", [P, GH, P], F32)) for k in range(SL)]
            sums = s.enter_context(nc.psum_tensor("sums", [P, 4], F32))
            s_in = sem("edges_loaded")
            s_low = sem("low_ready")
            s_init = sem("max_table_initialised")
            s_iota = sem("chunk_numbers_ready")
            s_part = sem("attribute_sums_ready")
            s_mean = sem("attribute_mean_ready")
            s_prep = sem("edge_logits_ready")
            s_got = [sem(f"source_{k}_gathered") for k in range(SL)]
            s_first = sem("first_edges_found")
            s_rows = sem("row_numbers_ready")
            s_lg = sem("logits_ready")
            s_lc = sem("logits_kept")
            s_sp = sem("logits_spread")
            s_mx = sem("maxima_ready")
            s_put = [sem(f"maxima_{k}_stored") for k in range(SL)]
            s_d = sem("dve_steps_gat")
            s_p = sem("pool_steps_gat")
            s_idx = sem("source_indices_written")
            s_key = sem("key_indices_written")
            with nc.Block() as block:
                @block.sync
                def _(sp):
                    sp.dma_start(src_i[:], a["src_cols"]).then_inc(s_in, 16)
                    sp.dma_start(dst_i[:], a["dst_cols"]).then_inc(s_in, 16)
                    sp.dma_start(attr[:], a["edge_attr"]).then_inc(s_in, 16)
                    sp.dma_start(w_edge[:], a["gat_w_edge"].rearrange("k c -> (k c)").partition_broadcast(P)
                                 .rearrange("p (k c) -> p k c", k=4)).then_inc(s_in, 16)
                    sp.dma_start(att_edge[:], a["att_edge"].rearrange("h c -> (h c)").partition_broadcast(P)).then_inc(s_in, 16)
                    sp.dma_start(dst_row[:], a["dst_row"].partition_broadcast(P)).then_inc(s_in, 16)
                    sp.wait_ge(s_low, 1)
                    parts = NP * CH * GH // P // 2240
                    table = max_table.rearrange("(p r w) h -> p r (w h)", p=P, r=parts)
                    for r in range(parts):
                        sp.dma_start(table[:, r, :], low[:]).then_inc(s_init, 16)
                    sp.wait_ge(s_init, 16 * parts)

                @block.gpsimd
                def _(pool):
                    step = Steps(pool, s_p)
                    pool.iota(chunk_i[:], pattern=[[1, CH]], base=0, channel_multiplier=0).then_inc(s_iota, 1)
                    step(pool.memset(before[:], 1.0))
                    pool.affine_select(out=before[:], in_=before[:], compare_op=ALU.is_ge, fill=0.0, base=-1,
                                       pattern=[[-1, P]], channel_multiplier=1).then_inc(s_iota, 1)
                    pool.wait_ge(s_in, 96)

                    def copy_source(k, c, turn):
                        pool.wait_ge(s_got[k], turn * 16)
                        pool.tensor_copy(src_now[k][:], src_i[:, bass.ds(c, 1)]).then_inc(s_idx, 1)

                    def copy_key(k, c, turn):
                        pool.wait_ge(s_put[k], turn * 16)
                        pool.wait_ge(s_rows, c + 1)
                        pool.tensor_copy(key_now[k][:], key_i[:, bass.ds(c, 1)]).then_inc(s_key, 1)

                    def gather(k):
                        pool.indirect_dma_start(source_now[k][:], None, source_table,
                                                bass.IndirectOffsetOnAxis(ap=src_now[k][:], axis=0)).then_inc(s_got[k], 16)

                    def store(k):
                        pool.indirect_dma_start(max_table, bass.IndirectOffsetOnAxis(ap=key_now[k][:], axis=0),
                                                max_now[k][:], None, bounds_check=NP * CH - 1,
                                                oob_is_err=False).then_inc(s_put[k], 16)

                    def store_ready(c):
                        pool.wait_ge(s_key, c + 1)
                        pool.wait_ge(s_mx, c + 1)

                    copy_source(0, 0, 0)
                    for k in range(1, SL):
                        pool.wait_ge(s_idx, k)
                        copy_source(k, k, 0)
                        gather(k - 1)
                    pool.wait_ge(s_idx, SL)
                    copy_key(0, 0, 0)
                    gather(SL - 1)
                    pool.wait_ge(s_init, 16 * (NP * CH * GH // P // 2240))
                    with pool.Fori(0, CH // SL - 1) as t:
                        for k in range(SL):
                            c = t * SL + k
                            store_ready(c)
                            copy_source(k, t * SL + (k + SL), t + 1)
                            store(k)
                            pool.wait_ge(s_lg, t * SL + (k + 1))
                            pool.wait_ge(s_idx, t * SL + (k + SL + 1))
                            copy_key((k + 1) % SL, t * SL + (k + 1), t + (k + 1) // SL)
                            gather(k)
                    for k in range(SL):
                        c = CH - SL + k
                        store_ready(c)
                        if k + 1 < SL:
                            copy_key(k + 1, c + 1, CH // SL - 1)
                        store(k)
                    for k in range(SL):
                        pool.wait_ge(s_put[k], 16 * CH // SL)

                @block.vector
                def _(dve):
                    step = Steps(dve, s_d)
                    dve.memset(low[:], NEG).then_inc(s_low, 1)
                    dve.wait_ge(s_in, 96)
                    step(dve.tensor_tensor(w_edge[:], w_edge[:], att_edge[:].unsqueeze(1).broadcast_to([P, 4, D]), ALU.mult))
                    step(dve.tensor_reduce(v_edge[:], w_edge[:].rearrange("p k (h c) -> p k h c", c=GC), AX.X, ALU.add))
                    dve.tensor_reduce(mean[:], attr[:].rearrange("p c k -> p k c"), AX.X, ALU.add).then_inc(s_part, 1)
                    dve.wait_ge(s_mean, 1)
                    step(dve.tensor_scalar(mean[:], sums[:], 1.0 / E, None, ALU.mult))
                    for h in range(GH):
                        for k in range(4):
                            real, loops = logit[:, 0:EC, h], logit[:, EC:CH, h]
                            again = mean[:, k:k + 1].broadcast_to([P, CH - EC])
                            if k == 0:
                                dve.tensor_scalar(real, attr[:, :, k], v_edge[:, k, h:h + 1], None, ALU.mult)
                                step(dve.tensor_scalar(loops, again, v_edge[:, k, h:h + 1], None, ALU.mult))
                            else:
                                dve.scalar_tensor_tensor(out=real, in0=attr[:, :, k], scalar=v_edge[:, k, h:h + 1],
                                                         in1=real, op0=ALU.mult, op1=ALU.add)
                                step(dve.scalar_tensor_tensor(out=loops, in0=again, scalar=v_edge[:, k, h:h + 1],
                                                              in1=loops, op0=ALU.mult, op1=ALU.add))
                    step(dve.tensor_copy(dst_f[:], dst_i[:]))
                    dve.wait_ge(s_iota, 2)
                    step(dve.scalar_tensor_tensor(out=key[:], in0=dst_f[:], scalar=float(CH), in1=chunk_i[:],
                                                  op0=ALU.mult, op1=ALU.add))

                    def first_edges(k, c):
                        row = dst_row[:, bass.ds(c * P, P)]
                        dve.tensor_scalar(other[k][:], row, dst_f[:, bass.ds(c, 1)], NEG, ALU.not_equal, ALU.mult)
                        dve.scalar_tensor_tensor(out=scratch_f[k][:], in0=row, scalar=dst_f[:, bass.ds(c, 1)], in1=before[:],
                                                 op0=ALU.is_equal, op1=ALU.mult, accum_out=earlier[k][:]).then_inc(s_first, 1)
                        dve.wait_ge(s_first, c + 1)
                        dve.scalar_tensor_tensor(out=key_i[:, bass.ds(c, 1)], in0=earlier[k][:], scalar=SKIP,
                                                 in1=key[:, bass.ds(c, 1)], op0=ALU.mult, op1=ALU.add).then_inc(s_rows, 1)

                    def logits(k, c, turn):
                        dve.wait_ge(s_got[k], turn * 16 + 16)
                        dve.tensor_tensor(logit_now[k][:], source_now[k][:], logit[:, bass.ds(c, 1), :], ALU.add).then_inc(s_lg, 1)

                    def maxima(k, c, turn):
                        dve.wait_ge(s_put[k], turn * 16)
                        dve.wait_ge(s_lc, c + 1)
                        dve.wait_ge(s_sp, c + 1)
                        dve.wait_ge(s_first, c + 1)
                        dve.scalar_tensor_tensor(out=row_idx[:, bass.ds(c, 1)], in0=earlier[k][:], scalar=SKIP,
                                                 in1=dst_f[:, bass.ds(c, 1)], op0=ALU.mult, op1=ALU.add)
                        for h in range(GH):
                            ins = dve.tensor_tensor_reduce(out=scratch_m[k][:, h, :], in0=spread[k][:, h, :], in1=other[k][:], scale=1.0,
                                                     scalar=NEG, op0=ALU.add, op1=ALU.max, accum_out=max_now[k][:, h:h + 1])
                        ins.then_inc(s_mx, 1)

                    with dve.Fori(0, CH // SL) as t:
                        for k in range(SL):
                            first_edges(k, t * SL + k)
                            logits(k, t * SL + k, t)
                            if k:
                                maxima(k - 1, t * SL + (k - 1), t)
                        maxima(SL - 1, t * SL + (SL - 1), t)

                @block.scalar
                def _(act):
                    with act.Fori(0, CH // SL) as t:
                        for k in range(SL):
                            act.wait_ge(s_lg, t * SL + (k + 1))
                            act.copy(logit[:, bass.ds(t * SL + k, 1), :], logit_now[k][:]).then_inc(s_lc, 1)

                @block.tensor
                def _(pe):
                    pe.wait_ge(s_part, 1)
                    pe.matmul(sums[:], ones[:], mean[:], start=True, stop=True).then_inc(s_mean, 1)
                    with pe.Fori(0, CH // SL) as t:
                        for k in range(SL):
                            pe.wait_ge(s_lg, t * SL + (k + 1))
                            for h in range(GH):
                                ins = pe.matmul(spread[k][:, h, :], logit_now[k][:, h:h + 1].broadcast_to([P, P]), ident[:],
                                                start=True, stop=True)
                            ins.then_inc(s_sp, 1)

        with ExitStack() as s:
            def sb(name, shape, dt=F32):
                return s.enter_context(nc.sbuf_tensor(name, shape, dt))

            def sem(name):
                return s.enter_context(nc.semaphore(name))

            SL = 4
            chunk_max = sb("chunk_max", [P, 2, CH, GH])
            node_max = sb("node_max", [P, NT, GH])
            target = sb("target", [P, NT, 2 * GH])
            dst_now = [sb(f"dst_now{k}", [P, 1], I32) for k in range(SL)]
            target_now = [sb(f"target_now{k}", [P, 2 * GH]) for k in range(SL)]
            edge_target = sb("edge_target", [P, CH, 2 * GH])
            zeros = sb("zeros", [P, NT * (D + GH)])
            s_cm = [sem(f"chunk_max_{b}_loaded") for b in range(2)]
            s_nm = sem("node_max_ready")
            s_tg = sem("target_ready")
            s_tab = sem("target_table_stored")
            s_got = [sem(f"target_{k}_gathered") for k in range(SL)]
            s_kept = sem("target_kept")
            s_z = sem("zeros_ready")
            s_clear = sem("sums_cleared")
            s_e = sem("exponents_ready")
            s_d = sem("dve_steps_max")
            s_idx = sem("target_indices_written")
            with nc.Block() as block:
                @block.sync
                def _(sp):
                    table = max_table.rearrange("(t p c) h -> t p c h", p=P, c=CH)
                    for t in range(NT):
                        if t >= 2:
                            sp.wait_ge(s_nm, t - 1)
                        sp.dma_start(chunk_max[:, t % 2, :, :], table[t]).then_inc(s_cm[t % 2], 16)
                    sp.wait_ge(s_tg, 1)
                    sp.dma_start(target_table.rearrange("(t p) j -> p t j", p=P), target[:]).then_inc(s_tab, 16)
                    sp.wait_ge(s_z, 1)
                    for k in range(SLOTS):
                        sp.dma_start(sums_table[k].rearrange("(p t) j -> p (t j)", p=P), zeros[:]).then_inc(s_clear, 16)
                    sp.wait_ge(s_clear, 16 * SLOTS)

                @block.vector
                def _(dve):
                    step = Steps(dve, s_d)
                    for t in range(NT):
                        dve.wait_ge(s_cm[t % 2], 16 * (t // 2 + 1))
                        dve.tensor_reduce(node_max[:, t, :], chunk_max[:, t % 2, :, :].rearrange("p c h -> p h c"),
                                          AX.X, ALU.max).then_inc(s_nm, 1)
                    dve.wait_ge(s_nm, NT)
                    step(dve.tensor_tensor(node_max[:], node_max[:], a_dst[:], ALU.add))
                    dve.tensor_copy(target[:, :, 0:GH], a_dst[:])
                    dve.scalar_tensor_tensor(out=target[:, :, GH:2 * GH], in0=node_max[:], scalar=SLOPE, in1=node_max[:],
                                             op0=ALU.mult, op1=ALU.max).then_inc(s_tg, 1)
                    dve.memset(zeros[:], 0.0).then_inc(s_z, 1)
                    dve.wait_ge(s_kept, CH)
                    step(dve.tensor_tensor(logit[:], logit[:], edge_target[:, :, 0:GH], ALU.add))
                    step(dve.scalar_tensor_tensor(out=logit[:], in0=logit[:], scalar=SLOPE, in1=logit[:],
                                                  op0=ALU.mult, op1=ALU.max))
                    dve.tensor_tensor(logit[:], logit[:], edge_target[:, :, GH:2 * GH], ALU.subtract).then_inc(s_e, 1)

                @block.gpsimd
                def _(pool):
                    def copy_index(k, c, turn):
                        pool.wait_ge(s_got[k], turn * 16)
                        pool.tensor_copy(dst_now[k][:], dst_i[:, bass.ds(c, 1)]).then_inc(s_idx, 1)

                    def gather(k):
                        pool.indirect_dma_start(target_now[k][:], None, target_table,
                                                bass.IndirectOffsetOnAxis(ap=dst_now[k][:], axis=0)).then_inc(s_got[k], 16)

                    copy_index(0, 0, 0)
                    pool.wait_ge(s_tab, 16)
                    with pool.Fori(0, CH // SL - 1) as t:
                        for k in range(SL):
                            pool.wait_ge(s_idx, t * SL + (k + 1))
                            pool.wait_ge(s_kept, t * SL)
                            copy_index((k + 1) % SL, t * SL + (k + 1), t + (k + 1) // SL)
                            gather(k)
                    for k in range(SL):
                        pool.wait_ge(s_idx, CH - SL + k + 1)
                        pool.wait_ge(s_kept, CH - SL)
                        if k + 1 < SL:
                            copy_index(k + 1, CH - SL + k + 1, CH // SL - 1)
                        gather(k)

                @block.scalar
                def _(act):
                    with act.Fori(0, CH // SL) as t:
                        for k in range(SL):
                            act.wait_ge(s_got[k], t * 16 + 16)
                            act.copy(edge_target[:, bass.ds(t * SL + k, 1), :], target_now[k][:]).then_inc(s_kept, 1)
                    act.wait_ge(s_e, 1)
                    act.activation(logit[:], logit[:], ACT.Exp)

        with ExitStack() as s:
            def sb(name, shape, dt=F32):
                return s.enter_context(nc.sbuf_tensor(name, shape, dt))

            def sem(name):
                return s.enter_context(nc.semaphore(name))

            SL = SLOTS
            src_now = [sb(f"fsrc_now{k}", [P, 1], I32) for k in range(SL)]
            row_now = [sb(f"row_now{k}", [P, 1], I32) for k in range(SL)]
            feat = [sb(f"feat{k}", [P, D]) for k in range(SL)]
            same = [sb(f"same{k}", [P, P]) for k in range(2)]
            summed_sb = [sb(f"summed_sb{k}", [P, D + GH]) for k in range(SL)]
            ps = [s.enter_context(nc.psum_tensor(f"gs{b}", [P, 512], F32)) for b in range(2)]
            pw = [s.enter_context(nc.psum_tensor(f"gw{b}", [P, 512], F32)) for b in range(2)]
            s_got = [sem(f"features_{k}_gathered") for k in range(SL)]
            s_msg = sem("messages_ready")
            s_sum = sem("messages_summed")
            s_cpf = sem("sums_copied_by_scalar")
            s_cpw = sem("weight_sums_copied_by_vector")
            s_add = [sem(f"sums_{k}_added") for k in range(SL)]
            s_idx = sem("feature_indices_written")
            s_row = sem("row_indices_written")
            with nc.Block() as block:
                @block.gpsimd
                def _(pool):

                    def copy_source(k, c, turn):
                        pool.wait_ge(s_got[k], turn * 16)
                        pool.tensor_copy(src_now[k][:], src_i[:, bass.ds(c, 1)]).then_inc(s_idx, 1)

                    def copy_row(k, c, turn):
                        pool.wait_ge(s_add[k], turn * 16)
                        pool.tensor_copy(row_now[k][:], row_idx[:, bass.ds(c, 1)]).then_inc(s_row, 1)

                    def gather(k):
                        pool.indirect_dma_start(feat[k][:], None, feature_table,
                                                bass.IndirectOffsetOnAxis(ap=src_now[k][:], axis=0)).then_inc(s_got[k], 16)

                    def add(k):
                        pool.indirect_dma_start(sums_table[k], bass.IndirectOffsetOnAxis(ap=row_now[k][:], axis=0),
                                                summed_sb[k][:], None, bounds_check=NP - 1, oob_is_err=False,
                                                compute_op=ALU.add).then_inc(s_add[k], 16)

                    def add_ready(c):
                        pool.wait_ge(s_row, c + 1)
                        pool.wait_ge(s_cpf, c + 1)
                        pool.wait_ge(s_cpw, c + 1)

                    copy_source(0, 0, 0)
                    for k in range(1, SL):
                        pool.wait_ge(s_idx, k)
                        copy_source(k, k, 0)
                        gather(k - 1)
                    pool.wait_ge(s_idx, SL)
                    copy_row(0, 0, 0)
                    gather(SL - 1)
                    with pool.Fori(0, CH // SL - 1) as t:
                        for k in range(SL):
                            add_ready(t * SL + k)
                            copy_source(k, t * SL + (k + SL), t + 1)
                            add(k)
                            pool.wait_ge(s_sum, t * SL + (k + 1))
                            pool.wait_ge(s_idx, t * SL + (k + SL + 1))
                            copy_row((k + 1) % SL, t * SL + (k + 1), t + (k + 1) // SL)
                            gather(k)
                    for k in range(SL):
                        add_ready(CH - SL + k)
                        if k + 1 < SL:
                            copy_row(k + 1, CH - SL + k + 1, CH // SL - 1)
                        add(k)
                    for k in range(SL):
                        pool.wait_ge(s_add[k], 16 * CH // SL)

                @block.vector
                def _(dve):
                    def messages(k, c, turn, first=False):
                        b = k % 2
                        if not first:
                            dve.wait_ge(s_sum, c - 1)
                        dve.tensor_scalar(same[b][:], dst_row[:, bass.ds(c * P, P)], dst_f[:, bass.ds(c, 1)], None, ALU.is_equal)
                        dve.wait_ge(s_got[k], turn * 16 + 16)
                        weights = logit[:, bass.ds(c, 1), :].rearrange("p o h -> p (o h)").unsqueeze(2).broadcast_to([P, GH, GC])
                        f = feat[k][:].rearrange("p (h c) -> p h c", c=GC)
                        dve.tensor_tensor(f, f, weights, ALU.mult).then_inc(s_msg, 1)

                    def weight_sums(k, c, turn):
                        dve.wait_ge(s_add[k], turn * 16)
                        dve.wait_ge(s_sum, c + 1)
                        dve.tensor_copy(summed_sb[k][:, D:D + GH], pw[k % 2][:, 0:GH]).then_inc(s_cpw, 1)

                    messages(0, 0, 0, first=True)
                    with dve.Fori(0, CH // SL - 1) as t:
                        for k in range(SL):
                            messages((k + 1) % SL, t * SL + (k + 1), t + (k + 1) // SL)
                            weight_sums(k, t * SL + k, t)
                    for k in range(SL):
                        c = CH - SL + k
                        if k + 1 < SL:
                            messages(k + 1, c + 1, CH // SL - 1)
                        weight_sums(k, c, CH // SL - 1)

                @block.tensor
                def _(pe):
                    with pe.Fori(0, CH // SL) as t:
                        for k in range(SL):
                            b = k % 2
                            c = t * SL + k
                            pe.wait_ge(s_msg, c + 1)
                            if k >= 2:
                                pe.wait_ge(s_cpf, t * SL + (k - 1))
                                pe.wait_ge(s_cpw, t * SL + (k - 1))
                            else:
                                pe.wait_ge(s_cpf, t * SL)
                                pe.wait_ge(s_cpw, t * SL)
                            pe.matmul(ps[b][:], same[b][:], feat[k][:], start=True, stop=True)
                            pe.matmul(pw[b][:, 0:GH], same[b][:], logit[:, bass.ds(c, 1), :], start=True, stop=True).then_inc(s_sum, 1)

                @block.scalar
                def _(act):
                    with act.Fori(0, CH // SL) as t:
                        for k in range(SL):
                            act.wait_ge(s_add[k], t * 16)
                            act.wait_ge(s_sum, t * SL + (k + 1))
                            act.copy(summed_sb[k][:, 0:D], ps[k % 2][:]).then_inc(s_cpf, 1)
        gat.close()

        with ExitStack() as s:
            def sb(name, shape, dt=F32):
                return s.enter_context(nc.sbuf_tensor(name, shape, dt))

            def sem(name):
                return s.enter_context(nc.semaphore(name))

            got = [[sb(f"got{b}_{k}", [P, D + GH]) for k in range(SLOTS)] for b in range(2)]
            node = sb("node", [P, NT, D])
            square = sb("square", [P, 2, D])
            weight = sb("weight", [P, 2, GH])
            bias = sb("bias", [P, D])
            gamma = sb("gamma", [P, D])
            beta = sb("beta", [P, D])
            scale = sb("scale", [P, D])
            eps_bn = sb("eps_bn", [P, 1])
            mean_ps = s.enter_context(nc.psum_tensor("mean_ps", [P, 512], F32))
            var_ps = s.enter_context(nc.psum_tensor("var_ps", [P, 512], F32))
            s_c = sem("batch_norm_constants_loaded")
            s_got = [sem(f"sums_{b}_loaded") for b in range(2)]
            s_free = sem("sums_read")
            s_node = sem("node_ready")
            s_mean = sem("mean_ready")
            s_sq = sem("square_ready")
            s_var = sem("variance_summed")
            s_varu = sem("squares_used")
            s_dev = sem("deviation_ready_bn")
            s_eps = sem("eps_ready")
            s_d = sem("dve_steps_bn")
            with nc.Block() as block:
                @block.sync
                def _(sp):
                    for t in range(NT):
                        b = t % 2
                        if t >= 2:
                            sp.wait_ge(s_free, t - 1)
                        for k in range(SLOTS):
                            sp.dma_start(got[b][k][:], sums_table[k][t * P:(t + 1) * P, :]).then_inc(s_got[b], 16)
                        if t == 0:
                            for dst, name in ((bias, "gat_bias"), (gamma, "gamma"), (beta, "beta")):
                                sp.dma_start(dst[:], a[name].partition_broadcast(P)).then_inc(s_c, 16)

                @block.vector
                def _(dve):
                    step = Steps(dve, s_d)
                    dve.memset(eps_bn[:], BN_EPS).then_inc(s_eps, 1)
                    for t in range(NT):
                        b = t % 2
                        g = got[b]
                        dve.wait_ge(s_got[b], 16 * SLOTS * (t // 2 + 1))
                        dve.tensor_tensor(g[0][:], g[0][:], g[1][:], ALU.add)
                        step(dve.tensor_tensor(g[2][:], g[2][:], g[3][:], ALU.add))
                        step(dve.tensor_tensor(g[0][:], g[0][:], g[2][:], ALU.add))
                        step(dve.tensor_scalar(weight[:, b, :], g[0][:, D:D + GH], 1e-16, None, ALU.add))
                        step(dve.reciprocal(weight[:, b, :], weight[:, b, :]))
                        f = g[0][:, 0:D].rearrange("p (h c) -> p h c", c=GC)
                        step(dve.tensor_tensor(f, f, weight[:, b, :].unsqueeze(2).broadcast_to([P, GH, GC]), ALU.mult))
                        if t == 0:
                            dve.wait_ge(s_c, 48)
                        ins = dve.tensor_tensor(node[:, t, :], g[0][:, 0:D], bias[:], ALU.add)
                        ins.then_inc(s_free, 1)
                    dve.wait_ge(s_mean, 1)
                    dve.wait_ge(s_free, NT)
                    for t in range(NT):
                        dve.scalar_tensor_tensor(out=node[:, t, :], in0=mean_ps[:], scalar=-1.0 / N, in1=node[:, t, :],
                                                 op0=ALU.mult, op1=ALU.add).then_inc(s_node, 1)
                    dve.wait_ge(s_dev, 1)
                    step(dve.reciprocal(scale[:], scale[:]))
                    step(dve.tensor_tensor(scale[:], scale[:], gamma[:], ALU.mult))
                    for t in range(NT):
                        dve.wait_ge(s_sq, t + 1)
                        step(dve.tensor_tensor(node[:, t, :], node[:, t, :], scale[:], ALU.mult))
                        step(dve.tensor_tensor(node[:, t, :], node[:, t, :], beta[:], ALU.add))
                        dve.tensor_tensor(x1[:, t, :], x1[:, t, :], node[:, t, :], ALU.add)

                @block.tensor
                def _(pe):
                    for t in range(NT):
                        pe.wait_ge(s_free, t + 1)
                        ins = pe.matmul(mean_ps[:], ones[0:rows(t), :], node[0:rows(t), t, :], start=(t == 0), stop=(t == NT - 1))
                    ins.then_inc(s_mean, 1)
                    for t in range(NT):
                        pe.wait_ge(s_sq, t + 1)
                        pe.matmul(var_ps[:], ones[0:rows(t), :], square[0:rows(t), t % 2, :], start=(t == 0),
                                  stop=(t == NT - 1)).then_inc(s_varu, 1)

                @block.scalar
                def _(act):
                    act.wait_ge(s_eps, 1)
                    for t in range(NT):
                        act.wait_ge(s_node, t + 1)
                        if t >= 2:
                            act.wait_ge(s_varu, t - 1)
                        act.activation(square[:, t % 2, :], node[:, t, :], ACT.Square).then_inc(s_sq, 1)
                    act.wait_ge(s_varu, NT)
                    act.activation(scale[:], var_ps[:], ACT.Sqrt, bias=eps_bn[:], scale=1.0 / N).then_inc(s_dev, 1)

        with ExitStack() as s:
            def sb(name, shape, dt=F32):
                return s.enter_context(nc.sbuf_tensor(name, shape, dt))

            def sem(name):
                return s.enter_context(nc.semaphore(name))

            HALO = NP + 2 * PAD
            yn = sb("yn", [P, NT, D])
            yn_t = sb("yn_t", [P, KT, HALO])
            rc_act = sb("rc_act", [P, KT, HALO])
            rc_w1 = sb("rc_w1", [P, RC_TAPS, KT, D])
            rc_w2 = sb("rc_w2", [P, RC_TAPS, KT, XE])
            sh_w1 = sb("sh_w1", [P, SH_TAPS, KT, HID])
            sh_w2 = sb("sh_w2", [P, HT, D])
            sh_act = sb("sh_act", [P, HT, N])
            rc_b1 = sb("rc_b1", [P, KT])
            rc_b2 = sb("rc_b2", [P, XE])
            sh_b1 = sb("sh_b1", [P, HT])
            e_b1 = [sb(f"e_b1_{b}", [P, HT]) for b in range(2)]
            out_bias = sb("out_bias", [XE + 1, D])
            ln_g = sb("ln_g", [P, D])
            ln_b = sb("ln_b", [P, D])
            e_w1 = [sb(f"e_w1_{b}", [P, KT, HID]) for b in range(2)]
            e_w2 = [sb(f"e_w2_{b}", [P, HT, D]) for b in range(2)]
            h_act = [sb(f"h_act{b}", [P, HT, N]) for b in range(2)]
            negative = sb("negative", [P, 2, 512])
            logits = sb("logits", [P, NT, XE])
            first = sb("first", [P, NT, XE])
            second = sb("second", [P, NT, XE])
            place = sb("place", [P, NT, XE])
            number = sb("number", [P, NT, XE])
            number_i = sb("number_i", [P, NT, XE], I32)
            top = sb("top", [P, 2, NT])
            which = sb("which", [P, NT])
            share = sb("share", [P, 2, NT])
            gates = sb("gates", [P, NT, XE + 1])
            gates_t = h_act[1][0:XE + 1, 0, :]
            stats = sb("f_stats", [P, 6])
            mv = sb("f_mv", [P, NT, 2])
            std = sb("f_std", [P, NT])
            rstd = sb("f_rstd", [P, NT])
            up = [s.enter_context(nc.psum_tensor(f"up{b}", [P, 512], F32)) for b in range(4)]
            down = [s.enter_context(nc.psum_tensor(f"down{b}", [P, 512], F32)) for b in range(4)]
            s_rcw = sem("router_weights_loaded")
            s_shw = sem("shared_weights_loaded")
            s_bias = sem("biases_loaded")
            s_exp = [sem(f"expert_{b}_loaded") for b in range(2)]
            s_iota = sem("expert_numbers_ready")
            s_zero = sem("halos_zeroed")
            s_stat = sem("x1_variance_ready")
            s_std = sem("x1_deviation_ready")
            s_yn = sem("yn_ready")
            s_tr = sem("yn_transposed")
            s_yt = sem("yn_t_ready")
            s_unit = sem("hidden_unit_ready")
            s_act = sem("hidden_unit_activated")
            s_low = sem("hidden_unit_minimum_taken")
            s_ex = sem("hidden_unit_exponent_ready")
            s_h = sem("expert_hidden_unit_ready")
            s_lg = sem("router_logits_ready")
            s_lgc = sem("router_logits_copied")
            s_gap = sem("top_difference_ready")
            s_gx = sem("top_exponent_ready")
            s_gate = sem("gates_ready")
            s_gt = sem("gates_transposed")
            s_gtc = sem("gates_t_ready")
            s_dn = sem("token_tile_ready")
            s_add = sem("token_tile_added")
            s_var = sem("z_variance_ready")
            s_dev = sem("z_deviation_ready")
            s_out = sem("out_tile_ready")
            s_st = sem("out_stored")
            s_d = sem("dve_steps_ffn")
            CONV = (KT + HT) * 3
            EU = HT * 3

            with nc.Block() as block:
                @block.sync
                def _(sp):
                    sp.dma_start(rc_w1[:], a["rc_w1"].rearrange("j (k p) o -> p j k o", p=P)).then_inc(s_rcw, 16)
                    with nc.allow_non_contiguous_dma(reason="small vectors, one number for a partition"):
                        sp.dma_start(rc_b1[:], a["rc_b1"].rearrange("(k p) -> p k", p=P)).then_inc(s_bias, 16)
                        sp.dma_start(sh_b1[:], a["sh_b1"].rearrange("(k p) -> p k", p=P)).then_inc(s_bias, 16)
                        sp.dma_start(rc_w2[:], a["rc_w2"].rearrange("j (k p) o -> p j k o", p=P)).then_inc(s_bias, 16)
                    sp.dma_start(rc_b2[:], a["rc_b2"].partition_broadcast(P)).then_inc(s_bias, 16)
                    sp.dma_start(out_bias[0:XE, :], a["e_b2"]).then_inc(s_bias, 16)
                    sp.dma_start(out_bias[XE:XE + 1, :], a["sh_b2"].partition_broadcast(1)).then_inc(s_bias, 16)
                    sp.dma_start(ln_g[:], a["ln_g"].partition_broadcast(P)).then_inc(s_bias, 16)
                    sp.dma_start(ln_b[:], a["ln_b"].partition_broadcast(P)).then_inc(s_bias, 16)
                    sp.dma_start(sh_w1[:], a["sh_w1"].rearrange("j (k p) o -> p j k o", p=P)).then_inc(s_shw, 16)
                    sp.dma_start(sh_w2[:], a["sh_w2"].rearrange("(k p) o -> p k o", p=P)).then_inc(s_shw, 16)

                    def expert(b, e):
                        sp.dma_start(e_w1[b][:], a["e_w1"][bass.ds(e, 1), :, :].rearrange("e (k p) o -> p (e k) o", p=P)).then_inc(s_exp[b], 16)
                        sp.dma_start(e_w2[b][:], a["e_w2"][bass.ds(e, 1), :, :].rearrange("e (k p) o -> p (e k) o", p=P)).then_inc(s_exp[b], 16)
                        sp.dma_start(e_b1[b][:], a["e_b1_cols"][bass.ds(e, 1), :, :].rearrange("e p k -> p (e k)")).then_inc(s_exp[b], 16)

                    for b in range(2):
                        expert(b, b)
                    with sp.Fori(1, XE // 2) as u:
                        for b in range(2):
                            sp.wait_ge(s_dn, u * (2 * NT) + (b * NT))
                            expert(b, u * 2 + b)
                    for t in range(NT):
                        sp.wait_ge(s_out, t + 1)
                        sp.dma_start(out[t * P:t * P + rows(t), :], yn[0:rows(t), t, :]).then_inc(s_st, 16)
                    sp.wait_ge(s_st, 16 * NT)

                @block.gpsimd
                def _(pool):
                    pool.iota(number_i[:], pattern=[[0, NT], [1, XE]], base=0, channel_multiplier=0).then_inc(s_iota, 1)

                @block.tensor
                def _(pe):
                    for t in range(NT):
                        pe.wait_ge(s_yn, t + 1)
                        if t >= 2:
                            pe.wait_ge(s_yt, t - 1)
                        for k in range(KT):
                            ins = pe.transpose(down[t % 2][:, k * P:(k + 1) * P], yn[:, t, k * P:(k + 1) * P], ident[:])
                        ins.then_inc(s_tr, 1)
                    pe.wait_ge(s_yt, NT)
                    pe.wait_ge(s_zero, 2)
                    i = 0
                    for w, taps, tiles, loaded, n_loaded in ((rc_w1, RC_TAPS, KT, s_rcw, 16), (sh_w1, SH_TAPS, HT, s_shw, 32)):
                        pe.wait_ge(loaded, n_loaded)
                        for m in range(tiles):
                            for at, n in SPANS:
                                if i >= 4:
                                    pe.wait_ge(s_act, i - 3)
                                for j in range(taps):
                                    first_col = at + PAD - taps // 2 + j
                                    for k in range(KT):
                                        ins = pe.matmul(up[i % 4][:, 0:n], w[:, j, k, m * P:(m + 1) * P],
                                                        yn_t[:, k, first_col:first_col + n],
                                                        start=(j == 0 and k == 0), stop=(j == taps - 1 and k == KT - 1))
                                ins.then_inc(s_unit, 1)
                                i += 1
                    pe.wait_ge(s_act, KT * 3)
                    pe.wait_ge(s_bias, 128)
                    for t in range(NT):
                        if t >= 2:
                            pe.wait_ge(s_lgc, t - 1)
                        for j in range(RC_TAPS):
                            first_col = t * P + PAD - RC_TAPS // 2 + j
                            for k in range(KT):
                                ins = pe.matmul(down[t % 2][:, 0:XE], rc_act[:, k, first_col:first_col + P], rc_w2[:, j, k, :],
                                                start=(j == 0 and k == 0), stop=(j == RC_TAPS - 1 and k == KT - 1))
                        ins.then_inc(s_lg, 1)

                    def first_layer(b, turn, before):
                        pe.wait_ge(s_exp[b], turn * 48 + 48)
                        for i in range(EU):
                            m, j = i // 3, i % 3
                            at, n = SPANS[j]
                            pe.wait_ge(s_act, before + (i - 3))
                            if isinstance(before, int) and before == CONV:
                                if i >= 4:
                                    pe.wait_ge(s_low, i - 3)
                            else:
                                pe.wait_ge(s_low, before + (i - 3 - CONV))
                            for k in range(KT):
                                ins = pe.matmul(up[(i + 2 * b + CONV) % 4][:, 0:n], e_w1[b][:, k, m * P:(m + 1) * P],
                                                yn_t[:, k, PAD + at:PAD + at + n], start=(k == 0), stop=(k == KT - 1))
                            ins.then_inc(s_unit, 1)

                    def second_layer(b, e, before):
                        pe.wait_ge(s_h, e * EU + EU)
                        for t in range(NT):
                            pe.wait_ge(s_add, before + (t - 3))
                            for k in range(HT):
                                ins = pe.matmul(down[(t + 2 * b + NT) % 4][0:rows(t), :], h_act[b][:, k, t * P:t * P + rows(t)],
                                                e_w2[b][:, k, :], start=(k == 0), stop=(k == HT - 1))
                            ins.then_inc(s_dn, 1)

                    first_layer(0, 0, CONV)
                    pe.wait_ge(s_gate, 1)
                    for t in range(NT):
                        q = t // 4
                        ins = pe.transpose(down[q][0:XE + 1, (t % 4) * P:(t % 4 + 1) * P], gates[:, t, :], ident[:])
                    ins.then_inc(s_gt, 1)
                    pe.wait_ge(s_gtc, 3)
                    pe.wait_ge(s_act, CONV)
                    for t in range(NT):
                        if t >= 4:
                            pe.wait_ge(s_add, t - 3)
                        n = rows(t)
                        for k in range(HT):
                            pe.matmul(down[t % 4][0:n, :], sh_act[:, k, t * P:t * P + n], sh_w2[:, k, :], start=(k == 0), stop=False)
                        pe.matmul(down[t % 4][0:n, :], gates_t[:, t * P:t * P + n], out_bias[:], start=False, stop=True).then_inc(s_dn, 1)
                    with pe.Fori(0, XE // 2 - 1) as u:
                        first_layer(1, u, u * (2 * EU) + (CONV + EU))
                        second_layer(0, u * 2, u * (2 * NT) + NT)
                        first_layer(0, u + 1, u * (2 * EU) + (CONV + 2 * EU))
                        second_layer(1, u * 2 + 1, u * (2 * NT) + 2 * NT)
                    first_layer(1, XE // 2 - 1, CONV + (XE - 1) * EU)
                    second_layer(0, XE - 2, (XE - 2) * NT + NT)
                    second_layer(1, XE - 1, (XE - 1) * NT + NT)

                @block.scalar
                def _(act):
                    act.wait_ge(s_stat, 1)
                    act.activation(std[:], mv[:, :, 1], ACT.Sqrt, bias=eps_ln[:]).then_inc(s_std, 1)
                    act.wait_ge(s_bias, 128)
                    act.wait_ge(s_zero, 2)
                    i = 0
                    for m in range(KT):
                        for at, n in SPANS:
                            act.wait_ge(s_unit, i + 1)
                            act.activation(rc_act[:, m, PAD + at:PAD + at + n], up[i % 4][:, 0:n], ACT.Gelu,
                                           bias=rc_b1[:, m:m + 1]).then_inc(s_act, 1)
                            i += 1
                    for m in range(HT):
                        for at, n in SPANS:
                            act.wait_ge(s_unit, i + 1)
                            act.activation(sh_act[:, m, at:at + n], up[i % 4][:, 0:n], ACT.Silu,
                                           bias=sh_b1[:, m:m + 1]).then_inc(s_act, 1)
                            i += 1

                    def expert(b, e):
                        for i in range(EU + 1):
                            if i < EU:
                                m, (at, n) = i // 3, SPANS[i % 3]
                                if not (isinstance(e, int) and e < 1):
                                    act.wait_ge(s_dn, e * NT)
                                act.wait_ge(s_unit, e * EU + (CONV + i + 1))
                                act.activation(h_act[b][:, m, at:at + n], up[(i + 2 * b + CONV) % 4][:, 0:n], ACT.Relu,
                                               bias=e_b1[b][:, m:m + 1]).then_inc(s_act, 1)
                            if i:
                                n = SPANS[(i - 1) % 3][1]
                                act.wait_ge(s_low, e * EU + i)
                                act.activation(negative[:, (i - 1) % 2, 0:n], negative[:, (i - 1) % 2, 0:n], ACT.Exp).then_inc(s_ex, 1)

                    act.wait_ge(s_gap, 1)
                    act.activation(share[:, 1, :], share[:, 0, :], ACT.Exp).then_inc(s_gx, 1)
                    expert(0, 0)
                    expert(1, 1)
                    with act.Fori(1, XE // 2) as u:
                        for b in range(2):
                            expert(b, u * 2 + b)
                    act.wait_ge(s_var, 1)
                    act.activation(std[:], mv[:, :, 1], ACT.Sqrt, bias=eps_ln[:]).then_inc(s_dev, 1)

                @block.vector
                def _(dve):
                    step = Steps(dve, s_d)
                    dve.memset(yn_t[:], 0.0).then_inc(s_zero, 1)
                    dve.memset(rc_act[:], 0.0).then_inc(s_zero, 1)
                    for t in range(NT):
                        step(dve.bn_stats(stats[:], x1[:, t, :]))
                        ins = dve.bn_aggr(mv[:, t, :], stats[:])
                        if t == NT - 1:
                            ins.then_inc(s_stat, 1)
                        else:
                            step(ins)
                    dve.wait_ge(s_std, 1)
                    step(dve.reciprocal(rstd[:], std[:]))
                    dve.wait_ge(s_zero, 2)

                    def to_columns(t):
                        n = rows(t)
                        dve.wait_ge(s_tr, t + 1)
                        dve.tensor_copy(yn_t[:, :, PAD + t * P:PAD + t * P + n],
                                        down[t % 2][:].rearrange("p (k n) -> p k n", k=KT)[:, :, 0:n]).then_inc(s_yt, 1)

                    for t in range(NT):
                        dve.tensor_scalar(yn[:, t, :], x1[:, t, :], mv[:, t, 0:1], rstd[:, t:t + 1],
                                          ALU.subtract, ALU.mult).then_inc(s_yn, 1)
                        if t >= 1:
                            to_columns(t - 1)
                    to_columns(NT - 1)
                    dve.wait_ge(s_bias, 128)
                    for t in range(NT):
                        step(dve.tensor_tensor(x1[:, t, :], x1[:, t, :], ln_b[:], ALU.add))
                    dve.wait_ge(s_iota, 1)
                    step(dve.tensor_copy(number[:], number_i[:]))
                    for t in range(NT):
                        dve.wait_ge(s_lg, t + 1)
                        dve.tensor_tensor(logits[:, t, :], down[t % 2][:, 0:XE], rc_b2[:], ALU.add).then_inc(s_lgc, 1)
                    dve.wait_ge(s_lgc, NT)

                    def spread(v):
                        return v.unsqueeze(2).broadcast_to([P, NT, XE])

                    for r, hot in enumerate((first, second)):
                        step(dve.tensor_reduce(top[:, r, :], logits[:], AX.X, ALU.max))
                        step(dve.tensor_tensor(place[:], logits[:], spread(top[:, r, :]), ALU.not_equal))
                        step(dve.scalar_tensor_tensor(out=place[:], in0=place[:], scalar=float(XE), in1=number[:],
                                                      op0=ALU.mult, op1=ALU.add))
                        step(dve.tensor_reduce(which[:], place[:], AX.X, ALU.min))
                        step(dve.tensor_tensor(hot[:], number[:], spread(which[:]), ALU.is_equal))
                        if r == 0:
                            step(dve.scalar_tensor_tensor(out=logits[:], in0=hot[:], scalar=NEG, in1=logits[:],
                                                          op0=ALU.mult, op1=ALU.add))
                    dve.tensor_tensor(share[:, 0, :], top[:, 1, :], top[:, 0, :], ALU.subtract).then_inc(s_gap, 1)
                    dve.wait_ge(s_gx, 1)
                    step(dve.tensor_scalar(share[:, 0, :], share[:, 1, :], 1.0, None, ALU.add))
                    step(dve.reciprocal(share[:, 0, :], share[:, 0, :]))
                    step(dve.tensor_tensor(share[:, 1, :], share[:, 1, :], share[:, 0, :], ALU.mult))
                    step(dve.tensor_tensor(first[:], first[:], spread(share[:, 0, :]), ALU.mult))
                    step(dve.tensor_tensor(second[:], second[:], spread(share[:, 1, :]), ALU.mult))
                    step(dve.memset(gates[:, :, XE:XE + 1], 1.0))
                    dve.tensor_tensor(gates[:, :, 0:XE], first[:], second[:], ALU.add).then_inc(s_gate, 1)
                    def minimum(b, e, i):
                        m, n = i // 3, SPANS[i % 3][1]
                        if isinstance(e, int) and e == 0:
                            if i >= 2:
                                dve.wait_ge(s_h, i - 1)
                        else:
                            dve.wait_ge(s_h, e * EU + (i - 1))
                        dve.wait_ge(s_act, e * EU + (CONV + i + 1))
                        dve.tensor_scalar(negative[:, i % 2, 0:n], up[(i + 2 * b + CONV) % 4][:, 0:n], e_b1[b][:, m:m + 1], 0.0,
                                          ALU.add, ALU.min).then_inc(s_low, 1)

                    def join(b, e, i):
                        m, (at, n) = i // 3, SPANS[i % 3]
                        dve.wait_ge(s_ex, e * EU + (i + 1))
                        dve.scalar_tensor_tensor(out=h_act[b][:, m, at:at + n], in0=negative[:, i % 2, 0:n], scalar=-1.0,
                                                 in1=h_act[b][:, m, at:at + n], op0=ALU.add, op1=ALU.add).then_inc(s_h, 1)

                    def hidden(b, e):
                        for i in range(EU + 1):
                            if i < EU:
                                minimum(b, e, i)
                            if i:
                                join(b, e, i - 1)

                    def add(b, e):
                        for t in range(NT):
                            n = rows(t)
                            dve.wait_ge(s_dn, e * NT + (NT + t + 1))
                            dve.wait_ge(s_add, e * NT + (t + 1))
                            dve.scalar_tensor_tensor(out=yn[0:n, t, :], in0=down[(t + 2 * b + NT) % 4][0:n, :],
                                                     scalar=gates[0:n, t, bass.ds(e, 1)], in1=yn[0:n, t, :],
                                                     op0=ALU.mult, op1=ALU.add).then_inc(s_add, 1)

                    hidden(0, 0)
                    dve.wait_ge(s_gt, 1)
                    for q in range(3):
                        n = SPANS[q][1]
                        dve.tensor_copy(gates_t[:, q * 512:q * 512 + n], down[q][0:XE + 1, 0:n]).then_inc(s_gtc, 1)
                    for t in range(NT):
                        n = rows(t)
                        dve.wait_ge(s_dn, t + 1)
                        dve.tensor_tensor(yn[0:n, t, :], yn[0:n, t, :], down[t % 4][0:n, :], ALU.add).then_inc(s_add, 1)
                    hidden(1, 1)
                    add(0, 0)
                    with dve.Fori(1, XE // 2) as u:
                        hidden(0, u * 2)
                        add(1, u * 2 - 1)
                        hidden(1, u * 2 + 1)
                        add(0, u * 2)
                    add(1, XE - 1)
                    dve.wait_ge(s_add, (XE + 1) * NT)
                    for t in range(NT):
                        step(dve.bn_stats(stats[:], yn[:, t, :]))
                        ins = dve.bn_aggr(mv[:, t, :], stats[:])
                        if t == NT - 1:
                            ins.then_inc(s_var, 1)
                        else:
                            step(ins)
                    dve.wait_ge(s_dev, 1)
                    step(dve.reciprocal(rstd[:], std[:]))
                    for t in range(NT):
                        step(dve.tensor_scalar(yn[:, t, :], yn[:, t, :], mv[:, t, 0:1], rstd[:, t:t + 1], ALU.subtract, ALU.mult))
                        step(dve.tensor_tensor(yn[:, t, :], yn[:, t, :], ln_g[:], ALU.mult))
                        dve.tensor_tensor(yn[:, t, :], yn[:, t, :], x1[:, t, :], ALU.add).then_inc(s_out, 1)


def lay_out(v):
    import numpy as np
    c = np.ascontiguousarray
    n_pad = EC * P - E
    loops = np.arange(NP, dtype=np.int32)
    tail = np.full(P, NP - 1, np.int32)
    src = np.concatenate([v["src"], np.full(n_pad, NP - 1, np.int32), loops, tail])
    dst = np.concatenate([v["dst"], np.full(n_pad, NP - 1, np.int32), loops, tail])
    attr = np.concatenate([v["edge_attr_4"], np.zeros((n_pad, 4), np.float32)])
    return {
        "x": v["x"],
        "src_cols": c(src.reshape(CH, P).T), "dst_cols": c(dst.reshape(CH, P).T), "dst_row": dst,
        "edge_attr": c(attr.reshape(EC, P, 4).transpose(1, 0, 2)),
        "gat_w": v["L0_gnn_W"], "gat_w_edge": v["L0_gnn_W_edge"], "att_src": v["L0_gnn_att_src"],
        "att_dst": v["L0_gnn_att_dst"], "att_edge": v["L0_gnn_att_edge"], "gat_bias": v["L0_gnn_bias"],
        "gamma": v["L0_gnn_gamma"], "beta": v["L0_gnn_beta"],
        "wq_t": c(v["L0_mix_Wq"].T), "wk_t": c(v["L0_mix_Wk"].T), "wv_t": c(v["L0_mix_Wv"].T), "wo_t": c(v["L0_mix_Wo"].T),
        "bq": v["L0_mix_bq"], "bk": v["L0_mix_bk"], "bv": v["L0_mix_bv"], "bo": v["L0_mix_bo"],
        "rc_w1": c(v["L0_ffn_rc_w1"].transpose(2, 1, 0)), "rc_b1": v["L0_ffn_rc_b1"],
        "rc_w2": c(v["L0_ffn_rc_w2"].transpose(2, 1, 0)), "rc_b2": v["L0_ffn_rc_b2"],
        "sh_w1": c(v["L0_ffn_sh_w1"].transpose(2, 1, 0)), "sh_b1": v["L0_ffn_sh_b1"],
        "sh_w2": c(v["L0_ffn_sh_w2"][:, :, 0].T), "sh_b2": v["L0_ffn_sh_b2"],
        "e_w1": v["L0_ffn_e_w1"], "e_b1_cols": c(v["L0_ffn_e_b1"].reshape(XE, HT, P).transpose(0, 2, 1)), "e_w2": v["L0_ffn_e_w2"], "e_b2": v["L0_ffn_e_b2"],
        "ln_g": v["L0_ffn_ln_g"], "ln_b": v["L0_ffn_ln_b"],
    }


def kernel(**inputs):
    import numpy as np
    import concourse.bacc as bacc
    from concourse.bass_utils import run_bass_kernel_spmd

    nc = bacc.Bacc("TRN2", target_bir_lowering=False, num_devices=1)
    laid = lay_out({name: np.asarray(v) for name, v in inputs.items()})
    arrays = {f"in_{name}": np.ascontiguousarray(v) for name, v in laid.items()}
    ins = {name: nc.dram_tensor(f"in_{name}", v.shape, mybir.dt.from_np(v.dtype), kind="ExternalInput").ap()
           for name, v in laid.items()}
    out = nc.dram_tensor("out_0_dram", (N, D), F32, kind="ExternalOutput").ap()
    layer(nc, ins, out)
    result = run_bass_kernel_spmd(nc, [arrays], core_ids=[0])
    return result.results[0]["out_0_dram"]
```

```python
from contextlib import ExitStack

import concourse.bass as bass
from concourse import mybir

F32 = mybir.dt.float32
F32R = mybir.dt.float32r
I32 = mybir.dt.int32
ALU = mybir.AluOpType
ACT = mybir.ActivationFunctionType
AX = mybir.AxisListType

P = 128
N = 1250
D = 512
KT = D // P
NT = -(-N // P)
NP = NT * P
LAST = N - (NT - 1) * P
SPANS = [(0, 512), (512, 512), (1024, N - 1024)]
FULL_SPANS = [(0, 512), (512, 512), (1024, NP - 1024)]

E = 20000
EC = -(-E // P)
CH = EC + NT + 1
GH, GC = 4, 128
SLOPE = 0.2
BN_EPS = LN_EPS = 1e-5
MH, MD = 8, 64
MIX_EPS = 1e-6
XE, HID = 10, 256
HT = HID // P
RC_TAPS, SH_TAPS = 3, 9
PAD = SH_TAPS // 2
PHASE_HEADS = MH // 2
PAIR = 2 * CH // PHASE_HEADS
GS = 12
SS = 4
assert CH % 12 == 0 and PAIR % 12 == 0
NEG = -3.0e38
SKIP = 1.0e6


class Steps:

    def __init__(self, eng, sem):
        self.eng, self.sem, self.done = eng, sem, 0

    def __call__(self, ins):
        self.done = self.done + 1
        ins.then_inc(self.sem, 1)
        self.eng.wait_ge(self.sem, self.done)


def rows(t):
    return P if t < NT - 1 else LAST


def layer(nc, a, out):
    ctx = ExitStack()

    def dram(name, shape, dt=F32):
        return nc.dram_tensor(name, shape, dt).ap()

    feature_table = dram("feature_table", [NP, D])
    source_table = dram("source_table", [NP, GH])
    target_table = dram("target_table", [NP, 2 * GH])
    max_table = dram("max_table", [NP * CH, GH])
    sums_table = [dram(f"sums_table{k}", [NP, D + GH]) for k in range(SS)]

    with ctx:
        def keep(name, shape, dt=F32):
            return ctx.enter_context(nc.sbuf_tensor(name, shape, dt))

        ident = keep("ident", [P, P])
        ones = keep("ones", [P, P])
        x1 = keep("x1", [P, NT, D])
        a_dst = keep("a_dst", [P, NT, GH])
        eps_ln = keep("eps_ln", [P, 1])
        gat = ExitStack()
        ctx.enter_context(gat)

        def gkeep(name, shape, dt=F32):
            return gat.enter_context(nc.sbuf_tensor(name, shape, dt))

        idx_i = gkeep("idx_i", [P, CH, 2], I32)
        dst_f = gkeep("dst_f", [P, CH])
        logit = gkeep("logit", [P, CH, GH])
        row_idx = gkeep("row_idx", [P, CH], I32)
        key = gkeep("key", [P, CH])
        before = gkeep("before", [P, P])

        mix = ExitStack()
        ctx.enter_context(mix)

        def mkeep(name, shape, dt=F32):
            return mix.enter_context(nc.sbuf_tensor(name, shape, dt))

        q_t = mkeep("q_t", [P, KT, NP])
        k_t = mkeep("k_t", [P, KT, NP])
        v_tok = mkeep("v_tok", [P, NT, D])
        with ExitStack() as s:
            def sb(name, shape, dt=F32):
                return s.enter_context(nc.sbuf_tensor(name, shape, dt))

            def sem(name):
                return s.enter_context(nc.semaphore(name))

            xn_t = sb("xn_t", [P, KT, NP])
            w_gat = sb("w_gat", [P, KT, D])
            w_att = sb("w_att", [P, KT, 2 * GH])
            att = sb("att", [P, 2, D])
            w_q = sb("w_q", [P, KT, D])
            w_k = sb("w_k", [P, KT, D])
            w_v = sb("w_v", [P, KT, D])
            b_qk = sb("b_qk", [P, 2, KT])
            b_v = sb("b_v", [P, D])
            xn = sb("xn", [P, 2, D])
            junk = sb("junk", [P, GC])
            stats = sb("stats", [P, 6])
            mv = sb("mv", [P, NT, 2])
            std = sb("std", [P, NT])
            rstd = sb("rstd", [P, NT])
            row = sb("row", [P, 2, D + GH])
            ksum = sb("ksum", [P, 2, 512])
            pair_ones = sb("pair_ones", [P, P])
            attr = sb("attr", [P, EC, 4])
            w_edge = sb("w_edge", [P, 4, D])
            att_edge = sb("att_edge", [P, D])
            v_edge = sb("v_edge", [P, 4, GH])
            mean = sb("mean", [P, 4])
            chunk_i = sb("chunk_i", [P, CH], I32)
            LOW = 2240
            LOW_PARTS = NP * CH * GH // P // LOW
            low = sb("low", [P, LOW])
            ps = [s.enter_context(nc.psum_tensor(f"ps{b}", [P, 512], F32)) for b in range(8)]
            s_in = sem("edges_loaded")
            s_low = sem("low_ready")
            s_init = sem("max_table_initialised")
            s_part = sem("attribute_sums_ready")
            s_mean = sem("attribute_mean_ready")
            s_x = sem("x_loaded")
            s_const = sem("constants_ready")
            s_zero = sem("x_padded")
            s_w = sem("weights_loaded")
            s_wq = sem("qkv_weights_loaded")
            s_stat = sem("variance_ready")
            s_std = sem("deviation_ready")
            s_xn = sem("xn_ready")
            s_tr = sem("xn_transposed")
            s_xt = sem("xn_t_ready")
            s_watt = sem("w_att_ready")
            s_h = sem("h_ready")
            s_row_h = sem("h_row_features_ready")
            s_row_a = sem("h_row_logits_ready")
            s_tab = [sem(f"h_row_{b}_stored") for b in range(2)]
            s_qk = sem("qk_ready")
            s_qk_out = sem("qk_copied")
            s_v = sem("v_ready")
            s_v_out = sem("v_copied")
            s_ks = sem("ksum_ready")
            s_ks_out = sem("q_scaled")
            s_d = sem("dve_steps")
            s_p = sem("pool_steps")

            with nc.Block() as block:
                @block.sync
                def _(sp):
                    sp.dma_start(x1[:, 0:NT - 1, :], a["x"][0:(NT - 1) * P, :].rearrange("(t p) d -> p t d", p=P)).then_inc(s_x, 16)
                    sp.wait_ge(s_zero, 1)
                    sp.dma_start(x1[0:LAST, NT - 1, :], a["x"][(NT - 1) * P:N, :]).then_inc(s_x, 16)
                    sp.dma_start(w_gat[:], a["gat_w"].rearrange("(k p) o -> p k o", p=P)).then_inc(s_w, 16)
                    sp.dma_start(att[:, 0, :], a["att_src"].rearrange("h c -> (h c)").partition_broadcast(P)).then_inc(s_w, 16)
                    sp.dma_start(att[:, 1, :], a["att_dst"].rearrange("h c -> (h c)").partition_broadcast(P)).then_inc(s_w, 16)
                    for w, name in ((w_q, "wq_t"), (w_k, "wk_t"), (w_v, "wv_t")):
                        sp.dma_start(w[:], a[name].rearrange("(k p) o -> p k o", p=P)).then_inc(s_wq, 16)
                    with nc.allow_non_contiguous_dma(reason="biases of 512 numbers, one for a partition"):
                        sp.dma_start(b_qk[:, 0, :], a["bq"].rearrange("(k p) -> p k", p=P)).then_inc(s_wq, 16)
                        sp.dma_start(b_qk[:, 1, :], a["bk"].rearrange("(k p) -> p k", p=P)).then_inc(s_wq, 16)
                    sp.dma_start(b_v[:], a["bv"].partition_broadcast(P)).then_inc(s_wq, 16)
                    sp.dma_start(idx_i[:], a["edges"]).then_inc(s_in, 16)
                    sp.dma_start(attr[:], a["edge_attr"]).then_inc(s_in, 16)
                    sp.dma_start(w_edge[:], a["gat_w_edge"].rearrange("k c -> (k c)").partition_broadcast(P)
                                 .rearrange("p (k c) -> p k c", k=4)).then_inc(s_in, 16)
                    sp.dma_start(att_edge[:], a["att_edge"].rearrange("h c -> (h c)").partition_broadcast(P)).then_inc(s_in, 16)
                    sp.wait_ge(s_low, 1)
                    table = max_table.rearrange("(p r w) h -> p r (w h)", p=P, r=LOW_PARTS)
                    for r in range(LOW_PARTS):
                        sp.dma_start(table[:, r, :], low[:]).then_inc(s_init, 16)
                    for t in range(NT):
                        sp.wait_ge(s_row_h, t + 1)
                        sp.dma_start(feature_table[t * P:(t + 1) * P, :], row[:, t % 2, 0:D]).then_inc(s_tab[t % 2], 16)
                        sp.wait_ge(s_row_a, t + 1)
                        sp.dma_start(source_table[t * P:(t + 1) * P, :], row[:, t % 2, D:D + GH]).then_inc(s_tab[t % 2], 16)
                    for b in range(2):
                        sp.wait_ge(s_tab[b], 32 * NT // 2)
                    sp.wait_ge(s_init, 16 * LOW_PARTS)

                @block.gpsimd
                def _(pool):
                    step = Steps(pool, s_p)
                    pool.memset(x1[:, NT - 1, :], 0.0).then_inc(s_zero, 1)
                    pool.memset(eps_ln[:], LN_EPS).then_inc(s_const, 1)
                    step(pool.memset(ones[:], 1.0))
                    step(pool.memset(ident[:], 0.0))
                    step(pool.memset(pair_ones[:], 0.0))
                    step(pool.memset(pair_ones[0:MD, 0:MD], 1.0))
                    step(pool.memset(pair_ones[MD:P, MD:P], 1.0))
                    pool.affine_select(out=ident[:], in_=ident[:], compare_op=ALU.not_equal, fill=1.0, base=0,
                                       pattern=[[-1, P]], channel_multiplier=1).then_inc(s_const, 1)
                    pool.iota(chunk_i[:], pattern=[[1, CH]], base=0, channel_multiplier=0).then_inc(s_const, 1)
                    step(pool.memset(before[:], 1.0))
                    pool.affine_select(out=before[:], in_=before[:], compare_op=ALU.is_ge, fill=0.0, base=-1,
                                       pattern=[[-1, P]], channel_multiplier=1).then_inc(s_const, 1)

                @block.vector
                def _(dve):
                    step = Steps(dve, s_d)
                    dve.memset(low[:], NEG).then_inc(s_low, 1)
                    dve.wait_ge(s_x, 32)
                    for t in range(NT):
                        step(dve.bn_stats(stats[:], x1[:, t, :]))
                        ins = dve.bn_aggr(mv[:, t, :], stats[:])
                        if t == NT - 1:
                            ins.then_inc(s_stat, 1)
                        else:
                            step(ins)
                    dve.wait_ge(s_w, 48)
                    for k in range(KT):
                        for j in range(2):
                            for h in range(GH):
                                cols = slice(h * GC, (h + 1) * GC)
                                step(dve.tensor_tensor_reduce(out=junk[:], in0=w_gat[:, k, cols], in1=att[:, j, cols],
                                                              scale=1.0, scalar=0.0, op0=ALU.mult, op1=ALU.add,
                                                              accum_out=w_att[:, k, j * GH + h:j * GH + h + 1]))
                    dve.wait_ge(s_std, 1)
                    step(dve.reciprocal(rstd[:], std[:]))
                    for t in range(NT):
                        if t >= 2:
                            dve.wait_ge(s_tr, t - 1)
                        dve.tensor_scalar(xn[:, t % 2, :], x1[:, t, :], mv[:, t, 0:1], rstd[:, t:t + 1],
                                          ALU.subtract, ALU.mult).then_inc(s_xn, 1)
                        if t >= 1:
                            dve.wait_ge(s_tr, t)
                            dve.tensor_copy(xn_t[:, :, (t - 1) * P:t * P],
                                            ps[(t - 1) % 2][:].rearrange("p (k n) -> p k n", k=KT)).then_inc(s_xt, 1)
                    dve.wait_ge(s_tr, NT)
                    dve.tensor_copy(xn_t[:, :, (NT - 1) * P:NT * P],
                                    ps[(NT - 1) % 2][:].rearrange("p (k n) -> p k n", k=KT)).then_inc(s_xt, 1)
                    for t in range(NT):
                        dve.wait_ge(s_h, t + 1)
                        if t >= 2:
                            dve.wait_ge(s_tab[t % 2], 32 * (t // 2))
                        dve.tensor_copy(a_dst[:, t, :], ps[4 + t % 2][:, GH:2 * GH])
                        dve.tensor_copy(row[:, t % 2, D:D + GH], ps[4 + t % 2][:, 0:GH]).then_inc(s_row_a, 1)
                    dve.wait_ge(s_in, 64)
                    step(dve.tensor_tensor(w_edge[:], w_edge[:], att_edge[:].unsqueeze(1).broadcast_to([P, 4, D]), ALU.mult))
                    step(dve.tensor_reduce(v_edge[:], w_edge[:].rearrange("p k (h c) -> p k h c", c=GC), AX.X, ALU.add))
                    dve.tensor_reduce(mean[:], attr[:].rearrange("p c k -> p k c"), AX.X, ALU.add).then_inc(s_part, 1)
                    dve.wait_ge(s_mean, 1)
                    step(dve.tensor_scalar(mean[:], ps[3][:, 0:4], 1.0 / E, None, ALU.mult))
                    for h in range(GH):
                        for k in range(4):
                            real, loops = logit[:, 0:EC, h], logit[:, EC:CH, h]
                            again = mean[:, k:k + 1].broadcast_to([P, CH - EC])
                            if k == 0:
                                dve.tensor_scalar(real, attr[:, :, k], v_edge[:, k, h:h + 1], None, ALU.mult)
                                step(dve.tensor_scalar(loops, again, v_edge[:, k, h:h + 1], None, ALU.mult))
                            else:
                                dve.scalar_tensor_tensor(out=real, in0=attr[:, :, k], scalar=v_edge[:, k, h:h + 1],
                                                         in1=real, op0=ALU.mult, op1=ALU.add)
                                step(dve.scalar_tensor_tensor(out=loops, in0=again, scalar=v_edge[:, k, h:h + 1],
                                                              in1=loops, op0=ALU.mult, op1=ALU.add))
                    step(dve.tensor_copy(dst_f[:], idx_i[:, :, 1]))
                    dve.wait_ge(s_const, 4)
                    step(dve.scalar_tensor_tensor(out=key[:], in0=dst_f[:], scalar=float(CH), in1=chunk_i[:],
                                                  op0=ALU.mult, op1=ALU.add))
                    for t in range(NT):
                        dve.wait_ge(s_v, t + 1)
                        dve.tensor_tensor(v_tok[:, t, :], ps[6 + t % 2][:], b_v[:], ALU.add).then_inc(s_v_out, 1)
                    for m in range(KT):
                        for j, (at, n) in enumerate(FULL_SPANS):
                            i = m * len(SPANS) + j
                            dve.wait_ge(s_ks, i + 1)
                            step(dve.tensor_scalar(ksum[:, i % 2, 0:n], ps[4 + i % 2][:, 0:n], MIX_EPS, None, ALU.add))
                            step(dve.reciprocal(ksum[:, i % 2, 0:n], ksum[:, i % 2, 0:n]))
                            dve.tensor_tensor(q_t[:, m, at:at + n], q_t[:, m, at:at + n], ksum[:, i % 2, 0:n],
                                              ALU.mult).then_inc(s_ks_out, 1)

                @block.scalar
                def _(act):
                    act.wait_ge(s_stat, 1)
                    act.wait_ge(s_const, 2)
                    act.activation(std[:], mv[:, :, 1], ACT.Sqrt, bias=eps_ln[:]).then_inc(s_std, 1)
                    for t in range(NT):
                        act.wait_ge(s_h, t + 1)
                        if t >= 2:
                            act.wait_ge(s_tab[t % 2], 32 * (t // 2))
                        act.copy(row[:, t % 2, 0:D], ps[2 + t % 2][:]).then_inc(s_row_h, 1)
                    act.wait_ge(s_wq, 96)
                    i = 0
                    for j, dst in enumerate((q_t, k_t)):
                        for m in range(KT):
                            for at, n in FULL_SPANS:
                                act.wait_ge(s_qk, i + 1)
                                act.activation(dst[:, m, at:at + n], ps[i % 2][:, 0:n], ACT.Relu,
                                               bias=b_qk[:, j, m:m + 1]).then_inc(s_qk_out, 1)
                                i += 1

                @block.tensor
                def _(pe):
                    pe.wait_ge(s_const, 2)
                    for t in range(NT):
                        pe.wait_ge(s_xn, t + 1)
                        if t >= 2:
                            pe.wait_ge(s_xt, t - 1)
                        for k in range(KT):
                            ins = pe.transpose(ps[t % 2][:, k * P:(k + 1) * P], xn[:, t % 2, k * P:(k + 1) * P], ident[:])
                        ins.then_inc(s_tr, 1)
                    pe.wait_ge(s_xt, NT)
                    pe.wait_ge(s_d, 2 * NT - 1 + 2 * GH * KT)
                    for t in range(NT):
                        if t >= 2:
                            pe.wait_ge(s_row_h, t - 1)
                            pe.wait_ge(s_row_a, t - 1)
                        for k in range(KT):
                            pe.matmul(ps[2 + t % 2][:], xn_t[:, k, t * P:(t + 1) * P], w_gat[:, k, :],
                                      start=(k == 0), stop=(k == KT - 1))
                        for k in range(KT):
                            ins = pe.matmul(ps[4 + t % 2][:, 0:2 * GH], xn_t[:, k, t * P:(t + 1) * P], w_att[:, k, :],
                                            start=(k == 0), stop=(k == KT - 1))
                        ins.then_inc(s_h, 1)
                    pe.wait_ge(s_wq, 96)
                    pe.wait_ge(s_row_h, NT)
                    pe.wait_ge(s_part, 1)
                    pe.matmul(ps[3][:, 0:4], ones[:], mean[:], start=True, stop=True).then_inc(s_mean, 1)
                    for t in range(NT):
                        if t >= 2:
                            pe.wait_ge(s_v_out, t - 1)
                        for k in range(KT):
                            ins = pe.matmul(ps[6 + t % 2][:], xn_t[:, k, t * P:(t + 1) * P], w_v[:, k, :],
                                            start=(k == 0), stop=(k == KT - 1))
                        ins.then_inc(s_v, 1)
                    i = 0
                    for w in (w_q, w_k):
                        for m in range(KT):
                            for at, n in FULL_SPANS:
                                if i >= 2:
                                    pe.wait_ge(s_qk_out, i - 1)
                                for k in range(KT):
                                    ins = pe.matmul(ps[i % 2][:, 0:n], w[:, k, m * P:(m + 1) * P], xn_t[:, k, at:at + n],
                                                    start=(k == 0), stop=(k == KT - 1))
                                ins.then_inc(s_qk, 1)
                                i += 1
                    pe.wait_ge(s_qk_out, i)
                    pe.wait_ge(s_row_a, NT)
                    for m in range(KT):
                        for j, (at, n) in enumerate(FULL_SPANS):
                            i = m * len(SPANS) + j
                            if i >= 2:
                                pe.wait_ge(s_ks_out, i - 1)
                            pe.matmul(ps[4 + i % 2][:, 0:n], pair_ones[:], k_t[:, m, at:at + n],
                                      start=True, stop=True).then_inc(s_ks, 1)

        att_out = mkeep("att_out", [P, KT, NP])

        UNITS = [(j, m) for j in range(3) for m in range(NT)]
        NU = len(UNITS)
        TILES = [(t, j) for t in range(NT) for j in range(3)]
        q_now = [mkeep(f"q_now{b}", [MD + 1, NP]) for b in range(2)]
        k_now = [mkeep(f"k_now{b}", [MD + 1, N]) for b in range(2)]
        v_now = [mkeep(f"v_now{b}", [P, NT, 2 * MD]) for b in range(2)]

        class Attention:

            def __init__(self, s, phase):
                def sb(name, shape, dt=F32):
                    return s.enter_context(nc.sbuf_tensor(f"{name}_{phase}", shape, dt))

                def psum(name):
                    return s.enter_context(nc.psum_tensor(f"{name}_{phase}", [P, 512], F32))

                def sem(name):
                    return s.enter_context(nc.semaphore(f"{name}_{phase}"))

                self.phase = phase
                self.pre = 1 - phase
                self.q_round = sb("q_round", [MD, NP], F32R)
                self.k_round = sb("k_round", [MD, N], F32R)
                self.prob = sb("prob", [P, 3, 512])
                self.part_max = sb("part_max", [P, NT, 3])
                self.neg_max = sb("neg_max", [P, NT])
                self.raw = sb("raw", [P, 2, 512])
                self.inv = sb("inv", [MD, 2, 512])
                self.logits_nm = psum("logits_nm")
                self.logits_mn = [psum(f"logits_mn{b}") for b in range(2)]
                self.summed = psum("summed")
                self.s_one = sem("constant_columns_ready")
                self.s_stage = [sem(f"head_{b}_staged") for b in range(2)]
                self.s_round = sem("qk_rounded")
                self.s_nm = sem("logits_nm_ready")
                self.s_max = sem("part_max_ready")
                self.s_neg = sem("neg_max_ready")
                self.s_row = sem("max_row_ready")
                self.s_rowc = sem("max_row_copied")
                self.s_mn = sem("logits_mn_ready")
                self.s_pr = sem("prob_ready")
                self.s_pv = sem("prob_used")
                self.s_raw = sem("sums_copied")
                self.s_inv = sem("inverse_ready")
                self.s_att = sem("span_done")

            def stage(self, sp, b, pair):
                lo = b * MD
                sp.dma_start(q_now[b][0:MD, :], q_t[lo:lo + MD, pair, :]).then_inc(self.s_stage[b], 16)
                sp.dma_start(k_now[b][0:MD, :], k_t[lo:lo + MD, pair, 0:N]).then_inc(self.s_stage[b], 16)
                sp.dma_start(v_now[b][:, :, 0:MD], v_tok[:, :, (pair * 2 + b) * MD:(pair * 2 + b + 1) * MD]).then_inc(self.s_stage[b], 16)

            def stage_next(self, sp, h):
                sp.wait_ge(self.s_raw, 3 * h + 3)
                if self.phase == 0 or h < 2:
                    self.stage(sp, h % 2, PHASE_HEADS // 2 * self.phase + h // 2 + 1)
                elif h == 2:
                    self.stage(sp, 0, MH // 2 - 1)

            def tile_logits(self, pe, made, i):
                t, j = TILES[i]
                at, n = SPANS[j]
                if i == 0:
                    pe.wait_ge(self.s_round, made * 2 + 2)
                    pe.wait_ge(self.s_rowc, made * 3)
                pe.wait_ge(self.s_max, made * NU + i)
                pe.matmul(self.logits_nm[:, 0:n], self.q_round[:, t * P:(t + 1) * P], self.k_round[:, at:at + n],
                          start=True, stop=True).then_inc(self.s_nm, 1)

            def max_row(self, pe, made, j):
                at, n = FULL_SPANS[j]
                pe.wait_ge(self.s_neg, made + 1)
                if j:
                    pe.wait_ge(self.s_rowc, made * 3 + j)
                for t in range(at // P, (at + n) // P):
                    ins = pe.matmul(self.logits_nm[0:1, t * P - at:(t + 1) * P - at], self.neg_max[:, t:t + 1], ident[:],
                                    start=True, stop=True)
                ins.then_inc(self.s_row, 1)

            def score(self, pe, h, b, u):
                j, m = UNITS[u]
                at, n = FULL_SPANS[j]
                if u > 1:
                    pe.wait_ge(self.s_pr, h * NU + (u - 1))
                pe.matmul(self.logits_mn[u % 2][0:rows(m), 0:n], k_now[b][:, m * P:m * P + rows(m)], q_now[b][:, at:at + n],
                          start=True, stop=True).then_inc(self.s_mn, 1)

            def product(self, pe, h, b, u):
                j, m = UNITS[u]
                n = FULL_SPANS[j][1]
                pe.wait_ge(self.s_pr, h * NU + (u + 1))
                if m == 0:
                    pe.wait_ge(self.s_raw, h * 3 + j)
                pe.matmul(self.summed[:, 0:n], v_now[b][0:rows(m), m, :], self.prob[0:rows(m), u % 3, 0:n],
                          start=(m == 0), stop=(m == NT - 1)).then_inc(self.s_pv, 1)

            def pe_start(self, pe):
                if self.phase == 0:
                    pe.wait_ge(self.s_one, 4)
                    pe.wait_ge(self.s_stage[0], 48)
                    for i in range(NU):
                        self.tile_logits(pe, 0, i)
                    for j in range(3):
                        self.max_row(pe, 0, j)

            def pe_unit(self, pe, p, b, u):
                h = p * 2 + b
                made = h + self.pre
                if u == 0:
                    pe.wait_ge(self.s_rowc, made * 3)
                    if b == 1 or self.phase == 0:
                        pe.wait_ge(self.s_stage[b], (p + self.pre) * 48)
                    self.score(pe, h, b, 0)
                if u + 1 < NU:
                    self.score(pe, h, b, u + 1)
                if u:
                    self.product(pe, h, b, u - 1)
                if u == NU - 1:
                    self.product(pe, h, b, u)
                for i in NEXT_AFTER[u]:
                    self.tile_logits(pe, made, i)
                if u == NU - 1:
                    for j in range(3):
                        self.max_row(pe, made, j)

            def round_next(self, dve, b, staged, made):
                dve.wait_ge(self.s_stage[b], staged)
                dve.wait_ge(self.s_nm, made * NU)
                dve.tensor_copy(self.q_round[:], q_now[b][0:MD, :]).then_inc(self.s_round, 1)
                dve.tensor_copy(self.k_round[:], k_now[b][0:MD, :]).then_inc(self.s_round, 1)

            def maximum(self, dve, made, i):
                t, j = TILES[i]
                n = SPANS[j][1]
                dve.wait_ge(self.s_nm, made * NU + (i + 1))
                dve.tensor_reduce(self.part_max[:, t, j:j + 1], self.logits_nm[:, 0:n], AX.X, ALU.max,
                                  negate=True).then_inc(self.s_max, 1)

            def join_maxima(self, dve, made):
                dve.wait_ge(self.s_max, made * NU + NU)
                dve.tensor_reduce(self.neg_max[:], self.part_max[:], AX.X, ALU.min).then_inc(self.s_neg, 1)

            def finish(self, dve, h, b, j, pair):
                at, n = FULL_SPANS[j]
                r = (b + j) % 2
                dve.wait_ge(self.s_raw, h * 3 + (j + 1))
                dve.reciprocal(self.inv[:, r, 0:n], self.raw[MD:P, r, 0:n]).then_inc(self.s_inv, 1)
                dve.wait_ge(self.s_inv, h * 3 + (j + 1))
                dve.tensor_tensor(att_out[b * MD:(b + 1) * MD, bass.ds(pair, 1), at:at + n], self.raw[0:MD, r, 0:n],
                                  self.inv[:, r, 0:n], ALU.mult).then_inc(self.s_att, 1)

            def dve_start(self, dve):
                if self.phase == 0:
                    for b in range(2):
                        dve.memset(k_now[b][MD:MD + 1, :], 1.0).then_inc(self.s_one, 1)
                        dve.memset(v_now[b][:, :, MD:2 * MD], 1.0).then_inc(self.s_one, 1)
                    self.round_next(dve, 0, 48, 0)
                    for i in range(NU):
                        self.maximum(dve, 0, i)
                    self.join_maxima(dve, 0)

            def dve_unit(self, dve, p, b, u):
                h = p * 2 + b
                made = h + self.pre
                if u == ROUND_AT:
                    self.round_next(dve, 1 - b, (p + (self.pre if b == 0 else self.pre + 1)) * 48, made)
                for i in NEXT_AFTER[u]:
                    self.maximum(dve, made, i)
                if u == NU - 1:
                    self.join_maxima(dve, made)
                for j in range(3):
                    if u == min(NT * (j + 1) + 2, NU - 1):
                        self.finish(dve, h, b, j, p + PHASE_HEADS // 2 * self.phase)

            def row(self, act, made, b, j):
                at, n = FULL_SPANS[j]
                act.wait_ge(self.s_row, made * 3 + (j + 1))
                act.copy(q_now[b][MD:MD + 1, at:at + n], self.logits_nm[0:1, 0:n]).then_inc(self.s_rowc, 1)

            def act_start(self, act):
                if self.phase == 0:
                    for j in range(3):
                        self.row(act, 0, 0, j)

            def copy_sums(self, act, h, b, j):
                n = FULL_SPANS[j][1]
                act.wait_ge(self.s_att, h * 3 + max(j - 1, 0))
                act.wait_ge(self.s_pv, h * NU + NT * (j + 1))
                act.copy(self.raw[:, (b + j) % 2, 0:n], self.summed[:, 0:n]).then_inc(self.s_raw, 1)

            def act_unit(self, act, p, b, u):
                h = p * 2 + b
                j, m = UNITS[u]
                n = FULL_SPANS[j][1]
                if u == 0 or u > 2:
                    act.wait_ge(self.s_pv, h * NU + max(u - 2, 0))
                act.wait_ge(self.s_mn, h * NU + (u + 1))
                act.activation(self.prob[0:rows(m), u % 3, 0:n], self.logits_mn[u % 2][0:rows(m), 0:n],
                               ACT.Exp).then_inc(self.s_pr, 1)
                for j in range(2):
                    if u == NT * (j + 1) + 1:
                        self.copy_sums(act, h, b, j)
                if u == NU - 1:
                    self.copy_sums(act, h, b, 2)
                    for j in range(3):
                        self.row(act, h + self.pre, 1 - b, j)

        ROUND_AT = 3
        NEXT_AFTER = [[i for i in range(NU) if ROUND_AT + 1 + i * (NU - ROUND_AT - 1) // NU == u] for u in range(NU)]
        EDGES_AFTER = [[i for i in range(PAIR // 2) if i * NU // (PAIR // 2) == u] for u in range(NU)]

        LAGS = 5

        def beside(eng, unit, edges):
            with eng.Fori(0, PHASE_HEADS // 2) as p:
                for b in range(2):
                    for u in range(NU):
                        unit(eng, p, b, u)
                        for i in EDGES_AFTER[u]:
                            edges(p, b * PAIR // 2 + i)
                for i in range(PAIR, PAIR + LAGS):
                    edges(p, i)

        def load_rows(sp, attention, load, used):
            for k in range(SS):
                load(k, k)
            for h in range(PHASE_HEADS):
                n = PAIR // 2 - (SS if h == PHASE_HEADS - 1 else 0)
                base = h * PAIR // 2
                with sp.Fori(0, n // SS) as t:
                    for r in range(SS):
                        sp.wait_ge(used, t * SS + (base + r + 1))
                        load((base + r) % SS, t * SS + (base + r + SS))
                for r in range(n // SS * SS, n):
                    sp.wait_ge(used, base + r + 1)
                    load((base + r) % SS, base + r + SS)
                attention.stage_next(sp, h)

        s_got = [mix.enter_context(nc.semaphore(f"slot_{k}_gathered")) for k in range(GS)]
        with ExitStack() as s:
            def sb(name, shape, dt=F32):
                return s.enter_context(nc.sbuf_tensor(name, shape, dt))

            def sem(name):
                return s.enter_context(nc.semaphore(name))

            attention = Attention(s, 0)
            src_now = [sb(f"src_now{k}", [P, 1], I32) for k in range(GS)]
            source_now = [sb(f"source_now{k}", [P, GH]) for k in range(GS)]
            targets = [sb(f"targets{k}", [P, P], I32) for k in range(SS)]
            logit_now = [sb(f"logit_now{k}", [P, GH]) for k in range(SS)]
            other = [sb(f"other{k}", [P, P]) for k in range(SS)]
            earlier = [sb(f"earlier{k}", [P, 1]) for k in range(SS)]
            scratch_f = [sb(f"scratch_f{k}", [P, P]) for k in range(SS)]
            scratch_m = [sb(f"scratch_m{k}", [P, GH, P]) for k in range(SS)]
            max_now = [sb(f"max_now{k}", [P, GH]) for k in range(SS)]
            key_now = [sb(f"key_now{k}", [P, 1], I32) for k in range(SS)]
            spread = [s.enter_context(nc.psum_tensor(f"spread{k}", [P, GH, P], F32)) for k in range(2)]
            s_row = [sem(f"targets_{k}_loaded") for k in range(SS)]
            s_idx = sem("source_indices_written")
            s_first = sem("first_edges_found")
            s_lg = sem("logits_ready")
            s_lc = sem("logits_kept")
            s_sp = sem("logits_spread")
            s_mx = sem("maxima_ready")
            s_put = [sem(f"maxima_{k}_stored") for k in range(SS)]
            with nc.Block() as block:
                @block.sync
                def _(sp):
                    def load(k, c):
                        sp.dma_start(targets[k][:], a["dst_row"][bass.ds(c * P, P)].partition_broadcast(P)).then_inc(s_row[k], 16)

                    for b in range(2):
                        attention.stage(sp, b, 0)
                    load_rows(sp, attention, load, s_first)
                    for b in range(2):
                        sp.wait_ge(attention.s_stage[b], 48 * 3)

                @block.gpsimd
                def _(pool):
                    def copy_index(k, c):
                        pool.tensor_copy(src_now[k][:], idx_i[:, bass.ds(c, 1), 0]).then_inc(s_idx, 1)

                    def gather(k):
                        pool.indirect_dma_start(source_now[k][:], None, source_table,
                                                bass.IndirectOffsetOnAxis(ap=src_now[k][:], axis=0)).then_inc(s_got[k], 16)

                    def store(k):
                        pool.indirect_dma_start(max_table, bass.IndirectOffsetOnAxis(ap=key_now[k][:], axis=0),
                                                max_now[k][:], None, bounds_check=NP * CH - 1,
                                                oob_is_err=False).then_inc(s_put[k], 16)

                    for k in range(GS):
                        if k:
                            pool.wait_ge(s_idx, k)
                        copy_index(k, k)
                        if k:
                            gather(k - 1)
                    with pool.Fori(0, CH // 12 - 1) as t:
                        for i in range(12):
                            c = t * 12 + i
                            pool.wait_ge(s_mx, t * 12 + (i + 1))
                            pool.wait_ge(s_idx, t * 12 + (i + GS))
                            copy_index(i % GS, t * 12 + (i + GS))
                            store(i % SS)
                            gather((i + GS - 1) % GS)
                    for c in range(CH - 12, CH):
                        pool.wait_ge(s_mx, c + 1)
                        if c + GS - 1 < CH:
                            pool.wait_ge(s_idx, c + GS)
                            if c + GS < CH:
                                copy_index(c % GS, c + GS)
                        store(c % SS)
                        if c + GS - 1 < CH:
                            gather((c + GS - 1) % GS)
                    for k in range(SS):
                        pool.wait_ge(s_put[k], 16 * CH // SS)

                @block.vector
                def _(dve):
                    def first_edges(p, i):
                        c, k = p * PAIR + i, i % SS
                        dve.wait_ge(s_mx, p * PAIR + max(i - SS + 1, 0))
                        dve.wait_ge(s_row[k], (p * (PAIR // SS) + i // SS) * 16 + 16)
                        dve.tensor_scalar(other[k][:], targets[k][:], dst_f[:, bass.ds(c, 1)], NEG, ALU.not_equal, ALU.mult)
                        dve.scalar_tensor_tensor(out=scratch_f[k][:], in0=targets[k][:], scalar=dst_f[:, bass.ds(c, 1)], in1=before[:],
                                                 op0=ALU.is_equal, op1=ALU.mult, accum_out=earlier[k][:]).then_inc(s_first, 1)

                    def logits(p, i):
                        dve.wait_ge(s_got[i % GS], (p * (PAIR // GS) + i // GS) * 16 + 16)
                        dve.tensor_tensor(logit_now[i % SS][:], source_now[i % GS][:], logit[:, bass.ds(p * PAIR + i, 1), :],
                                          ALU.add).then_inc(s_lg, 1)

                    def maxima(p, i):
                        c, k = p * PAIR + i, i % SS
                        dve.wait_ge(s_lc, c + 1)
                        dve.wait_ge(s_sp, c + 1)
                        dve.wait_ge(s_first, c + 1)
                        dve.wait_ge(s_put[k], (p * (PAIR // SS) + i // SS) * 16)
                        dve.scalar_tensor_tensor(out=key_now[k][:], in0=earlier[k][:], scalar=SKIP,
                                                 in1=key[:, bass.ds(c, 1)], op0=ALU.mult, op1=ALU.add)
                        dve.scalar_tensor_tensor(out=row_idx[:, bass.ds(c, 1)], in0=earlier[k][:], scalar=SKIP,
                                                 in1=dst_f[:, bass.ds(c, 1)], op0=ALU.mult, op1=ALU.add)
                        for h in range(GH):
                            ins = dve.tensor_tensor_reduce(out=scratch_m[k][:, h, :], in0=spread[i % 2][:, h, :], in1=other[k][:],
                                                           scale=1.0, scalar=NEG, op0=ALU.add, op1=ALU.max,
                                                           accum_out=max_now[k][:, h:h + 1])
                        ins.then_inc(s_mx, 1)

                    def edges(p, i):
                        if i < PAIR:
                            first_edges(p, i)
                            logits(p, i)
                        if 0 <= i - 2 < PAIR:
                            maxima(p, i - 2)

                    attention.dve_start(dve)
                    beside(dve, attention.dve_unit, edges)

                @block.scalar
                def _(act):
                    def keep_logits(p, i):
                        act.wait_ge(s_lg, p * PAIR + (i + 1))
                        act.copy(logit[:, bass.ds(p * PAIR + i, 1), :], logit_now[i % SS][:]).then_inc(s_lc, 1)

                    def edges(p, i):
                        if 0 <= i - 1 < PAIR:
                            keep_logits(p, i - 1)

                    attention.act_start(act)
                    beside(act, attention.act_unit, edges)

                @block.tensor
                def _(pe):
                    def spread_logits(p, i):
                        c, k = p * PAIR + i, i % SS
                        pe.wait_ge(s_lg, c + 1)
                        pe.wait_ge(s_mx, p * PAIR + max(i - 1, 0))
                        for h in range(GH):
                            ins = pe.matmul(spread[i % 2][:, h, :], logit_now[k][:, h:h + 1].broadcast_to([P, P]), ident[:],
                                            start=True, stop=True)
                        ins.then_inc(s_sp, 1)

                    def edges(p, i):
                        if 0 <= i - 1 < PAIR:
                            spread_logits(p, i - 1)

                    attention.pe_start(pe)
                    beside(pe, attention.pe_unit, edges)

        with ExitStack() as s:
            def sb(name, shape, dt=F32):
                return s.enter_context(nc.sbuf_tensor(name, shape, dt))

            def sem(name):
                return s.enter_context(nc.semaphore(name))

            chunk_max = sb("chunk_max", [P, 3, CH, GH])
            node_max = sb("node_max", [P, NT, GH])
            target = sb("target", [P, NT, 2 * GH])
            zeros = sb("zeros", [P, NT * (D + GH)])
            s_cm = [sem(f"chunk_max_{b}_loaded") for b in range(3)]
            s_nm = sem("node_max_ready")
            s_tg = sem("target_ready")
            s_tab = sem("target_table_stored")
            s_z = sem("zeros_ready")
            s_clear = sem("sums_cleared")
            s_d = sem("dve_steps_max")
            with nc.Block() as block:
                @block.sync
                def _(sp):
                    table = max_table.rearrange("(t p c) h -> t p c h", p=P, c=CH)
                    for t in range(NT):
                        if t >= 3:
                            sp.wait_ge(s_nm, t - 2)
                        sp.dma_start(chunk_max[:, t % 3, :, :], table[t]).then_inc(s_cm[t % 3], 16)
                    sp.wait_ge(s_tg, 1)
                    sp.dma_start(target_table.rearrange("(t p) j -> p t j", p=P), target[:]).then_inc(s_tab, 16)
                    sp.wait_ge(s_tab, 16)

                @block.gpsimd
                def _(pool):
                    pool.memset(zeros[:], 0.0).then_inc(s_z, 1)

                @block.scalar
                def _(act):
                    act.wait_ge(s_z, 1)
                    for k in range(SS):
                        act.dma_start(sums_table[k].rearrange("(p t) j -> p (t j)", p=P), zeros[:]).then_inc(s_clear, 16)
                    act.wait_ge(s_clear, 16 * SS)

                @block.vector
                def _(dve):
                    step = Steps(dve, s_d)
                    for t in range(NT):
                        dve.wait_ge(s_cm[t % 3], 16 * (t // 3 + 1))
                        dve.tensor_reduce(node_max[:, t, :], chunk_max[:, t % 3, :, :].rearrange("p c h -> p h c"),
                                          AX.X, ALU.max).then_inc(s_nm, 1)
                    dve.wait_ge(s_nm, NT)
                    step(dve.tensor_tensor(node_max[:], node_max[:], a_dst[:], ALU.add))
                    dve.tensor_copy(target[:, :, 0:GH], a_dst[:])
                    dve.scalar_tensor_tensor(out=target[:, :, GH:2 * GH], in0=node_max[:], scalar=SLOPE, in1=node_max[:],
                                             op0=ALU.mult, op1=ALU.max).then_inc(s_tg, 1)

        with ExitStack() as s:
            def sb(name, shape, dt=F32):
                return s.enter_context(nc.sbuf_tensor(name, shape, dt))

            def sem(name):
                return s.enter_context(nc.semaphore(name))

            attention = Attention(s, 1)
            idx_now = [sb(f"idx_now{k}", [P, 2], I32) for k in range(GS)]
            feat = [sb(f"feat{k}", [P, D]) for k in range(GS)]
            target_now = [sb(f"target_now{k}", [P, 2 * GH]) for k in range(GS)]
            targets = [sb(f"targets2_{k}", [P, P], I32) for k in range(SS)]
            same = [sb(f"same{k}", [P, P]) for k in range(SS)]
            expo = [sb(f"expo{k}", [P, GH]) for k in range(SS)]
            weight = [sb(f"weight{k}", [P, GH]) for k in range(SS)]
            row_now = [sb(f"row_now{k}", [P, 1], I32) for k in range(SS)]
            summed_sb = [sb(f"summed_sb{k}", [P, D + GH]) for k in range(SS)]
            ps = [s.enter_context(nc.psum_tensor(f"gs{b}", [P, 512], F32)) for b in range(2)]
            pw = [s.enter_context(nc.psum_tensor(f"gw{b}", [P, 512], F32)) for b in range(2)]
            s_row = [sem(f"targets2_{k}_loaded") for k in range(SS)]
            s_idx = sem("indices_written")
            GOT = 16 * CH // GS
            s_same = sem("same_targets_found")
            s_ch = sem("exponent_chain")
            s_wt = sem("weights_ready")
            s_msg = sem("messages_ready")
            s_sum = sem("messages_summed")
            s_cpf = sem("sums_copied_by_scalar")
            s_cpw = sem("weight_sums_copied_by_vector")
            s_add = [sem(f"sums_{k}_added") for k in range(SS)]
            with nc.Block() as block:
                @block.sync
                def _(sp):
                    def load(k, c):
                        sp.dma_start(targets[k][:], a["dst_row"][bass.ds(c * P, P)].partition_broadcast(P)).then_inc(s_row[k], 16)

                    load_rows(sp, attention, load, s_same)
                    for b in range(2):
                        sp.wait_ge(attention.s_stage[b], 48 * (2 - b))

                @block.gpsimd
                def _(pool):
                    def copy_indices(k, c):
                        pool.tensor_copy(idx_now[k][:], idx_i[:, bass.ds(c, 1), :]).then_inc(s_idx, 1)

                    def gather(k):
                        pool.indirect_dma_start(target_now[k][:], None, target_table,
                                                bass.IndirectOffsetOnAxis(ap=idx_now[k][:, 1:2], axis=0)).then_inc(s_got[k], 16)
                        pool.indirect_dma_start(feat[k][:], None, feature_table,
                                                bass.IndirectOffsetOnAxis(ap=idx_now[k][:, 0:1], axis=0)).then_inc(s_got[k], 16)

                    def add(k):
                        pool.indirect_dma_start(sums_table[k], bass.IndirectOffsetOnAxis(ap=row_now[k][:], axis=0),
                                                summed_sb[k][:], None, bounds_check=NP - 1, oob_is_err=False,
                                                compute_op=ALU.add).then_inc(s_add[k], 16)

                    for k in range(GS):
                        if k:
                            pool.wait_ge(s_idx, k)
                        copy_indices(k, k)
                        if k:
                            gather(k - 1)
                    with pool.Fori(0, CH // 12 - 1) as t:
                        for i in range(12):
                            pool.wait_ge(s_cpf, t * 12 + (i + 1))
                            pool.wait_ge(s_cpw, t * 12 + (i + 1))
                            pool.wait_ge(s_idx, t * 12 + (i + GS))
                            copy_indices(i % GS, t * 12 + (i + GS))
                            add(i % SS)
                            gather((i + GS - 1) % GS)
                    for c in range(CH - 12, CH):
                        pool.wait_ge(s_cpf, c + 1)
                        pool.wait_ge(s_cpw, c + 1)
                        if c + GS - 1 < CH:
                            pool.wait_ge(s_idx, c + GS)
                            if c + GS < CH:
                                copy_indices(c % GS, c + GS)
                        add(c % SS)
                        if c + GS - 1 < CH:
                            gather((c + GS - 1) % GS)
                    for k in range(SS):
                        pool.wait_ge(s_add[k], 16 * CH // SS)

                @block.vector
                def _(dve):
                    def exponents(p, i):
                        c, k, g = p * PAIR + i, i % SS, i % GS
                        dve.wait_ge(s_row[k], (p * (PAIR // SS) + i // SS) * 16 + 16)
                        dve.tensor_scalar(same[k][:], targets[k][:], dst_f[:, bass.ds(c, 1)], None, ALU.is_equal).then_inc(s_same, 1)
                        dve.wait_ge(s_got[g], (p * (PAIR // GS) + i // GS) * 32 + (GOT + 32))
                        dve.tensor_tensor(expo[k][:], logit[:, bass.ds(c, 1), :], target_now[g][:, 0:GH], ALU.add).then_inc(s_ch, 1)
                        dve.wait_ge(s_ch, c * 3 + 1)
                        dve.scalar_tensor_tensor(out=expo[k][:], in0=expo[k][:], scalar=SLOPE, in1=expo[k][:],
                                                 op0=ALU.mult, op1=ALU.max).then_inc(s_ch, 1)
                        dve.wait_ge(s_ch, c * 3 + 2)
                        dve.tensor_tensor(expo[k][:], expo[k][:], target_now[g][:, GH:2 * GH], ALU.subtract).then_inc(s_ch, 1)

                    def messages(p, i):
                        c, g = p * PAIR + i, i % GS
                        dve.wait_ge(s_wt, c + 1)
                        f = feat[g][:].rearrange("p (h c) -> p h c", c=GC)
                        dve.tensor_tensor(f, f, weight[i % SS][:].unsqueeze(2).broadcast_to([P, GH, GC]), ALU.mult).then_inc(s_msg, 1)

                    def weight_sums(p, i):
                        c, k = p * PAIR + i, i % SS
                        dve.wait_ge(s_add[k], (p * (PAIR // SS) + i // SS) * 16)
                        dve.tensor_copy(row_now[k][:], row_idx[:, bass.ds(c, 1)])
                        dve.wait_ge(s_sum, c + 1)
                        dve.tensor_copy(summed_sb[k][:, D:D + GH], pw[i % 2][:, 0:GH]).then_inc(s_cpw, 1)

                    def edges(p, i):
                        if 0 <= i - 4 < PAIR:
                            weight_sums(p, i - 4)
                        if i < PAIR:
                            exponents(p, i)
                        if 0 <= i - 2 < PAIR:
                            messages(p, i - 2)

                    attention.dve_start(dve)
                    beside(dve, attention.dve_unit, edges)

                @block.scalar
                def _(act):
                    def copy_sums(p, i):
                        c, k, turn = p * PAIR + i, i % SS, p * (PAIR // SS) + i // SS
                        act.wait_ge(s_add[k], turn * 16)
                        act.wait_ge(s_sum, c + 1)
                        act.copy(summed_sb[k][:, 0:D], ps[i % 2][:]).then_inc(s_cpf, 1)

                    def weights(p, i):
                        act.wait_ge(s_ch, (p * PAIR + i) * 3 + 3)
                        act.activation(weight[i % SS][:], expo[i % SS][:], ACT.Exp).then_inc(s_wt, 1)

                    def edges(p, i):
                        if 0 <= i - 1 < PAIR:
                            weights(p, i - 1)
                        if 0 <= i - 4 < PAIR:
                            copy_sums(p, i - 4)

                    attention.act_start(act)
                    beside(act, attention.act_unit, edges)

                @block.tensor
                def _(pe):
                    def sum_messages(p, i):
                        c, b = p * PAIR + i, i % 2
                        pe.wait_ge(s_msg, c + 1)
                        pe.wait_ge(s_cpf, p * PAIR + max(i - 1, 0))
                        pe.wait_ge(s_cpw, p * PAIR + max(i - 1, 0))
                        pe.matmul(pw[b][:, 0:GH], same[i % SS][:], weight[i % SS][:], start=True, stop=True)
                        pe.matmul(ps[b][:], same[i % SS][:], feat[i % GS][:], start=True, stop=True).then_inc(s_sum, 1)

                    def edges(p, i):
                        if 0 <= i - 3 < PAIR:
                            sum_messages(p, i - 3)

                    attention.pe_start(pe)
                    beside(pe, attention.pe_unit, edges)

        with ExitStack() as s:
            def sb(name, shape, dt=F32):
                return s.enter_context(nc.sbuf_tensor(name, shape, dt))

            def sem(name):
                return s.enter_context(nc.semaphore(name))

            w_o = sb("w_o", [P, KT, D])
            b_o = sb("b_o", [P, D])
            ps = [s.enter_context(nc.psum_tensor(f"mo{b}", [P, 512], F32)) for b in range(2)]
            s_w = sem("wo_loaded")
            s_m = sem("mixed")
            s_x = sem("mix_added")
            s_b = sem("bias_added")
            with nc.Block() as block:
                @block.sync
                def _(sp):
                    sp.dma_start(w_o[:], a["wo_t"].rearrange("(k p) o -> p k o", p=P)).then_inc(s_w, 16)
                    sp.dma_start(b_o[:], a["bo"].partition_broadcast(P)).then_inc(s_w, 16)

                @block.tensor
                def _(pe):
                    pe.wait_ge(s_w, 32)
                    for t in range(NT):
                        if t >= 2:
                            pe.wait_ge(s_x, t - 1)
                        for k in range(KT):
                            ins = pe.matmul(ps[t % 2][:], att_out[:, k, t * P:(t + 1) * P], w_o[:, k, :],
                                            start=(k == 0), stop=(k == KT - 1))
                        ins.then_inc(s_m, 1)

                @block.vector
                def _(dve):
                    dve.wait_ge(s_w, 32)
                    for t in range(NT):
                        dve.tensor_tensor(x1[:, t, :], x1[:, t, :], b_o[:], ALU.add).then_inc(s_b, 1)
                    for t in range(NT):
                        dve.wait_ge(s_b, t + 1)
                        dve.wait_ge(s_m, t + 1)
                        dve.tensor_tensor(x1[:, t, :], x1[:, t, :], ps[t % 2][:], ALU.add).then_inc(s_x, 1)
        mix.close()
        gat.close()

        with ExitStack() as s:
            def sb(name, shape, dt=F32):
                return s.enter_context(nc.sbuf_tensor(name, shape, dt))

            def sem(name):
                return s.enter_context(nc.semaphore(name))

            got = [[sb(f"got{b}_{k}", [P, D + GH]) for k in range(SS)] for b in range(2)]
            node = sb("node", [P, NT, D])
            square = sb("square", [P, 2, D])
            weight = sb("weight", [P, 2, GH])
            bias = sb("bias", [P, D])
            gamma = sb("gamma", [P, D])
            beta = sb("beta", [P, D])
            scale = sb("scale", [P, D])
            eps_bn = sb("eps_bn", [P, 1])
            mean_ps = s.enter_context(nc.psum_tensor("mean_ps", [P, 512], F32))
            var_ps = s.enter_context(nc.psum_tensor("var_ps", [P, 512], F32))
            s_c = sem("batch_norm_constants_loaded")
            s_got = [sem(f"sums_{b}_loaded") for b in range(2)]
            s_free = sem("sums_read")
            s_node = sem("node_ready")
            s_mean = sem("mean_ready")
            s_sq = sem("square_ready")
            s_var = sem("variance_summed")
            s_varu = sem("squares_used")
            s_dev = sem("deviation_ready_bn")
            s_eps = sem("eps_ready")
            s_d = sem("dve_steps_bn")
            with nc.Block() as block:
                @block.sync
                def _(sp):
                    for t in range(NT):
                        b = t % 2
                        if t >= 2:
                            sp.wait_ge(s_free, t - 1)
                        for k in range(SS):
                            sp.dma_start(got[b][k][:], sums_table[k][t * P:(t + 1) * P, :]).then_inc(s_got[b], 16)
                        if t == 0:
                            for dst, name in ((bias, "gat_bias"), (gamma, "gamma"), (beta, "beta")):
                                sp.dma_start(dst[:], a[name].partition_broadcast(P)).then_inc(s_c, 16)

                @block.vector
                def _(dve):
                    step = Steps(dve, s_d)
                    dve.memset(eps_bn[:], BN_EPS).then_inc(s_eps, 1)
                    for t in range(NT):
                        b = t % 2
                        g = got[b]
                        dve.wait_ge(s_got[b], 16 * SS * (t // 2 + 1))
                        dve.tensor_tensor(g[0][:], g[0][:], g[1][:], ALU.add)
                        step(dve.tensor_tensor(g[2][:], g[2][:], g[3][:], ALU.add))
                        step(dve.tensor_tensor(g[0][:], g[0][:], g[2][:], ALU.add))
                        step(dve.tensor_scalar(weight[:, b, :], g[0][:, D:D + GH], 1e-16, None, ALU.add))
                        step(dve.reciprocal(weight[:, b, :], weight[:, b, :]))
                        f = g[0][:, 0:D].rearrange("p (h c) -> p h c", c=GC)
                        step(dve.tensor_tensor(f, f, weight[:, b, :].unsqueeze(2).broadcast_to([P, GH, GC]), ALU.mult))
                        if t == 0:
                            dve.wait_ge(s_c, 48)
                        ins = dve.tensor_tensor(node[:, t, :], g[0][:, 0:D], bias[:], ALU.add)
                        ins.then_inc(s_free, 1)
                    dve.wait_ge(s_mean, 1)
                    dve.wait_ge(s_free, NT)
                    for t in range(NT):
                        dve.scalar_tensor_tensor(out=node[:, t, :], in0=mean_ps[:], scalar=-1.0 / N, in1=node[:, t, :],
                                                 op0=ALU.mult, op1=ALU.add).then_inc(s_node, 1)
                    dve.wait_ge(s_dev, 1)
                    step(dve.reciprocal(scale[:], scale[:]))
                    step(dve.tensor_tensor(scale[:], scale[:], gamma[:], ALU.mult))
                    for t in range(NT):
                        dve.wait_ge(s_sq, t + 1)
                        step(dve.tensor_tensor(node[:, t, :], node[:, t, :], scale[:], ALU.mult))
                        step(dve.tensor_tensor(node[:, t, :], node[:, t, :], beta[:], ALU.add))
                        dve.tensor_tensor(x1[:, t, :], x1[:, t, :], node[:, t, :], ALU.add)

                @block.tensor
                def _(pe):
                    for t in range(NT):
                        pe.wait_ge(s_free, t + 1)
                        ins = pe.matmul(mean_ps[:], ones[0:rows(t), :], node[0:rows(t), t, :], start=(t == 0), stop=(t == NT - 1))
                    ins.then_inc(s_mean, 1)
                    for t in range(NT):
                        pe.wait_ge(s_sq, t + 1)
                        pe.matmul(var_ps[:], ones[0:rows(t), :], square[0:rows(t), t % 2, :], start=(t == 0),
                                  stop=(t == NT - 1)).then_inc(s_varu, 1)

                @block.scalar
                def _(act):
                    act.wait_ge(s_eps, 1)
                    for t in range(NT):
                        act.wait_ge(s_node, t + 1)
                        if t >= 2:
                            act.wait_ge(s_varu, t - 1)
                        act.activation(square[:, t % 2, :], node[:, t, :], ACT.Square).then_inc(s_sq, 1)
                    act.wait_ge(s_varu, NT)
                    act.activation(scale[:], var_ps[:], ACT.Sqrt, bias=eps_bn[:], scale=1.0 / N).then_inc(s_dev, 1)

        with ExitStack() as s:
            def sb(name, shape, dt=F32):
                return s.enter_context(nc.sbuf_tensor(name, shape, dt))

            def sem(name):
                return s.enter_context(nc.semaphore(name))

            HALO = NP + 2 * PAD
            yn = sb("yn", [P, NT, D])
            yn_t = sb("yn_t", [P, KT, HALO])
            rc_act = sb("rc_act", [P, KT, HALO])
            rc_w1 = sb("rc_w1", [P, RC_TAPS, KT, D])
            rc_w2 = sb("rc_w2", [P, RC_TAPS, KT, XE])
            sh_w1 = sb("sh_w1", [P, SH_TAPS, KT, HID])
            sh_w2 = sb("sh_w2", [P, HT, D])
            sh_act = sb("sh_act", [P, HT, N])
            rc_b1 = sb("rc_b1", [P, KT])
            rc_b2 = sb("rc_b2", [P, XE])
            sh_b1 = sb("sh_b1", [P, HT])
            e_b1 = [sb(f"e_b1_{b}", [P, HT]) for b in range(2)]
            out_bias = sb("out_bias", [XE + 1, D])
            ln_g = sb("ln_g", [P, D])
            ln_b = sb("ln_b", [P, D])
            e_w1 = [sb(f"e_w1_{b}", [P, KT, HID]) for b in range(2)]
            e_w2 = [sb(f"e_w2_{b}", [P, HT, D]) for b in range(2)]
            h_act = [sb(f"h_act{b}", [P, HT, N]) for b in range(2)]
            negative = sb("negative", [P, 2, 512])
            logits = sb("logits", [P, NT, XE])
            first = sb("first", [P, NT, XE])
            second = sb("second", [P, NT, XE])
            place = sb("place", [P, NT, XE])
            number = sb("number", [P, NT, XE])
            number_i = sb("number_i", [P, NT, XE], I32)
            top = sb("top", [P, 2, NT])
            which = sb("which", [P, NT])
            share = sb("share", [P, 2, NT])
            gates = sb("gates", [P, NT, XE + 1])
            gates_t = h_act[1][0:XE + 1, 0, :]
            stats = sb("f_stats", [P, 6])
            mv = sb("f_mv", [P, NT, 2])
            std = sb("f_std", [P, NT])
            rstd = sb("f_rstd", [P, NT])
            up = [s.enter_context(nc.psum_tensor(f"up{b}", [P, 512], F32)) for b in range(4)]
            down = [s.enter_context(nc.psum_tensor(f"down{b}", [P, 512], F32)) for b in range(4)]
            s_rcw = sem("router_weights_loaded")
            s_shw = sem("shared_weights_loaded")
            s_bias = sem("biases_loaded")
            s_exp = [sem(f"expert_{b}_loaded") for b in range(2)]
            s_iota = sem("expert_numbers_ready")
            s_zero = sem("halos_zeroed")
            s_stat = sem("x1_variance_ready")
            s_std = sem("x1_deviation_ready")
            s_yn = sem("yn_ready")
            s_tr = sem("yn_transposed")
            s_yt = sem("yn_t_ready")
            s_unit = sem("hidden_unit_ready")
            s_act = sem("hidden_unit_activated")
            s_low = sem("hidden_unit_minimum_taken")
            s_ex = sem("hidden_unit_exponent_ready")
            s_h = sem("expert_hidden_unit_ready")
            s_lg = sem("router_logits_ready")
            s_lgc = sem("router_logits_copied")
            s_gap = sem("top_difference_ready")
            s_gx = sem("top_exponent_ready")
            s_gate = sem("gates_ready")
            s_gt = sem("gates_transposed")
            s_gtc = sem("gates_t_ready")
            s_dn = sem("token_tile_ready")
            s_add = sem("token_tile_added")
            s_var = sem("z_variance_ready")
            s_dev = sem("z_deviation_ready")
            s_out = sem("out_tile_ready")
            s_st = sem("out_stored")
            s_d = sem("dve_steps_ffn")
            CONV = (KT + HT) * 3
            EU = HT * 3

            with nc.Block() as block:
                @block.sync
                def _(sp):
                    sp.dma_start(rc_w1[:], a["rc_w1"].rearrange("j (k p) o -> p j k o", p=P)).then_inc(s_rcw, 16)
                    with nc.allow_non_contiguous_dma(reason="small vectors, one number for a partition"):
                        sp.dma_start(rc_b1[:], a["rc_b1"].rearrange("(k p) -> p k", p=P)).then_inc(s_bias, 16)
                        sp.dma_start(sh_b1[:], a["sh_b1"].rearrange("(k p) -> p k", p=P)).then_inc(s_bias, 16)
                        sp.dma_start(rc_w2[:], a["rc_w2"].rearrange("j (k p) o -> p j k o", p=P)).then_inc(s_bias, 16)
                    sp.dma_start(rc_b2[:], a["rc_b2"].partition_broadcast(P)).then_inc(s_bias, 16)
                    sp.dma_start(out_bias[0:XE, :], a["e_b2"]).then_inc(s_bias, 16)
                    sp.dma_start(out_bias[XE:XE + 1, :], a["sh_b2"].partition_broadcast(1)).then_inc(s_bias, 16)
                    sp.dma_start(ln_g[:], a["ln_g"].partition_broadcast(P)).then_inc(s_bias, 16)
                    sp.dma_start(ln_b[:], a["ln_b"].partition_broadcast(P)).then_inc(s_bias, 16)
                    sp.dma_start(sh_w1[:], a["sh_w1"].rearrange("j (k p) o -> p j k o", p=P)).then_inc(s_shw, 16)
                    sp.dma_start(sh_w2[:], a["sh_w2"].rearrange("(k p) o -> p k o", p=P)).then_inc(s_shw, 16)

                    def expert(b, e):
                        sp.dma_start(e_w1[b][:], a["e_w1"][bass.ds(e, 1), :, :].rearrange("e (k p) o -> p (e k) o", p=P)).then_inc(s_exp[b], 16)
                        sp.dma_start(e_w2[b][:], a["e_w2"][bass.ds(e, 1), :, :].rearrange("e (k p) o -> p (e k) o", p=P)).then_inc(s_exp[b], 16)
                        sp.dma_start(e_b1[b][:], a["e_b1_cols"][bass.ds(e, 1), :, :].rearrange("e p k -> p (e k)")).then_inc(s_exp[b], 16)

                    for b in range(2):
                        expert(b, b)
                    with sp.Fori(1, XE // 2) as u:
                        for b in range(2):
                            sp.wait_ge(s_dn, u * (2 * NT) + (b * NT))
                            expert(b, u * 2 + b)
                    for t in range(NT):
                        sp.wait_ge(s_out, t + 1)
                        sp.dma_start(out[t * P:t * P + rows(t), :], yn[0:rows(t), t, :]).then_inc(s_st, 16)
                    sp.wait_ge(s_st, 16 * NT)

                @block.gpsimd
                def _(pool):
                    pool.iota(number_i[:], pattern=[[0, NT], [1, XE]], base=0, channel_multiplier=0).then_inc(s_iota, 1)

                @block.tensor
                def _(pe):
                    for t in range(NT):
                        pe.wait_ge(s_yn, t + 1)
                        if t >= 2:
                            pe.wait_ge(s_yt, t - 1)
                        for k in range(KT):
                            ins = pe.transpose(down[t % 2][:, k * P:(k + 1) * P], yn[:, t, k * P:(k + 1) * P], ident[:])
                        ins.then_inc(s_tr, 1)
                    pe.wait_ge(s_yt, NT)
                    pe.wait_ge(s_zero, 2)
                    i = 0
                    for w, taps, tiles, loaded, n_loaded in ((rc_w1, RC_TAPS, KT, s_rcw, 16), (sh_w1, SH_TAPS, HT, s_shw, 32)):
                        pe.wait_ge(loaded, n_loaded)
                        for m in range(tiles):
                            for at, n in SPANS:
                                if i >= 4:
                                    pe.wait_ge(s_act, i - 3)
                                for j in range(taps):
                                    first_col = at + PAD - taps // 2 + j
                                    for k in range(KT):
                                        ins = pe.matmul(up[i % 4][:, 0:n], w[:, j, k, m * P:(m + 1) * P],
                                                        yn_t[:, k, first_col:first_col + n],
                                                        start=(j == 0 and k == 0), stop=(j == taps - 1 and k == KT - 1))
                                ins.then_inc(s_unit, 1)
                                i += 1
                    pe.wait_ge(s_act, KT * 3)
                    pe.wait_ge(s_bias, 128)
                    for t in range(NT):
                        if t >= 2:
                            pe.wait_ge(s_lgc, t - 1)
                        for j in range(RC_TAPS):
                            first_col = t * P + PAD - RC_TAPS // 2 + j
                            for k in range(KT):
                                ins = pe.matmul(down[t % 2][:, 0:XE], rc_act[:, k, first_col:first_col + P], rc_w2[:, j, k, :],
                                                start=(j == 0 and k == 0), stop=(j == RC_TAPS - 1 and k == KT - 1))
                        ins.then_inc(s_lg, 1)

                    def first_layer(b, turn, before):
                        pe.wait_ge(s_exp[b], turn * 48 + 48)
                        for i in range(EU):
                            m, j = i // 3, i % 3
                            at, n = SPANS[j]
                            pe.wait_ge(s_act, before + (i - 3))
                            if isinstance(before, int) and before == CONV:
                                if i >= 4:
                                    pe.wait_ge(s_low, i - 3)
                            else:
                                pe.wait_ge(s_low, before + (i - 3 - CONV))
                            for k in range(KT):
                                ins = pe.matmul(up[(i + 2 * b + CONV) % 4][:, 0:n], e_w1[b][:, k, m * P:(m + 1) * P],
                                                yn_t[:, k, PAD + at:PAD + at + n], start=(k == 0), stop=(k == KT - 1))
                            ins.then_inc(s_unit, 1)

                    def second_layer(b, e, before):
                        pe.wait_ge(s_h, e * EU + EU)
                        for t in range(NT):
                            pe.wait_ge(s_add, before + (t - 3))
                            for k in range(HT):
                                ins = pe.matmul(down[(t + 2 * b + NT) % 4][0:rows(t), :], h_act[b][:, k, t * P:t * P + rows(t)],
                                                e_w2[b][:, k, :], start=(k == 0), stop=(k == HT - 1))
                            ins.then_inc(s_dn, 1)

                    first_layer(0, 0, CONV)
                    pe.wait_ge(s_gate, 1)
                    for t in range(NT):
                        q = t // 4
                        ins = pe.transpose(down[q][0:XE + 1, (t % 4) * P:(t % 4 + 1) * P], gates[:, t, :], ident[:])
                    ins.then_inc(s_gt, 1)
                    pe.wait_ge(s_gtc, 3)
                    pe.wait_ge(s_act, CONV)
                    for t in range(NT):
                        if t >= 4:
                            pe.wait_ge(s_add, t - 3)
                        n = rows(t)
                        for k in range(HT):
                            pe.matmul(down[t % 4][0:n, :], sh_act[:, k, t * P:t * P + n], sh_w2[:, k, :], start=(k == 0), stop=False)
                        pe.matmul(down[t % 4][0:n, :], gates_t[:, t * P:t * P + n], out_bias[:], start=False, stop=True).then_inc(s_dn, 1)
                    with pe.Fori(0, XE // 2 - 1) as u:
                        first_layer(1, u, u * (2 * EU) + (CONV + EU))
                        second_layer(0, u * 2, u * (2 * NT) + NT)
                        first_layer(0, u + 1, u * (2 * EU) + (CONV + 2 * EU))
                        second_layer(1, u * 2 + 1, u * (2 * NT) + 2 * NT)
                    first_layer(1, XE // 2 - 1, CONV + (XE - 1) * EU)
                    second_layer(0, XE - 2, (XE - 2) * NT + NT)
                    second_layer(1, XE - 1, (XE - 1) * NT + NT)

                @block.scalar
                def _(act):
                    act.wait_ge(s_stat, 1)
                    act.activation(std[:], mv[:, :, 1], ACT.Sqrt, bias=eps_ln[:]).then_inc(s_std, 1)
                    act.wait_ge(s_bias, 128)
                    act.wait_ge(s_zero, 2)
                    i = 0
                    for m in range(KT):
                        for at, n in SPANS:
                            act.wait_ge(s_unit, i + 1)
                            act.activation(rc_act[:, m, PAD + at:PAD + at + n], up[i % 4][:, 0:n], ACT.Gelu,
                                           bias=rc_b1[:, m:m + 1]).then_inc(s_act, 1)
                            i += 1
                    for m in range(HT):
                        for at, n in SPANS:
                            act.wait_ge(s_unit, i + 1)
                            act.activation(sh_act[:, m, at:at + n], up[i % 4][:, 0:n], ACT.Silu,
                                           bias=sh_b1[:, m:m + 1]).then_inc(s_act, 1)
                            i += 1

                    def expert(b, e):
                        for i in range(EU + 1):
                            if i < EU:
                                m, (at, n) = i // 3, SPANS[i % 3]
                                if not (isinstance(e, int) and e < 1):
                                    act.wait_ge(s_dn, e * NT)
                                act.wait_ge(s_unit, e * EU + (CONV + i + 1))
                                act.activation(h_act[b][:, m, at:at + n], up[(i + 2 * b + CONV) % 4][:, 0:n], ACT.Relu,
                                               bias=e_b1[b][:, m:m + 1]).then_inc(s_act, 1)
                            if i:
                                n = SPANS[(i - 1) % 3][1]
                                act.wait_ge(s_low, e * EU + i)
                                act.activation(negative[:, (i - 1) % 2, 0:n], negative[:, (i - 1) % 2, 0:n], ACT.Exp).then_inc(s_ex, 1)

                    act.wait_ge(s_gap, 1)
                    act.activation(share[:, 1, :], share[:, 0, :], ACT.Exp).then_inc(s_gx, 1)
                    expert(0, 0)
                    expert(1, 1)
                    with act.Fori(1, XE // 2) as u:
                        for b in range(2):
                            expert(b, u * 2 + b)
                    act.wait_ge(s_var, 1)
                    act.activation(std[:], mv[:, :, 1], ACT.Sqrt, bias=eps_ln[:]).then_inc(s_dev, 1)

                @block.vector
                def _(dve):
                    step = Steps(dve, s_d)
                    dve.memset(yn_t[:], 0.0).then_inc(s_zero, 1)
                    dve.memset(rc_act[:], 0.0).then_inc(s_zero, 1)
                    for t in range(NT):
                        step(dve.bn_stats(stats[:], x1[:, t, :]))
                        ins = dve.bn_aggr(mv[:, t, :], stats[:])
                        if t == NT - 1:
                            ins.then_inc(s_stat, 1)
                        else:
                            step(ins)
                    dve.wait_ge(s_std, 1)
                    step(dve.reciprocal(rstd[:], std[:]))
                    dve.wait_ge(s_zero, 2)

                    def to_columns(t):
                        n = rows(t)
                        dve.wait_ge(s_tr, t + 1)
                        dve.tensor_copy(yn_t[:, :, PAD + t * P:PAD + t * P + n],
                                        down[t % 2][:].rearrange("p (k n) -> p k n", k=KT)[:, :, 0:n]).then_inc(s_yt, 1)

                    for t in range(NT):
                        dve.tensor_scalar(yn[:, t, :], x1[:, t, :], mv[:, t, 0:1], rstd[:, t:t + 1],
                                          ALU.subtract, ALU.mult).then_inc(s_yn, 1)
                        if t >= 1:
                            to_columns(t - 1)
                    to_columns(NT - 1)
                    dve.wait_ge(s_bias, 128)
                    for t in range(NT):
                        step(dve.tensor_tensor(x1[:, t, :], x1[:, t, :], ln_b[:], ALU.add))
                    dve.wait_ge(s_iota, 1)
                    step(dve.tensor_copy(number[:], number_i[:]))
                    for t in range(NT):
                        dve.wait_ge(s_lg, t + 1)
                        dve.tensor_tensor(logits[:, t, :], down[t % 2][:, 0:XE], rc_b2[:], ALU.add).then_inc(s_lgc, 1)
                    dve.wait_ge(s_lgc, NT)

                    def spread(v):
                        return v.unsqueeze(2).broadcast_to([P, NT, XE])

                    for r, hot in enumerate((first, second)):
                        step(dve.tensor_reduce(top[:, r, :], logits[:], AX.X, ALU.max))
                        step(dve.tensor_tensor(place[:], logits[:], spread(top[:, r, :]), ALU.not_equal))
                        step(dve.scalar_tensor_tensor(out=place[:], in0=place[:], scalar=float(XE), in1=number[:],
                                                      op0=ALU.mult, op1=ALU.add))
                        step(dve.tensor_reduce(which[:], place[:], AX.X, ALU.min))
                        step(dve.tensor_tensor(hot[:], number[:], spread(which[:]), ALU.is_equal))
                        if r == 0:
                            step(dve.scalar_tensor_tensor(out=logits[:], in0=hot[:], scalar=NEG, in1=logits[:],
                                                          op0=ALU.mult, op1=ALU.add))
                    dve.tensor_tensor(share[:, 0, :], top[:, 1, :], top[:, 0, :], ALU.subtract).then_inc(s_gap, 1)
                    dve.wait_ge(s_gx, 1)
                    step(dve.tensor_scalar(share[:, 0, :], share[:, 1, :], 1.0, None, ALU.add))
                    step(dve.reciprocal(share[:, 0, :], share[:, 0, :]))
                    step(dve.tensor_tensor(share[:, 1, :], share[:, 1, :], share[:, 0, :], ALU.mult))
                    step(dve.tensor_tensor(first[:], first[:], spread(share[:, 0, :]), ALU.mult))
                    step(dve.tensor_tensor(second[:], second[:], spread(share[:, 1, :]), ALU.mult))
                    step(dve.memset(gates[:, :, XE:XE + 1], 1.0))
                    dve.tensor_tensor(gates[:, :, 0:XE], first[:], second[:], ALU.add).then_inc(s_gate, 1)
                    def minimum(b, e, i):
                        m, n = i // 3, SPANS[i % 3][1]
                        if isinstance(e, int) and e == 0:
                            if i >= 2:
                                dve.wait_ge(s_h, i - 1)
                        else:
                            dve.wait_ge(s_h, e * EU + (i - 1))
                        dve.wait_ge(s_act, e * EU + (CONV + i + 1))
                        dve.tensor_scalar(negative[:, i % 2, 0:n], up[(i + 2 * b + CONV) % 4][:, 0:n], e_b1[b][:, m:m + 1], 0.0,
                                          ALU.add, ALU.min).then_inc(s_low, 1)

                    def join(b, e, i):
                        m, (at, n) = i // 3, SPANS[i % 3]
                        dve.wait_ge(s_ex, e * EU + (i + 1))
                        dve.scalar_tensor_tensor(out=h_act[b][:, m, at:at + n], in0=negative[:, i % 2, 0:n], scalar=-1.0,
                                                 in1=h_act[b][:, m, at:at + n], op0=ALU.add, op1=ALU.add).then_inc(s_h, 1)

                    def hidden(b, e):
                        for i in range(EU + 1):
                            if i < EU:
                                minimum(b, e, i)
                            if i:
                                join(b, e, i - 1)

                    def add(b, e):
                        for t in range(NT):
                            n = rows(t)
                            dve.wait_ge(s_dn, e * NT + (NT + t + 1))
                            dve.wait_ge(s_add, e * NT + (t + 1))
                            dve.scalar_tensor_tensor(out=yn[0:n, t, :], in0=down[(t + 2 * b + NT) % 4][0:n, :],
                                                     scalar=gates[0:n, t, bass.ds(e, 1)], in1=yn[0:n, t, :],
                                                     op0=ALU.mult, op1=ALU.add).then_inc(s_add, 1)

                    hidden(0, 0)
                    dve.wait_ge(s_gt, 1)
                    for q in range(3):
                        n = SPANS[q][1]
                        dve.tensor_copy(gates_t[:, q * 512:q * 512 + n], down[q][0:XE + 1, 0:n]).then_inc(s_gtc, 1)
                    for t in range(NT):
                        n = rows(t)
                        dve.wait_ge(s_dn, t + 1)
                        dve.tensor_tensor(yn[0:n, t, :], yn[0:n, t, :], down[t % 4][0:n, :], ALU.add).then_inc(s_add, 1)
                    hidden(1, 1)
                    add(0, 0)
                    with dve.Fori(1, XE // 2) as u:
                        hidden(0, u * 2)
                        add(1, u * 2 - 1)
                        hidden(1, u * 2 + 1)
                        add(0, u * 2)
                    add(1, XE - 1)
                    dve.wait_ge(s_add, (XE + 1) * NT)
                    for t in range(NT):
                        step(dve.bn_stats(stats[:], yn[:, t, :]))
                        ins = dve.bn_aggr(mv[:, t, :], stats[:])
                        if t == NT - 1:
                            ins.then_inc(s_var, 1)
                        else:
                            step(ins)
                    dve.wait_ge(s_dev, 1)
                    step(dve.reciprocal(rstd[:], std[:]))
                    for t in range(NT):
                        step(dve.tensor_scalar(yn[:, t, :], yn[:, t, :], mv[:, t, 0:1], rstd[:, t:t + 1], ALU.subtract, ALU.mult))
                        step(dve.tensor_tensor(yn[:, t, :], yn[:, t, :], ln_g[:], ALU.mult))
                        dve.tensor_tensor(yn[:, t, :], yn[:, t, :], x1[:, t, :], ALU.add).then_inc(s_out, 1)


def lay_out(v):
    import numpy as np
    c = np.ascontiguousarray
    n_pad = EC * P - E
    loops = np.arange(NP, dtype=np.int32)
    tail = np.full(P, NP - 1, np.int32)
    src = np.concatenate([v["src"], np.full(n_pad, NP - 1, np.int32), loops, tail])
    dst = np.concatenate([v["dst"], np.full(n_pad, NP - 1, np.int32), loops, tail])
    attr = np.concatenate([v["edge_attr_4"], np.zeros((n_pad, 4), np.float32)])
    return {
        "x": v["x"],
        "edges": c(np.stack([src.reshape(CH, P).T, dst.reshape(CH, P).T], axis=2)), "dst_row": dst,
        "edge_attr": c(attr.reshape(EC, P, 4).transpose(1, 0, 2)),
        "gat_w": v["L0_gnn_W"], "gat_w_edge": v["L0_gnn_W_edge"], "att_src": v["L0_gnn_att_src"],
        "att_dst": v["L0_gnn_att_dst"], "att_edge": v["L0_gnn_att_edge"], "gat_bias": v["L0_gnn_bias"],
        "gamma": v["L0_gnn_gamma"], "beta": v["L0_gnn_beta"],
        "wq_t": c(v["L0_mix_Wq"].T), "wk_t": c(v["L0_mix_Wk"].T), "wv_t": c(v["L0_mix_Wv"].T), "wo_t": c(v["L0_mix_Wo"].T),
        "bq": v["L0_mix_bq"], "bk": v["L0_mix_bk"], "bv": v["L0_mix_bv"], "bo": v["L0_mix_bo"],
        "rc_w1": c(v["L0_ffn_rc_w1"].transpose(2, 1, 0)), "rc_b1": v["L0_ffn_rc_b1"],
        "rc_w2": c(v["L0_ffn_rc_w2"].transpose(2, 1, 0)), "rc_b2": v["L0_ffn_rc_b2"],
        "sh_w1": c(v["L0_ffn_sh_w1"].transpose(2, 1, 0)), "sh_b1": v["L0_ffn_sh_b1"],
        "sh_w2": c(v["L0_ffn_sh_w2"][:, :, 0].T), "sh_b2": v["L0_ffn_sh_b2"],
        "e_w1": v["L0_ffn_e_w1"], "e_b1_cols": c(v["L0_ffn_e_b1"].reshape(XE, HT, P).transpose(0, 2, 1)), "e_w2": v["L0_ffn_e_w2"], "e_b2": v["L0_ffn_e_b2"],
        "ln_g": v["L0_ffn_ln_g"], "ln_b": v["L0_ffn_ln_b"],
    }


def kernel(**inputs):
    import numpy as np
    import concourse.bacc as bacc
    from concourse.bass_utils import run_bass_kernel_spmd

    nc = bacc.Bacc("TRN2", target_bir_lowering=False, num_devices=1)
    laid = lay_out({name: np.asarray(v) for name, v in inputs.items()})
    arrays = {f"in_{name}": np.ascontiguousarray(v) for name, v in laid.items()}
    ins = {name: nc.dram_tensor(f"in_{name}", v.shape, mybir.dt.from_np(v.dtype), kind="ExternalInput").ap()
           for name, v in laid.items()}
    out = nc.dram_tensor("out_0_dram", (N, D), F32, kind="ExternalOutput").ap()
    layer(nc, ins, out)
    result = run_bass_kernel_spmd(nc, [arrays], core_ids=[0])
    return result.results[0]["out_0_dram"]
```

```python
from contextlib import ExitStack

import concourse.bass as bass
from concourse import mybir

F32 = mybir.dt.float32
F32R = mybir.dt.float32r
I32 = mybir.dt.int32
ALU = mybir.AluOpType
ACT = mybir.ActivationFunctionType
AX = mybir.AxisListType

P = 128
N = 1250
D = 512
KT = D // P
NT = -(-N // P)
NP = NT * P
LAST = N - (NT - 1) * P
SPANS = [(0, 512), (512, 512), (1024, N - 1024)]
FULL_SPANS = [(0, 512), (512, 512), (1024, NP - 1024)]

E = 20000
EC = -(-E // P)
CH = EC + NT + 1
GH, GC = 4, 128
SLOPE = 0.2
BN_EPS = LN_EPS = 1e-5
MH, MD = 8, 64
MIX_EPS = 1e-6
XE, HID = 10, 256
HT = HID // P
RC_TAPS, SH_TAPS = 3, 9
PAD = SH_TAPS // 2
PASS_HEADS = [2, MH - 2]
EARLY_PARTS = [60, 24]
EARLY = sum(EARLY_PARTS)
PAIRS = [2 * (CH - EARLY) // PASS_HEADS[0], 2 * CH // PASS_HEADS[1]]
GS = 14
SS = 4
TURN = 28
assert CH % TURN == EARLY % TURN == PAIRS[0] % TURN == PAIRS[1] % TURN == TURN % GS == TURN % SS == 0
NEG = -3.0e38
SKIP = 1.0e6


class Steps:

    def __init__(self, eng, sem):
        self.eng, self.sem, self.done = eng, sem, 0

    def __call__(self, ins):
        self.done = self.done + 1
        ins.then_inc(self.sem, 1)
        self.eng.wait_ge(self.sem, self.done)


def rows(t):
    return P if t < NT - 1 else LAST


def layer(nc, a, out):
    ctx = ExitStack()

    def dram(name, shape, dt=F32):
        return nc.dram_tensor(name, shape, dt).ap()

    feature_table = dram("feature_table", [NP, D])
    source_table = dram("source_table", [NP, GH])
    target_table = dram("target_table", [NP, 2 * GH])
    max_table = dram("max_table", [NP * CH, GH])
    sums_table = [dram(f"sums_table{k}", [NP, D + GH]) for k in range(SS)]

    with ctx:
        def keep(name, shape, dt=F32):
            return ctx.enter_context(nc.sbuf_tensor(name, shape, dt))

        ident = keep("ident", [P, P])
        ones = keep("ones", [P, P])
        x1 = keep("x1", [P, NT, D])
        a_dst = keep("a_dst", [P, NT, GH])
        eps_ln = keep("eps_ln", [P, 1])
        mv_x1 = keep("mv_x1", [P, NT, 2])
        gat = ExitStack()
        ctx.enter_context(gat)

        def gkeep(name, shape, dt=F32):
            return gat.enter_context(nc.sbuf_tensor(name, shape, dt))

        idx_i = gkeep("idx_i", [P, CH, 2], I32)
        dst_f = gkeep("dst_f", [P, CH])
        logit = gkeep("logit", [P, CH, GH])
        row_idx = gkeep("row_idx", [P, CH], I32)
        key = gkeep("key", [P, CH])
        before = gkeep("before", [P, P])

        mix = ExitStack()
        ctx.enter_context(mix)

        def mkeep(name, shape, dt=F32):
            return mix.enter_context(nc.sbuf_tensor(name, shape, dt))

        q_t = mkeep("q_t", [P, KT, NP])
        k_t = mkeep("k_t", [P, KT, NP])
        v_tok = mkeep("v_tok", [P, NT, D])
        xn_t = mkeep("xn_t", [P, KT, NP])
        pair_ones = mkeep("pair_ones", [P, P])
        att_out = mkeep("att_out", [P, KT, NP])

        def in_place_of(tensor, i):
            return tensor[:].rearrange("p k n -> p (k n)")[:, i * KT * D:(i + 1) * KT * D].rearrange("p (k o) -> p k o", k=KT)

        w_v = in_place_of(q_t, 0)
        w_k, w_q = in_place_of(att_out, 0), in_place_of(att_out, 1)
        b_q = mkeep("b_q", [P, KT])
        b_k = mkeep("b_k", [P, KT])
        with ExitStack() as s:
            def sb(name, shape, dt=F32):
                return s.enter_context(nc.sbuf_tensor(name, shape, dt))

            semaphores = []

            def sem(name):
                semaphores.append(nc.alloc_semaphore(name))
                return semaphores[-1]

            w_gat = sb("w_gat", [P, KT, D])
            w_att = sb("w_att", [P, KT, 2 * GH])
            att = sb("att", [P, 2, D])
            xn = sb("xn", [P, 2, D])
            junk = sb("junk", [P, GC])
            stats = sb("stats", [P, NT, 6])
            mv = sb("mv", [P, NT, 2])
            std = sb("std", [P, NT])
            rstd = sb("rstd", [P, NT])
            row = sb("row", [P, 4, D + GH])
            attr = sb("attr", [P, EC, 4])
            w_edge = sb("w_edge", [P, 4, D])
            att_edge = sb("att_edge", [P, D])
            v_edge = sb("v_edge", [P, 4, GH])
            mean = sb("mean", [P, 4])
            chunk_i = sb("chunk_i", [P, CH], I32)
            LOW = 2240
            LOW_PARTS = NP * CH * GH // P // LOW
            low = sb("low", [P, LOW])
            ZERO_PARTS = 4
            zeros = sb("zeros", [P, NT * (D + GH) // ZERO_PARTS])
            ps = [s.enter_context(nc.psum_tensor(f"ps{b}", [P, 512], F32)) for b in range(8)]
            s_in = sem("edges_loaded")
            s_low = sem("low_ready")
            s_init = sem("tables_initialised")
            s_part = sem("attribute_sums_ready")
            s_mean = sem("attribute_mean_ready")
            s_x = [sem(f"x_part_{i}_loaded") for i in range(4)]
            s_const = sem("constants_ready")
            s_zero = sem("x_padded")
            s_w = sem("weights_loaded")
            s_wq = sem("projection_weights_loaded")
            s_bn = sem("tile_stats_ready")
            s_stat = sem("variance_ready")
            s_std = sem("deviation_ready")
            s_xn = sem("xn_ready")
            s_tr = sem("xn_transposed")
            s_xt = sem("xn_t_ready")
            s_h = sem("h_ready")
            s_row_h = sem("h_row_features_ready")
            s_row_a = sem("h_row_logits_ready")
            s_tab = [sem(f"h_row_{b}_stored") for b in range(4)]
            s_d = sem("dve_steps")
            s_p = sem("pool_steps")

            with nc.Block() as block:
                @block.sync
                def _(sp):
                    for t in range(0, NT - 1, 3):
                        sp.dma_start(x1[:, t:t + 3, :], a["x"][t * P:(t + 3) * P, :].rearrange("(t p) d -> p t d", p=P)).then_inc(s_x[t // 3], 16)
                    sp.wait_ge(s_zero, 1)
                    sp.dma_start(x1[0:LAST, NT - 1, :], a["x"][(NT - 1) * P:N, :]).then_inc(s_x[3], 16)
                    sp.dma_start(w_gat[:], a["gat_w"].rearrange("(k p) o -> p k o", p=P)).then_inc(s_w, 16)
                    sp.dma_start(att[:, 0, :], a["att_src"].rearrange("h c -> (h c)").partition_broadcast(P)).then_inc(s_w, 16)
                    sp.dma_start(att[:, 1, :], a["att_dst"].rearrange("h c -> (h c)").partition_broadcast(P)).then_inc(s_w, 16)
                    for dst, name in ((w_v, "wv_t"), (w_k, "wk_t"), (w_q, "wq_t")):
                        sp.dma_start(dst, a[name].rearrange("(k p) o -> p k o", p=P)).then_inc(s_wq, 16)
                    with nc.allow_non_contiguous_dma(reason="biases of 512 numbers, one for a partition"):
                        sp.dma_start(b_k[:], a["bk"].rearrange("(k p) -> p k", p=P)).then_inc(s_wq, 16)
                        sp.dma_start(b_q[:], a["bq"].rearrange("(k p) -> p k", p=P)).then_inc(s_wq, 16)
                    sp.dma_start(idx_i[:], a["edges"]).then_inc(s_in, 16)
                    sp.dma_start(attr[:], a["edge_attr"]).then_inc(s_in, 16)
                    sp.dma_start(w_edge[:], a["gat_w_edge"].rearrange("k c -> (k c)").partition_broadcast(P)
                                 .rearrange("p (k c) -> p k c", k=4)).then_inc(s_in, 16)
                    sp.dma_start(att_edge[:], a["att_edge"].rearrange("h c -> (h c)").partition_broadcast(P)).then_inc(s_in, 16)
                    sp.wait_ge(s_low, 1)
                    table = max_table.rearrange("(p r w) h -> p r (w h)", p=P, r=LOW_PARTS)
                    for r in range(LOW_PARTS):
                        sp.dma_start(table[:, r, :], low[:]).then_inc(s_init, 16)
                    sp.wait_ge(s_low, 2)
                    for table in sums_table:
                        view = table.rearrange("(p t) j -> p (t j)", p=P).rearrange("p (r w) -> p r w", r=ZERO_PARTS)
                        for r in range(ZERO_PARTS):
                            sp.dma_start(view[:, r, :], zeros[:]).then_inc(s_init, 16)
                    for t in range(NT):
                        sp.wait_ge(s_row_h, t + 1)
                        sp.dma_start(feature_table[t * P:(t + 1) * P, :], row[:, t % 4, 0:D]).then_inc(s_tab[t % 4], 16)
                        sp.wait_ge(s_row_a, t + 1)
                        sp.dma_start(source_table[t * P:(t + 1) * P, :], row[:, t % 4, D:D + GH]).then_inc(s_tab[t % 4], 16)
                    for b in range(4):
                        sp.wait_ge(s_tab[b], 32 * len(range(b, NT, 4)))
                    sp.wait_ge(s_init, 16 * (LOW_PARTS + SS * ZERO_PARTS))
                    sp.wait_ge(s_wq, 16 * 5)

                @block.gpsimd
                def _(pool):
                    step = Steps(pool, s_p)
                    pool.memset(x1[:, NT - 1, :], 0.0).then_inc(s_zero, 1)
                    pool.memset(eps_ln[:], LN_EPS).then_inc(s_const, 1)
                    pool.memset(low[:], NEG).then_inc(s_low, 1)
                    pool.memset(zeros[:], 0.0).then_inc(s_low, 1)
                    step(pool.memset(ones[:], 1.0))
                    step(pool.memset(ident[:], 0.0))
                    step(pool.memset(pair_ones[:], 0.0))
                    step(pool.memset(pair_ones[0:MD, 0:MD], 1.0))
                    step(pool.memset(pair_ones[MD:P, MD:P], 1.0))
                    pool.affine_select(out=ident[:], in_=ident[:], compare_op=ALU.not_equal, fill=1.0, base=0,
                                       pattern=[[-1, P]], channel_multiplier=1).then_inc(s_const, 1)
                    pool.iota(chunk_i[:], pattern=[[1, CH]], base=0, channel_multiplier=0).then_inc(s_const, 1)
                    step(pool.memset(before[:], 1.0))
                    pool.affine_select(out=before[:], in_=before[:], compare_op=ALU.is_ge, fill=0.0, base=-1,
                                       pattern=[[-1, P]], channel_multiplier=1).then_inc(s_const, 1)

                @block.vector
                def _(dve):
                    step = Steps(dve, s_d)
                    for t in range(NT + 1):
                        if t < NT:
                            if t % 3 == 0:
                                dve.wait_ge(s_x[t // 3], 16)
                            dve.bn_stats(stats[:, t, :], x1[:, t, :]).then_inc(s_bn, 1)
                        if t:
                            dve.wait_ge(s_bn, t)
                            ins = dve.bn_aggr(mv[:, t - 1, :], stats[:, t - 1, :])
                    ins.then_inc(s_stat, 1)
                    dve.wait_ge(s_w, 48)
                    for k in range(KT):
                        for j in range(2):
                            for h in range(GH):
                                cols = slice(h * GC, (h + 1) * GC)
                                step(dve.tensor_tensor_reduce(out=junk[:], in0=w_gat[:, k, cols], in1=att[:, j, cols],
                                                              scale=1.0, scalar=0.0, op0=ALU.mult, op1=ALU.add,
                                                              accum_out=w_att[:, k, j * GH + h:j * GH + h + 1]))
                    dve.wait_ge(s_std, 1)
                    step(dve.reciprocal(rstd[:], std[:]))
                    for t in range(NT):
                        if t >= 2:
                            dve.wait_ge(s_tr, t - 1)
                        dve.tensor_scalar(xn[:, t % 2, :], x1[:, t, :], mv[:, t, 0:1], rstd[:, t:t + 1],
                                          ALU.subtract, ALU.mult).then_inc(s_xn, 1)
                        if t >= 1:
                            dve.wait_ge(s_tr, t)
                            dve.tensor_copy(xn_t[:, :, (t - 1) * P:t * P],
                                            ps[(t - 1) % 2][:].rearrange("p (k n) -> p k n", k=KT)).then_inc(s_xt, 1)
                    dve.wait_ge(s_tr, NT)
                    dve.tensor_copy(xn_t[:, :, (NT - 1) * P:NT * P],
                                    ps[(NT - 1) % 2][:].rearrange("p (k n) -> p k n", k=KT)).then_inc(s_xt, 1)
                    dve.wait_ge(s_in, 64)
                    step(dve.tensor_tensor(w_edge[:], w_edge[:], att_edge[:].unsqueeze(1).broadcast_to([P, 4, D]), ALU.mult))
                    step(dve.tensor_reduce(v_edge[:], w_edge[:].rearrange("p k (h c) -> p k h c", c=GC), AX.X, ALU.add))
                    dve.tensor_reduce(mean[:], attr[:].rearrange("p c k -> p k c"), AX.X, ALU.add).then_inc(s_part, 1)
                    dve.wait_ge(s_mean, 1)
                    step(dve.tensor_scalar(mean[:], ps[6][:, 0:4], 1.0 / E, None, ALU.mult))
                    for h in range(GH):
                        for k in range(4):
                            real, loops = logit[:, 0:EC, h], logit[:, EC:CH, h]
                            again = mean[:, k:k + 1].broadcast_to([P, CH - EC])
                            if k == 0:
                                dve.tensor_scalar(real, attr[:, :, k], v_edge[:, k, h:h + 1], None, ALU.mult)
                                step(dve.tensor_scalar(loops, again, v_edge[:, k, h:h + 1], None, ALU.mult))
                            else:
                                dve.scalar_tensor_tensor(out=real, in0=attr[:, :, k], scalar=v_edge[:, k, h:h + 1],
                                                         in1=real, op0=ALU.mult, op1=ALU.add)
                                step(dve.scalar_tensor_tensor(out=loops, in0=again, scalar=v_edge[:, k, h:h + 1],
                                                              in1=loops, op0=ALU.mult, op1=ALU.add))
                    step(dve.tensor_copy(dst_f[:], idx_i[:, :, 1]))
                    dve.wait_ge(s_const, 4)
                    step(dve.scalar_tensor_tensor(out=key[:], in0=dst_f[:], scalar=float(CH), in1=chunk_i[:],
                                                  op0=ALU.mult, op1=ALU.add))

                @block.scalar
                def _(act):
                    act.wait_ge(s_stat, 1)
                    act.wait_ge(s_const, 2)
                    act.activation(std[:], mv[:, :, 1], ACT.Sqrt, bias=eps_ln[:]).then_inc(s_std, 1)
                    for t in range(NT):
                        act.wait_ge(s_h, t + 1)
                        if t >= 4:
                            act.wait_ge(s_tab[t % 4], 32 * (t // 4))
                        act.copy(row[:, t % 4, 0:D], ps[2 + t % 2][:]).then_inc(s_row_h, 1)
                        act.copy(a_dst[:, t, :], ps[4 + t % 2][:, GH:2 * GH])
                        act.copy(row[:, t % 4, D:D + GH], ps[4 + t % 2][:, 0:GH]).then_inc(s_row_a, 1)

                @block.tensor
                def _(pe):
                    pe.wait_ge(s_const, 2)
                    for t in range(NT):
                        pe.wait_ge(s_xn, t + 1)
                        if t >= 2:
                            pe.wait_ge(s_xt, t - 1)
                        for k in range(KT):
                            ins = pe.transpose(ps[t % 2][:, k * P:(k + 1) * P], xn[:, t % 2, k * P:(k + 1) * P], ident[:])
                        ins.then_inc(s_tr, 1)
                    pe.wait_ge(s_xt, NT)
                    pe.wait_ge(s_d, 2 * GH * KT)
                    for t in range(NT):
                        if t >= 2:
                            pe.wait_ge(s_row_h, t - 1)
                            pe.wait_ge(s_row_a, t - 1)
                        for k in range(KT):
                            pe.matmul(ps[2 + t % 2][:], xn_t[:, k, t * P:(t + 1) * P], w_gat[:, k, :],
                                      start=(k == 0), stop=(k == KT - 1))
                        for k in range(KT):
                            ins = pe.matmul(ps[4 + t % 2][:, 0:2 * GH], xn_t[:, k, t * P:(t + 1) * P], w_att[:, k, :],
                                            start=(k == 0), stop=(k == KT - 1))
                        ins.then_inc(s_h, 1)
                        if t == NT // 2:
                            pe.wait_ge(s_part, 1)
                            pe.matmul(ps[6][:, 0:4], ones[:], mean[:], start=True, stop=True).then_inc(s_mean, 1)
            nc.clear_and_free_semaphores(semaphores)
            nc.all_engine_barrier()


        UNITS = [(j, m) for j in range(3) for m in range(NT)]
        NU = len(UNITS)
        TILES = [(t, j) for t in range(NT) for j in range(3)]
        q_now = [mkeep(f"q_now{b}", [MD + 1, NP]) for b in range(2)]
        k_now = [mkeep(f"k_now{b}", [MD + 1, N]) for b in range(2)]
        v_now = [mkeep(f"v_now{b}", [P, NT, 2 * MD]) for b in range(2)]

        class Attention:

            def __init__(self, s, phase, stage_sem):
                def sb(name, shape, dt=F32):
                    return s.enter_context(nc.sbuf_tensor(f"{name}_{phase}", shape, dt))

                def psum(name):
                    return s.enter_context(nc.psum_tensor(f"{name}_{phase}", [P, 512], F32))

                def sem(name):
                    return stage_sem(f"{name}_{phase}")

                self.phase = phase
                self.pre = 1 - phase
                self.q_round = sb("q_round", [MD, NP], F32R)
                self.k_round = sb("k_round", [MD, N], F32R)
                self.prob = sb("prob", [P, 3, 512])
                self.part_max = sb("part_max", [P, NT, 3])
                self.neg_max = sb("neg_max", [P, NT])
                self.raw = sb("raw", [P, 2, 512])
                self.inv = sb("inv", [MD, 2, 512])
                self.nm_banks = 2 - phase
                self.logits_nm = [psum(f"logits_nm{b}") for b in range(self.nm_banks)]
                self.logits_mn = [psum(f"logits_mn{b}") for b in range(2)]
                self.summed = psum("summed")
                self.pair_chunks = PAIRS[phase]
                self.heads = PASS_HEADS[phase]
                self.first_pair = PASS_HEADS[0] // 2 * phase
                self.first_chunk = EARLY if phase == 0 else 0
                self.s_one = sem("constant_columns_ready")
                self.s_stage = [sem(f"head_{b}_staged") for b in range(2)]
                self.s_round = sem("qk_rounded")
                self.s_nm = sem("logits_nm_ready")
                self.s_max = sem("part_max_ready")
                self.s_neg = sem("neg_max_ready")
                self.s_row = sem("max_row_ready")
                self.s_rowc = sem("max_row_copied")
                self.s_mn = sem("logits_mn_ready")
                self.s_pr = sem("prob_ready")
                self.s_pv = sem("prob_used")
                self.s_raw = sem("sums_copied")
                self.s_inv = sem("inverse_ready")
                self.s_att = sem("span_done")

            def stage(self, sp, b, pair):
                lo = b * MD
                sp.dma_start(q_now[b][0:MD, :], q_t[lo:lo + MD, pair, :]).then_inc(self.s_stage[b], 16)
                sp.dma_start(k_now[b][0:MD, :], k_t[lo:lo + MD, pair, 0:N]).then_inc(self.s_stage[b], 16)
                sp.dma_start(v_now[b][:, :, 0:MD], v_tok[:, :, (pair * 2 + b) * MD:(pair * 2 + b + 1) * MD]).then_inc(self.s_stage[b], 16)

            def stage_next(self, sp, h):
                sp.wait_ge(self.s_raw, 3 * h + 3)
                if self.phase == 0 or h < self.heads - 2:
                    self.stage(sp, h % 2, self.first_pair + h // 2 + 1)
                elif h == self.heads - 2:
                    self.stage(sp, 0, MH // 2 - 1)

            def tile_logits(self, pe, made, i):
                t, j = TILES[i]
                at, n = SPANS[j]
                if i == 0:
                    pe.wait_ge(self.s_round, made * 2 + 2)
                    pe.wait_ge(self.s_rowc, made * 3)
                    pe.wait_ge(self.s_max, made * NU)
                elif i >= self.nm_banks:
                    pe.wait_ge(self.s_max, made * NU + (i - self.nm_banks + 1))
                pe.matmul(self.logits_nm[i % self.nm_banks][:, 0:n], self.q_round[:, t * P:(t + 1) * P], self.k_round[:, at:at + n],
                          start=True, stop=True).then_inc(self.s_nm, 1)

            def max_row(self, pe, made, j):
                at, n = FULL_SPANS[j]
                pe.wait_ge(self.s_neg, made + 1)
                if j:
                    pe.wait_ge(self.s_rowc, made * 3 + j)
                for t in range(at // P, (at + n) // P):
                    ins = pe.matmul(self.logits_nm[0][0:1, t * P - at:(t + 1) * P - at], self.neg_max[:, t:t + 1], ident[:],
                                    start=True, stop=True)
                ins.then_inc(self.s_row, 1)

            def score(self, pe, h, b, u):
                j, m = UNITS[u]
                at, n = FULL_SPANS[j]
                if u > 1:
                    pe.wait_ge(self.s_pr, h * NU + (u - 1))
                pe.matmul(self.logits_mn[u % 2][0:rows(m), 0:n], k_now[b][:, m * P:m * P + rows(m)], q_now[b][:, at:at + n],
                          start=True, stop=True).then_inc(self.s_mn, 1)

            def product(self, pe, h, b, u):
                j, m = UNITS[u]
                n = FULL_SPANS[j][1]
                pe.wait_ge(self.s_pr, h * NU + (u + 1))
                if m == 0:
                    pe.wait_ge(self.s_raw, h * 3 + j)
                pe.matmul(self.summed[:, 0:n], v_now[b][0:rows(m), m, :], self.prob[0:rows(m), u % 3, 0:n],
                          start=(m == 0), stop=(m == NT - 1)).then_inc(self.s_pv, 1)

            def pe_first(self, pe, i):
                if i == 0:
                    pe.wait_ge(self.s_one, 4)
                    pe.wait_ge(self.s_stage[0], 48)
                self.tile_logits(pe, 0, i)
                if i == NU - 1:
                    for j in range(3):
                        self.max_row(pe, 0, j)

            def pe_unit(self, pe, p, b, u):
                h = p * 2 + b
                made = h + self.pre
                if u == 0:
                    pe.wait_ge(self.s_rowc, made * 3)
                    if b == 1 or self.phase == 0:
                        pe.wait_ge(self.s_stage[b], (p + self.pre) * 48)
                    self.score(pe, h, b, 0)
                if u + 1 < NU:
                    self.score(pe, h, b, u + 1)
                if u:
                    self.product(pe, h, b, u - 1)
                if u == NU - 1:
                    self.product(pe, h, b, u)
                for i in NEXT_AFTER[u]:
                    self.tile_logits(pe, made, i)
                if u == NU - 1:
                    for j in range(3):
                        self.max_row(pe, made, j)

            def round_next(self, dve, b, staged, made):
                dve.wait_ge(self.s_stage[b], staged)
                dve.wait_ge(self.s_nm, made * NU)
                dve.tensor_copy(self.q_round[:], q_now[b][0:MD, :]).then_inc(self.s_round, 1)
                dve.tensor_copy(self.k_round[:], k_now[b][0:MD, :]).then_inc(self.s_round, 1)

            def maximum(self, dve, made, i):
                t, j = TILES[i]
                n = SPANS[j][1]
                dve.wait_ge(self.s_nm, made * NU + (i + 1))
                dve.tensor_reduce(self.part_max[:, t, j:j + 1], self.logits_nm[i % self.nm_banks][:, 0:n], AX.X, ALU.max,
                                  negate=True).then_inc(self.s_max, 1)

            def join_maxima(self, dve, made):
                dve.wait_ge(self.s_max, made * NU + NU)
                dve.tensor_reduce(self.neg_max[:], self.part_max[:], AX.X, ALU.min).then_inc(self.s_neg, 1)

            def finish(self, dve, h, b, j, pair):
                at, n = FULL_SPANS[j]
                r = (b + j) % 2
                dve.wait_ge(self.s_raw, h * 3 + (j + 1))
                dve.reciprocal(self.inv[:, r, 0:n], self.raw[MD:P, r, 0:n]).then_inc(self.s_inv, 1)
                dve.wait_ge(self.s_inv, h * 3 + (j + 1))
                dve.tensor_tensor(att_out[b * MD:(b + 1) * MD, bass.ds(pair, 1), at:at + n], self.raw[0:MD, r, 0:n],
                                  self.inv[:, r, 0:n], ALU.mult).then_inc(self.s_att, 1)

            def constant_columns(self, dve):
                for b in range(2):
                    dve.memset(k_now[b][MD:MD + 1, :], 1.0).then_inc(self.s_one, 1)
                    dve.memset(v_now[b][:, :, MD:2 * MD], 1.0).then_inc(self.s_one, 1)

            def dve_first(self, dve, i):
                if i == 0:
                    self.round_next(dve, 0, 48, 0)
                self.maximum(dve, 0, i)
                if i == NU - 1:
                    self.join_maxima(dve, 0)

            def dve_unit(self, dve, p, b, u):
                h = p * 2 + b
                made = h + self.pre
                if u == ROUND_AT:
                    self.round_next(dve, 1 - b, (p + (self.pre if b == 0 else self.pre + 1)) * 48, made)
                for i in NEXT_AFTER[u]:
                    self.maximum(dve, made, i)
                if u == NU - 1:
                    self.join_maxima(dve, made)
                for j in range(3):
                    if u == min(NT * (j + 1) + 4, NU - 1):
                        self.finish(dve, h, b, j, p + self.first_pair)

            def row(self, act, made, b, j):
                at, n = FULL_SPANS[j]
                act.wait_ge(self.s_row, made * 3 + (j + 1))
                act.copy(q_now[b][MD:MD + 1, at:at + n], self.logits_nm[0][0:1, 0:n]).then_inc(self.s_rowc, 1)

            def act_first(self, act, i):
                if i == NU - 1:
                    for j in range(3):
                        self.row(act, 0, 0, j)

            def copy_sums(self, act, h, b, j):
                n = FULL_SPANS[j][1]
                act.wait_ge(self.s_att, h * 3 + max(j - 1, 0))
                act.wait_ge(self.s_pv, h * NU + NT * (j + 1))
                act.copy(self.raw[:, (b + j) % 2, 0:n], self.summed[:, 0:n]).then_inc(self.s_raw, 1)

            def act_unit(self, act, p, b, u):
                h = p * 2 + b
                j, m = UNITS[u]
                n = FULL_SPANS[j][1]
                if u == 0 or u > 2:
                    act.wait_ge(self.s_pv, h * NU + max(u - 2, 0))
                act.wait_ge(self.s_mn, h * NU + (u + 1))
                act.activation(self.prob[0:rows(m), u % 3, 0:n], self.logits_mn[u % 2][0:rows(m), 0:n],
                               ACT.Exp).then_inc(self.s_pr, 1)
                for j in range(2):
                    if u == NT * (j + 1) + 1:
                        self.copy_sums(act, h, b, j)
                if u == NU - 1:
                    self.copy_sums(act, h, b, 2)
                    for j in range(3):
                        self.row(act, h + self.pre, 1 - b, j)

        ROUND_AT = 2
        NEXT_AFTER = [[i for i in range(NU) if ROUND_AT + 1 + i * (NU - ROUND_AT - 1) // NU == u] for u in range(NU)]
        EDGES_AFTER = [[[i for i in range(pair // 2) if i * NU // (pair // 2) == u] for u in range(NU)] for pair in PAIRS]

        LAGS = 5

        def beside(eng, attention, unit, edges):
            pair = attention.pair_chunks

            def two_heads(p):
                for b in range(2):
                    for u in range(NU):
                        unit(eng, p, b, u)
                        for i in EDGES_AFTER[attention.phase][u]:
                            edges(p, b * pair // 2 + i, 0, pair)
                for i in range(pair, pair + LAGS):
                    edges(p, i, 0, pair)

            two_heads(0)
            if attention.heads > 2:
                with eng.Fori(1, attention.heads // 2) as p:
                    two_heads(p)

        def load_rows(sp, load, used, first, n):
            with sp.Fori(0, n // SS) as t:
                for r in range(SS):
                    sp.wait_ge(used, t * SS + (first + r + 1))
                    load((first + r) % SS, t * SS + (first + r + SS))
            for r in range(n // SS * SS, n):
                sp.wait_ge(used, first + r + 1)
                load((first + r) % SS, first + r + SS)

        def load_beside(sp, attention, load, used):
            half = attention.pair_chunks // 2
            for h in range(attention.heads):
                load_rows(sp, load, used, attention.first_chunk + h * half, half - (SS if h == attention.heads - 1 else 0))
                attention.stage_next(sp, h)

        s_got = [mix.enter_context(nc.semaphore(f"slot_{k}_gathered")) for k in range(GS)]
        with ExitStack() as s:
            def sb(name, shape, dt=F32):
                return s.enter_context(nc.sbuf_tensor(name, shape, dt))

            semaphores = []

            def sem(name):
                semaphores.append(nc.alloc_semaphore(name))
                return semaphores[-1]

            attention = Attention(s, 0, sem)
            src_now = [sb(f"src_now{k}", [P, 1], I32) for k in range(GS)]
            source_now = [sb(f"source_now{k}", [P, GH]) for k in range(GS)]
            targets = [sb(f"targets{k}", [P, P], I32) for k in range(SS)]
            logit_now = [sb(f"logit_now{k}", [P, GH]) for k in range(SS)]
            other = [sb(f"other{k}", [P, P]) for k in range(SS)]
            earlier = [sb(f"earlier{k}", [P, 1]) for k in range(SS)]
            scratch_f = [sb(f"scratch_f{k}", [P, P]) for k in range(SS)]
            scratch_m = [sb(f"scratch_m{k}", [P, GH, P]) for k in range(SS)]
            max_now = [sb(f"max_now{k}", [P, GH]) for k in range(SS)]
            key_now = [sb(f"key_now{k}", [P, 1], I32) for k in range(SS)]
            spread = [s.enter_context(nc.psum_tensor(f"spread{k}", [P, GH, P], F32)) for k in range(2)]
            s_row = [sem(f"targets_{k}_loaded") for k in range(SS)]
            s_idx = sem("source_indices_written")
            s_first = sem("first_edges_found")
            s_rows = sem("row_numbers_ready")
            s_lg = sem("logits_ready")
            s_lc = sem("logits_kept")
            s_sp = sem("logits_spread")
            s_mx = sem("maxima_ready")
            s_put = [sem(f"maxima_{k}_stored") for k in range(SS)]
            ksum, b_v = attention.raw[:, 0, :], attention.raw[:, 1, :]
            s_wv = sem("v_bias_loaded")
            s_v = sem("v_ready")
            s_v_out = sem("v_copied")
            s_k = sem("k_ready")
            s_q = sem("q_ready")
            s_k_out = sem("k_copied")
            s_q_out = sem("q_copied")
            s_ks = sem("ksum_ready")
            s_ki = sem("ksum_steps")
            QK = [(m, j) for m in range(KT) for j in range(3)]
            PROJECTIONS = [("v", t) for t in range(NT)] + [("qk", i) for i in range(len(QK))] + [("maxima", i) for i in range(NU)]
            EARLY_AFTER = [1] * NT + [4] * len(QK)
            EARLY_AFTER[0] += EARLY_PARTS[0] - sum(EARLY_AFTER)
            EARLY_AFTER += [(i + 1) * EARLY_PARTS[1] // NU - i * EARLY_PARTS[1] // NU for i in range(NU)]
            EARLY_FROM = [sum(EARLY_AFTER[:n]) for n in range(len(EARLY_AFTER))]

            def beside_projections(project, edges):
                for n, (what, i) in enumerate(PROJECTIONS):
                    project(what, i)
                    for c in range(EARLY_FROM[n], EARLY_FROM[n] + EARLY_AFTER[n]):
                        edges(0, c - EARLY, -EARLY, 0)
                for c in range(LAGS):
                    edges(0, c, -EARLY, 0)

            with nc.Block() as block:
                @block.sync
                def _(sp):
                    def load(k, c):
                        sp.dma_start(targets[k][:], a["dst_row"][bass.ds(c * P, P)].partition_broadcast(P)).then_inc(s_row[k], 16)

                    for k in range(SS):
                        load(k, k)
                    sp.dma_start(b_v, a["bv"].partition_broadcast(P)).then_inc(s_wv, 16)
                    load_rows(sp, load, s_first, 0, EARLY_PARTS[0])
                    sp.wait_ge(s_v_out, NT)
                    sp.wait_ge(s_k_out, len(QK))
                    sp.wait_ge(s_ki, 3 * len(QK))
                    for b in range(2):
                        attention.stage(sp, b, 0)
                    load_rows(sp, load, s_first, EARLY_PARTS[0], EARLY_PARTS[1])
                    load_beside(sp, attention, load, s_first)
                    for b in range(2):
                        sp.wait_ge(attention.s_stage[b], 48 * 2)

                @block.gpsimd
                def _(pool):
                    def copy_index(k, c):
                        pool.tensor_copy(src_now[k][:], idx_i[:, bass.ds(c, 1), 0]).then_inc(s_idx, 1)

                    def gather(k):
                        pool.indirect_dma_start(source_now[k][:], None, source_table,
                                                bass.IndirectOffsetOnAxis(ap=src_now[k][:], axis=0)).then_inc(s_got[k], 16)

                    def store(k):
                        pool.indirect_dma_start(max_table, bass.IndirectOffsetOnAxis(ap=key_now[k][:], axis=0),
                                                max_now[k][:], None, bounds_check=NP * CH - 1,
                                                oob_is_err=False).then_inc(s_put[k], 16)

                    for k in range(GS):
                        if k:
                            pool.wait_ge(s_idx, k)
                        copy_index(k, k)
                        if k:
                            gather(k - 1)
                    with pool.Fori(0, CH // TURN - 1) as t:
                        for i in range(TURN):
                            pool.wait_ge(s_mx, t * TURN + (i + 1))
                            pool.wait_ge(s_rows, t * TURN + (i + 1))
                            pool.wait_ge(s_idx, t * TURN + (i + GS))
                            copy_index(i % GS, t * TURN + (i + GS))
                            store(i % SS)
                            gather((i + GS - 1) % GS)
                    for c in range(CH - TURN, CH):
                        pool.wait_ge(s_mx, c + 1)
                        pool.wait_ge(s_rows, c + 1)
                        if c + GS - 1 < CH:
                            pool.wait_ge(s_idx, c + GS)
                            if c + GS < CH:
                                copy_index(c % GS, c + GS)
                        store(c % SS)
                        if c + GS - 1 < CH:
                            gather((c + GS - 1) % GS)
                    for k in range(SS):
                        pool.wait_ge(s_put[k], 16 * CH // SS)

                @block.vector
                def _(dve):
                    def first_edges(p, i, low):
                        c, k = EARLY + p * PAIRS[0] + i, i % SS
                        if i - SS >= low:
                            dve.wait_ge(s_mx, c + 1 - SS)
                        elif c >= SS:
                            dve.wait_ge(s_mx, EARLY)
                        if c >= SS:
                            dve.wait_ge(s_rows, c + 1 - SS)
                        dve.wait_ge(s_row[k], (p * (PAIRS[0] // SS) + (EARLY + i) // SS) * 16 + 16)
                        dve.tensor_scalar(other[k][:], targets[k][:], dst_f[:, bass.ds(c, 1)], NEG, ALU.not_equal, ALU.mult)
                        dve.scalar_tensor_tensor(out=scratch_f[k][:], in0=targets[k][:], scalar=dst_f[:, bass.ds(c, 1)], in1=before[:],
                                                 op0=ALU.is_equal, op1=ALU.mult, accum_out=earlier[k][:]).then_inc(s_first, 1)

                    def logits(p, i):
                        dve.wait_ge(s_got[i % GS], (p * (PAIRS[0] // GS) + (EARLY + i) // GS) * 16 + 16)
                        dve.tensor_tensor(logit_now[i % SS][:], source_now[i % GS][:], logit[:, bass.ds(EARLY + p * PAIRS[0] + i, 1), :],
                                          ALU.add).then_inc(s_lg, 1)

                    def maxima(p, i):
                        c, k = EARLY + p * PAIRS[0] + i, i % SS
                        dve.wait_ge(s_lc, c + 1)
                        dve.wait_ge(s_sp, c + 1)
                        dve.wait_ge(s_put[k], (EARLY + i) // SS * 16)
                        for h in range(GH):
                            ins = dve.tensor_tensor_reduce(out=scratch_m[k][:, h, :], in0=spread[i % 2][:, h, :], in1=other[k][:],
                                                           scale=1.0, scalar=NEG, op0=ALU.add, op1=ALU.max,
                                                           accum_out=max_now[k][:, h:h + 1])
                        ins.then_inc(s_mx, 1)

                    def edges(p, i, low, high):
                        if i < high:
                            first_edges(p, i, low)
                            logits(p, i)
                        if low <= i - 2 < high:
                            maxima(p, i - 2)

                    def scale_q(i):
                        m, j = QK[i]
                        at, n = FULL_SPANS[j]
                        dve.wait_ge(s_ks, i + 1)
                        dve.wait_ge(s_ki, 3 * i)
                        dve.tensor_scalar(ksum[:, 0:n], attention.summed[:, 0:n], MIX_EPS, None, ALU.add).then_inc(s_ki, 1)
                        dve.wait_ge(s_ki, 3 * i + 1)
                        dve.reciprocal(ksum[:, 0:n], ksum[:, 0:n]).then_inc(s_ki, 1)
                        dve.wait_ge(s_ki, 3 * i + 2)
                        dve.wait_ge(s_q_out, i + 1)
                        dve.tensor_tensor(q_t[:, m, at:at + n], q_t[:, m, at:at + n], ksum[:, 0:n], ALU.mult).then_inc(s_ki, 1)

                    def project(what, i):
                        if what == "v":
                            if i == 0:
                                dve.wait_ge(s_wv, 16)
                            else:
                                add_bias(i - 1)
                        elif what == "qk":
                            if i == 0:
                                add_bias(NT - 1)
                            elif i >= 2:
                                scale_q(i - 2)
                        else:
                            if i == 0:
                                scale_q(len(QK) - 2)
                                scale_q(len(QK) - 1)
                            attention.dve_first(dve, i)

                    def add_bias(t):
                        dve.wait_ge(s_v, t + 1)
                        dve.tensor_tensor(v_tok[:, t, :], attention.logits_nm[t % 2][:], b_v, ALU.add).then_inc(s_v_out, 1)

                    attention.constant_columns(dve)
                    beside_projections(project, edges)
                    beside(dve, attention, attention.dve_unit, edges)

                @block.scalar
                def _(act):
                    def keep_logits(p, i):
                        act.wait_ge(s_lg, p * PAIRS[0] + (EARLY + i + 1))
                        act.copy(logit[:, bass.ds(EARLY + p * PAIRS[0] + i, 1), :], logit_now[i % SS][:]).then_inc(s_lc, 1)

                    def store_rows(p, i):
                        c, k = EARLY + p * PAIRS[0] + i, i % SS
                        act.wait_ge(s_put[k], (EARLY + i) // SS * 16)
                        act.wait_ge(s_first, c + 1)
                        act.activation(key_now[k][:], earlier[k][:], ACT.Identity, bias=key[:, c:c + 1], scale=SKIP)
                        act.activation(row_idx[:, c:c + 1], earlier[k][:], ACT.Identity, bias=dst_f[:, c:c + 1],
                                       scale=SKIP).then_inc(s_rows, 1)

                    def edges(p, i, low, high):
                        if low <= i - 1 < high:
                            store_rows(p, i - 1)
                            keep_logits(p, i - 1)

                    def project(what, i):
                        if what == "qk":
                            m, j = QK[i]
                            at, n = FULL_SPANS[j]
                            act.wait_ge(s_k, i + 1)
                            act.activation(k_t[:, m, at:at + n], attention.logits_mn[0][:, 0:n], ACT.Relu,
                                           bias=b_k[:, m:m + 1]).then_inc(s_k_out, 1)
                            act.wait_ge(s_q, i + 1)
                            act.activation(q_t[:, m, at:at + n], attention.logits_mn[1][:, 0:n], ACT.Relu,
                                           bias=b_q[:, m:m + 1]).then_inc(s_q_out, 1)
                        elif what == "maxima":
                            attention.act_first(act, i)

                    beside_projections(project, edges)

                    beside(act, attention, attention.act_unit, edges)

                @block.tensor
                def _(pe):
                    def spread_logits(p, i, low):
                        c, k = EARLY + p * PAIRS[0] + i, i % SS
                        pe.wait_ge(s_lg, c + 1)
                        pe.wait_ge(s_mx, EARLY + p * PAIRS[0] + max(i - 1, low))
                        for h in range(GH):
                            ins = pe.matmul(spread[i % 2][:, h, :], logit_now[k][:, h:h + 1].broadcast_to([P, P]), ident[:],
                                            start=True, stop=True)
                        ins.then_inc(s_sp, 1)

                    def edges(p, i, low, high):
                        if low <= i - 1 < high:
                            spread_logits(p, i - 1, low)

                    def sum_k(i):
                        m, j = QK[i]
                        at, n = FULL_SPANS[j]
                        pe.wait_ge(s_k_out, i + 1)
                        if i:
                            pe.wait_ge(s_ki, 3 * i - 2)
                        pe.matmul(attention.summed[:, 0:n], pair_ones[:], k_t[:, m, at:at + n], start=True, stop=True).then_inc(s_ks, 1)

                    def project(what, i):
                        if what == "v":
                            if i >= 2:
                                pe.wait_ge(s_v_out, i - 1)
                            for k in range(KT):
                                ins = pe.matmul(attention.logits_nm[i % 2][:], xn_t[:, k, i * P:(i + 1) * P], w_v[:, k, :],
                                                start=(k == 0), stop=(k == KT - 1))
                            ins.then_inc(s_v, 1)
                        elif what == "maxima":
                            if i == 0:
                                sum_k(len(QK) - 1)
                            attention.pe_first(pe, i)
                        else:
                            m, j = QK[i]
                            at, n = FULL_SPANS[j]
                            for bank, w, done, read in ((0, w_k, s_k, s_k_out), (1, w_q, s_q, s_q_out)):
                                if i:
                                    pe.wait_ge(read, i)
                                for k in range(KT):
                                    ins = pe.matmul(attention.logits_mn[bank][:, 0:n], w[:, k, m * P:(m + 1) * P],
                                                    xn_t[:, k, at:at + n], start=(k == 0), stop=(k == KT - 1))
                                ins.then_inc(done, 1)
                            if i:
                                sum_k(i - 1)

                    beside_projections(project, edges)
                    beside(pe, attention, attention.pe_unit, edges)
            nc.clear_and_free_semaphores(semaphores)
            nc.all_engine_barrier()

        with ExitStack() as s:
            def sb(name, shape, dt=F32):
                return s.enter_context(nc.sbuf_tensor(name, shape, dt))

            def sem(name):
                return s.enter_context(nc.semaphore(name))

            chunk_max = sb("chunk_max", [P, 4, CH, GH])
            node_max = sb("node_max", [P, NT, GH])
            target = sb("target", [P, NT, 2 * GH])
            s_cm = [sem(f"chunk_max_{b}_loaded") for b in range(4)]
            s_nm = sem("node_max_ready")
            s_tg = sem("target_ready")
            s_tab = sem("target_table_stored")
            s_d = sem("dve_steps_max")
            with nc.Block() as block:
                @block.sync
                def _(sp):
                    table = max_table.rearrange("(t p c) h -> t p c h", p=P, c=CH)
                    for t in range(NT):
                        if t >= 4:
                            sp.wait_ge(s_nm, t - 3)
                        sp.dma_start(chunk_max[:, t % 4, :, :], table[t]).then_inc(s_cm[t % 4], 16)
                    sp.wait_ge(s_tg, 1)
                    sp.dma_start(target_table.rearrange("(t p) j -> p t j", p=P), target[:]).then_inc(s_tab, 16)
                    sp.wait_ge(s_tab, 16)

                @block.vector
                def _(dve):
                    step = Steps(dve, s_d)
                    for t in range(NT):
                        dve.wait_ge(s_cm[t % 4], 16 * (t // 4 + 1))
                        dve.tensor_reduce(node_max[:, t, :], chunk_max[:, t % 4, :, :].rearrange("p c h -> p h c"),
                                          AX.X, ALU.max).then_inc(s_nm, 1)
                    dve.wait_ge(s_nm, NT)
                    step(dve.tensor_tensor(node_max[:], node_max[:], a_dst[:], ALU.add))
                    dve.tensor_copy(target[:, :, 0:GH], a_dst[:])
                    dve.scalar_tensor_tensor(out=target[:, :, GH:2 * GH], in0=node_max[:], scalar=SLOPE, in1=node_max[:],
                                             op0=ALU.mult, op1=ALU.max).then_inc(s_tg, 1)

        with ExitStack() as s:
            def sb(name, shape, dt=F32):
                return s.enter_context(nc.sbuf_tensor(name, shape, dt))

            def sem(name):
                return s.enter_context(nc.semaphore(name))

            attention = Attention(s, 1, sem)
            idx_now = [sb(f"idx_now{k}", [P, 2], I32) for k in range(GS)]
            feat = [xn_t[:].rearrange("p k n -> p (k n)")[:, k * D:(k + 1) * D] if (k + 1) * D <= KT * NP
                    else sb(f"feat{k}", [P, D])[:] for k in range(GS)]
            target_now = [sb(f"target_now{k}", [P, 2 * GH]) for k in range(GS)]
            targets = [sb(f"targets2_{k}", [P, P], I32) for k in range(SS)]
            same = [sb(f"same{k}", [P, P]) for k in range(SS)]
            expo = [sb(f"expo{k}", [P, GH]) for k in range(SS)]
            weight = [sb(f"weight{k}", [P, GH]) for k in range(SS)]
            row_now = [sb(f"row_now{k}", [P, 1], I32) for k in range(SS)]
            summed_sb = [sb(f"summed_sb{k}", [P, D + GH]) for k in range(SS)]
            ps = [s.enter_context(nc.psum_tensor(f"gs{b}", [P, 512], F32)) for b in range(2)]
            pw = [s.enter_context(nc.psum_tensor(f"gw{b}", [P, 512], F32)) for b in range(2)]
            s_row = [sem(f"targets2_{k}_loaded") for k in range(SS)]
            s_idx = sem("indices_written")
            GOT = 16 * CH // GS
            s_same = sem("same_targets_found")
            s_ch = sem("exponent_chain")
            s_wt = sem("weights_ready")
            s_msg = sem("messages_ready")
            s_sum = sem("messages_summed")
            s_cpf = sem("sums_copied_by_scalar")
            s_cpw = sem("weight_sums_copied_by_vector")
            s_add = [sem(f"sums_{k}_added") for k in range(SS)]
            with nc.Block() as block:
                @block.sync
                def _(sp):
                    def load(k, c):
                        sp.dma_start(targets[k][:], a["dst_row"][bass.ds(c * P, P)].partition_broadcast(P)).then_inc(s_row[k], 16)

                    for k in range(SS):
                        load(k, k)
                    load_beside(sp, attention, load, s_same)
                    for b in range(2):
                        sp.wait_ge(attention.s_stage[b], 48 * (attention.heads // 2 - b))

                @block.gpsimd
                def _(pool):
                    def copy_indices(k, c):
                        pool.tensor_copy(idx_now[k][:], idx_i[:, bass.ds(c, 1), :]).then_inc(s_idx, 1)

                    def gather(k):
                        pool.indirect_dma_start(target_now[k][:], None, target_table,
                                                bass.IndirectOffsetOnAxis(ap=idx_now[k][:, 1:2], axis=0)).then_inc(s_got[k], 16)
                        pool.indirect_dma_start(feat[k], None, feature_table,
                                                bass.IndirectOffsetOnAxis(ap=idx_now[k][:, 0:1], axis=0)).then_inc(s_got[k], 16)

                    def add(k):
                        pool.indirect_dma_start(sums_table[k], bass.IndirectOffsetOnAxis(ap=row_now[k][:], axis=0),
                                                summed_sb[k][:], None, bounds_check=NP - 1, oob_is_err=False,
                                                compute_op=ALU.add).then_inc(s_add[k], 16)

                    for k in range(GS):
                        if k:
                            pool.wait_ge(s_idx, k)
                        copy_indices(k, k)
                        if k:
                            gather(k - 1)
                    with pool.Fori(0, CH // TURN - 1) as t:
                        for i in range(TURN):
                            pool.wait_ge(s_cpf, t * TURN + (i + 1))
                            pool.wait_ge(s_cpw, t * TURN + (i + 1))
                            pool.wait_ge(s_idx, t * TURN + (i + GS))
                            copy_indices(i % GS, t * TURN + (i + GS))
                            add(i % SS)
                            gather((i + GS - 1) % GS)
                    for c in range(CH - TURN, CH):
                        pool.wait_ge(s_cpf, c + 1)
                        pool.wait_ge(s_cpw, c + 1)
                        if c + GS - 1 < CH:
                            pool.wait_ge(s_idx, c + GS)
                            if c + GS < CH:
                                copy_indices(c % GS, c + GS)
                        add(c % SS)
                        if c + GS - 1 < CH:
                            gather((c + GS - 1) % GS)
                    for k in range(SS):
                        pool.wait_ge(s_add[k], 16 * CH // SS)

                @block.vector
                def _(dve):
                    def exponents(p, i):
                        c, k, g = p * PAIRS[1] + i, i % SS, i % GS
                        dve.wait_ge(s_row[k], (p * (PAIRS[1] // SS) + i // SS) * 16 + 16)
                        dve.tensor_scalar(same[k][:], targets[k][:], dst_f[:, bass.ds(c, 1)], None, ALU.is_equal).then_inc(s_same, 1)
                        dve.wait_ge(s_got[g], (p * (PAIRS[1] // GS) + i // GS) * 32 + (GOT + 32))
                        dve.tensor_tensor(expo[k][:], logit[:, bass.ds(c, 1), :], target_now[g][:, 0:GH], ALU.add).then_inc(s_ch, 1)
                        dve.wait_ge(s_ch, c * 3 + 1)
                        dve.scalar_tensor_tensor(out=expo[k][:], in0=expo[k][:], scalar=SLOPE, in1=expo[k][:],
                                                 op0=ALU.mult, op1=ALU.max).then_inc(s_ch, 1)
                        dve.wait_ge(s_ch, c * 3 + 2)
                        dve.tensor_tensor(expo[k][:], expo[k][:], target_now[g][:, GH:2 * GH], ALU.subtract).then_inc(s_ch, 1)

                    def messages(p, i):
                        c, g = p * PAIRS[1] + i, i % GS
                        dve.wait_ge(s_wt, c + 1)
                        f = feat[g].rearrange("p (h c) -> p h c", c=GC)
                        dve.tensor_tensor(f, f, weight[i % SS][:].unsqueeze(2).broadcast_to([P, GH, GC]), ALU.mult).then_inc(s_msg, 1)

                    def weight_sums(p, i):
                        c, k = p * PAIRS[1] + i, i % SS
                        dve.wait_ge(s_add[k], (p * (PAIRS[1] // SS) + i // SS) * 16)
                        dve.tensor_copy(row_now[k][:], row_idx[:, bass.ds(c, 1)])
                        dve.wait_ge(s_sum, c + 1)
                        dve.tensor_copy(summed_sb[k][:, D:D + GH], pw[i % 2][:, 0:GH]).then_inc(s_cpw, 1)

                    def edges(p, i, low, high):
                        if low <= i - 4 < high:
                            weight_sums(p, i - 4)
                        if i < high:
                            exponents(p, i)
                        if low <= i - 2 < high:
                            messages(p, i - 2)

                    beside(dve, attention, attention.dve_unit, edges)

                @block.scalar
                def _(act):
                    def copy_sums(p, i):
                        c, k, turn = p * PAIRS[1] + i, i % SS, p * (PAIRS[1] // SS) + i // SS
                        act.wait_ge(s_add[k], turn * 16)
                        act.wait_ge(s_sum, c + 1)
                        act.copy(summed_sb[k][:, 0:D], ps[i % 2][:]).then_inc(s_cpf, 1)

                    def weights(p, i):
                        act.wait_ge(s_ch, (p * PAIRS[1] + i) * 3 + 3)
                        act.activation(weight[i % SS][:], expo[i % SS][:], ACT.Exp).then_inc(s_wt, 1)

                    def edges(p, i, low, high):
                        if low <= i - 1 < high:
                            weights(p, i - 1)
                        if low <= i - 4 < high:
                            copy_sums(p, i - 4)

                    beside(act, attention, attention.act_unit, edges)

                @block.tensor
                def _(pe):
                    def sum_messages(p, i):
                        c, b = p * PAIRS[1] + i, i % 2
                        pe.wait_ge(s_msg, c + 1)
                        pe.wait_ge(s_cpf, p * PAIRS[1] + max(i - 1, 0))
                        pe.wait_ge(s_cpw, p * PAIRS[1] + max(i - 1, 0))
                        pe.matmul(pw[b][:, 0:GH], same[i % SS][:], weight[i % SS][:], start=True, stop=True)
                        pe.matmul(ps[b][:], same[i % SS][:], feat[i % GS], start=True, stop=True).then_inc(s_sum, 1)

                    def edges(p, i, low, high):
                        if low <= i - 3 < high:
                            sum_messages(p, i - 3)

                    beside(pe, attention, attention.pe_unit, edges)

        with ExitStack() as s:
            def sb(name, shape, dt=F32):
                return s.enter_context(nc.sbuf_tensor(name, shape, dt))

            def sem(name):
                return s.enter_context(nc.semaphore(name))

            w_o = sb("w_o", [P, KT, D])
            got = [[sb(f"got{b}_{k}", [P, D + GH]) for k in range(SS)] for b in range(2)]
            node = q_t[:].rearrange("p k n -> p (k n)").rearrange("p (t d) -> p t d", d=D)
            square = sb("square", [P, 2, D])
            weight = sb("node_weight", [P, 2, GH])
            bias = sb("bias", [P, D])
            gamma = sb("gamma", [P, D])
            shift = sb("shift", [P, 2, D])
            scale = sb("scale", [P, D])
            eps_bn = sb("eps_bn", [P, 1])
            stats = sb("stats_x1", [P, NT, 6])
            mixed = [s.enter_context(nc.psum_tensor(f"mixed{b}", [P, 512], F32)) for b in range(4)]
            mean_ps = s.enter_context(nc.psum_tensor("mean_ps", [P, 512], F32))
            var_ps = s.enter_context(nc.psum_tensor("var_ps", [P, 512], F32))
            s_w = sem("wo_loaded")
            s_c = sem("batch_norm_constants_loaded")
            s_sh = sem("shifts_summed")
            s_xs = sem("shift_added")
            s_m = sem("mixed_ready")
            s_x = sem("mixed_added")
            s_got = [sem(f"sums_{b}_loaded") for b in range(2)]
            s_g23 = sem("second_pair_of_sums_added")
            s_free = sem("sums_read")
            s_node = sem("node_ready")
            s_mean = sem("mean_ready")
            s_sq = sem("square_ready")
            s_varu = sem("squares_used")
            s_dev = sem("deviation_ready_bn")
            s_eps = sem("eps_ready")
            s_scale = sem("scale_ready")
            s_sc = sem("node_scaled")
            s_done = sem("x1_ready")
            s_st = sem("x1_stats_ready")
            s_d = sem("dve_steps_bn")
            with nc.Block() as block:
                @block.sync
                def _(sp):
                    sp.dma_start(w_o[:], a["wo_t"].rearrange("(k p) o -> p k o", p=P)).then_inc(s_w, 16)
                    for t in range(NT):
                        b = t % 2
                        if t >= 2:
                            sp.wait_ge(s_free, t - 1)
                        for k in range(SS):
                            sp.dma_start(got[b][k][:], sums_table[k][t * P:(t + 1) * P, :]).then_inc(s_got[b], 16)

                @block.gpsimd
                def _(pool):
                    pool.wait_ge(s_c, 64)
                    pool.tensor_tensor(shift[:, 0, :], shift[:, 0, :], shift[:, 1, :], ALU.add).then_inc(s_sh, 1)
                    pool.wait_ge(s_sh, 1)
                    for t in range(NT):
                        pool.wait_ge(s_got[t % 2], 16 * SS * (t // 2 + 1))
                        pool.tensor_tensor(got[t % 2][2][:], got[t % 2][2][:], got[t % 2][3][:], ALU.add).then_inc(s_g23, 1)
                        pool.tensor_tensor(x1[:, t, :], x1[:, t, :], shift[:, 0, :], ALU.add).then_inc(s_xs, 1)
                    pool.wait_ge(s_scale, 1)
                    pool.wait_ge(s_sq, NT)
                    for t in range(NT):
                        pool.tensor_tensor(node[:, t, :], node[:, t, :], scale[:], ALU.mult).then_inc(s_sc, 1)

                @block.tensor
                def _(pe):
                    pe.wait_ge(s_w, 16)
                    for t in range(NT):
                        if t >= 4:
                            pe.wait_ge(s_x, t - 3)
                        for k in range(KT):
                            ins = pe.matmul(mixed[t % 4][:], att_out[:, k, t * P:(t + 1) * P], w_o[:, k, :],
                                            start=(k == 0), stop=(k == KT - 1))
                        ins.then_inc(s_m, 1)
                    for t in range(NT):
                        pe.wait_ge(s_free, t + 1)
                        ins = pe.matmul(mean_ps[:], ones[0:rows(t), :], node[0:rows(t), t, :], start=(t == 0), stop=(t == NT - 1))
                    ins.then_inc(s_mean, 1)
                    for t in range(NT):
                        pe.wait_ge(s_sq, t + 1)
                        pe.matmul(var_ps[:], ones[0:rows(t), :], square[0:rows(t), t % 2, :], start=(t == 0),
                                  stop=(t == NT - 1)).then_inc(s_varu, 1)

                @block.vector
                def _(dve):
                    step = Steps(dve, s_d)
                    dve.memset(eps_bn[:], BN_EPS).then_inc(s_eps, 1)
                    for t in range(NT):
                        b = t % 2
                        g = got[b]
                        dve.wait_ge(s_got[b], 16 * SS * (t // 2 + 1))
                        step(dve.tensor_tensor(g[0][:], g[0][:], g[1][:], ALU.add))
                        dve.wait_ge(s_g23, t + 1)
                        step(dve.tensor_tensor(g[0][:], g[0][:], g[2][:], ALU.add))
                        step(dve.tensor_scalar(weight[:, b, :], g[0][:, D:D + GH], 1e-16, None, ALU.add))
                        step(dve.reciprocal(weight[:, b, :], weight[:, b, :]))
                        f = g[0][:, 0:D].rearrange("p (h c) -> p h c", c=GC)
                        step(dve.tensor_tensor(f, f, weight[:, b, :].unsqueeze(2).broadcast_to([P, GH, GC]), ALU.mult))
                        if t == 0:
                            dve.wait_ge(s_c, 64)
                        dve.tensor_tensor(node[:, t, :], g[0][:, 0:D], bias[:], ALU.add).then_inc(s_free, 1)
                        dve.wait_ge(s_xs, t + 1)
                        dve.wait_ge(s_m, t + 1)
                        dve.tensor_tensor(x1[:, t, :], x1[:, t, :], mixed[t % 4][:], ALU.add).then_inc(s_x, 1)
                    dve.wait_ge(s_mean, 1)
                    dve.wait_ge(s_free, NT)
                    for t in range(NT):
                        dve.scalar_tensor_tensor(out=node[:, t, :], in0=mean_ps[:], scalar=-1.0 / N, in1=node[:, t, :],
                                                 op0=ALU.mult, op1=ALU.add).then_inc(s_node, 1)
                    dve.wait_ge(s_dev, 1)
                    step(dve.reciprocal(scale[:], scale[:]))
                    dve.tensor_tensor(scale[:], scale[:], gamma[:], ALU.mult).then_inc(s_scale, 1)
                    dve.wait_ge(s_x, NT)
                    for t in range(NT + 3):
                        if 0 <= t - 1 < NT:
                            dve.wait_ge(s_sc, t)
                            dve.tensor_tensor(x1[:, t - 1, :], x1[:, t - 1, :], node[:, t - 1, :], ALU.add).then_inc(s_done, 1)
                        if 0 <= t - 2 < NT:
                            dve.wait_ge(s_done, t - 1)
                            dve.bn_stats(stats[:, t - 2, :], x1[:, t - 2, :]).then_inc(s_st, 1)
                        if 0 <= t - 3 < NT:
                            dve.wait_ge(s_st, t - 2)
                            dve.bn_aggr(mv_x1[:, t - 3, :], stats[:, t - 3, :])

                @block.scalar
                def _(act):
                    for dst, name in ((bias[:], "gat_bias"), (shift[:, 0, :], "bo"), (shift[:, 1, :], "beta"), (gamma[:], "gamma")):
                        act.dma_start(dst, a[name].partition_broadcast(P)).then_inc(s_c, 16)
                    act.wait_ge(s_eps, 1)
                    for t in range(NT):
                        act.wait_ge(s_node, t + 1)
                        if t >= 2:
                            act.wait_ge(s_varu, t - 1)
                        act.activation(square[:, t % 2, :], node[:, t, :], ACT.Square).then_inc(s_sq, 1)
                    act.wait_ge(s_varu, NT)
                    act.activation(scale[:], var_ps[:], ACT.Sqrt, bias=eps_bn[:], scale=1.0 / N).then_inc(s_dev, 1)
        mix.close()
        gat.close()

        with ExitStack() as s:
            def sb(name, shape, dt=F32):
                return s.enter_context(nc.sbuf_tensor(name, shape, dt))

            def sem(name):
                return s.enter_context(nc.semaphore(name))

            HALO = NP + 2 * PAD
            yn = sb("yn", [P, NT, D])
            yn_t = [sb(f"yn_t_{part}", [P, KT, HALO], F32R) for part in ("hi", "lo")]
            rc_act = sb("rc_act", [P, KT, HALO])
            rc_w2 = sb("rc_w2", [P, KT, RC_TAPS * 32])
            sh_w2 = sb("sh_w2", [P, HT, D])
            CW = RC_TAPS * KT * P
            EW = KT * HID
            w_f32 = [sb(f"w_f32_{b}", [P, 2 * EW]) for b in range(2)]
            w_split = [[sb(f"w_{part}_{b}", [P, 2 * EW], F32R) for part in ("hi", "lo")] for b in range(2)]
            rc_b1 = sb("rc_b1", [P, KT])
            rc_b2 = sb("rc_b2", [P, XE])
            sh_b1 = sb("sh_b1", [P, HT])
            e_b1 = [sb(f"e_b1_{b}", [P, HT]) for b in range(2)]
            out_bias = sb("out_bias", [XE + 1, D])
            ln_g = sb("ln_g", [P, D])
            h_act = [[sb(f"h_{part}_{b}", [P, HT, N], F32R) for part in ("hi", "lo")] for b in range(2)]
            hidden_f32 = sb("hidden_f32", [P, 3, 512])
            logits = sb("logits", [P, NT, XE])
            number_i = sb("number_i", [P, NT, XE], I32)
            top = sb("top", [P, 2, NT])
            which = sb("which", [P, NT])
            share = sb("share", [P, 2, NT])
            first, second, place, number = (rc_act[:, 1 + HT, i * 128:i * 128 + NT * XE].rearrange("p (t e) -> p t e", e=XE)
                                            for i in range(4))
            tap_sel = sb("tap_sel", [P, XE])
            ln_b = hidden_f32[:, 2, :]
            tap_sum = tap_sel[0:RC_TAPS * 32, :]
            tap_out = hidden_f32[0:RC_TAPS * 32].rearrange("p a b -> p (a b)")[:, 0:HALO]
            gates = sb("gates", [P, NT, XE + 1])
            gates_t = rc_act[0:XE + 1, 0, 0:N]
            sh_act = rc_act[:, 1:1 + HT, 0:N]
            negative = rc_act[:, 1 + HT, 0:1024].rearrange("p (b n) -> p b n", b=2)
            stats = sb("f_stats", [P, NT, 6])
            mv = mv_x1
            std = sb("f_std", [P, NT])
            rstd = sb("f_rstd", [P, NT])
            up = [s.enter_context(nc.psum_tensor(f"up{b}", [P, 512], F32)) for b in range(6)]
            down = [s.enter_context(nc.psum_tensor(f"down{b}", [P, 512], F32)) for b in range(2)]
            s_cw = [sem(f"conv_weights_{b}_loaded") for b in range(2)]
            s_chi = sem("conv_weights_high_ready")
            s_clo = sem("conv_weights_low_ready")
            s_bias = sem("biases_loaded")
            s_exp = [sem(f"expert_{b}_loaded") for b in range(2)]
            s_ehi = [sem(f"expert_layer_{j}_high_ready") for j in range(2)]
            s_elo = [sem(f"expert_layer_{j}_low_ready") for j in range(2)]
            s_iota = sem("expert_numbers_ready")
            s_wz = sem("router_weights_zeroed")
            s_xb = sem("x1_shifted")
            s_tap = sem("tap_outputs_ready")
            s_tapc = sem("tap_outputs_copied")
            s_zero = sem("halos_zeroed")
            s_stat = sem("z_variance_ready")
            s_std = sem("deviation_of_x1_then_z_ready")
            s_yn = sem("yn_ready")
            s_tr = sem("yn_transposed")
            s_yh = sem("yn_t_high_ready")
            s_yt = sem("yn_t_low_ready")
            s_part = sem("conv_portion_used")
            s_unit = sem("hidden_unit_ready")
            s_act = sem("hidden_unit_activated")
            s_low = sem("hidden_unit_minimum_taken")
            s_ex = sem("hidden_unit_exponent_ready")
            s_elu = sem("hidden_unit_elu_ready")
            s_hh = sem("hidden_unit_high_ready")
            s_h = sem("hidden_unit_low_ready")
            s_lg = sem("router_logits_ready")
            s_lgc = sem("router_logits_copied")
            s_gap = sem("top_difference_ready")
            s_gx = sem("top_exponent_ready")
            s_gate = sem("gates_ready")
            s_gt = sem("gates_transposed")
            s_gtc = sem("gates_t_ready")
            s_dn = sem("token_tile_ready")
            s_add = sem("token_tile_added")
            s_zs = sem("z_stats_ready")
            s_norm = sem("z_normalised")
            s_gn = sem("z_scaled")
            s_out = sem("out_tile_ready")
            s_st = sem("out_stored")
            s_d = sem("dve_steps_ffn")
            PORTIONS = [("rc_w1", m, 0) for m in range(KT)] + [("sh_w1", m, 3 * r) for m in range(HT) for r in range(3)]
            NPOR = len(PORTIONS)
            CONV = (KT + HT) * 3
            EU = HT * 3
            ROUTE_AFTER = KT
            GATES_AT = KT + 1

            def need(eng, sem, count):
                if not (isinstance(count, int) and count <= 0):
                    eng.wait_ge(sem, count)

            def conv_view(w):
                return w[:, 0:CW].rearrange("p (j k o) -> p j k o", j=RC_TAPS, k=KT)

            def layer_view(w, j):
                return w[:, j * EW:(j + 1) * EW].rearrange("p (k o) -> p k o", k=KT if j == 0 else HT)

            with nc.Block() as block:
                @block.sync
                def _(sp):
                    def portion(n):
                        name, m, tap = PORTIONS[n]
                        sp.dma_start(conv_view(w_f32[n % 2]), a[name][m, tap:tap + RC_TAPS].rearrange("j (k p) o -> p j k o", p=P)).then_inc(s_cw[n % 2], 16)

                    for n in range(2):
                        portion(n)
                    with nc.allow_non_contiguous_dma(reason="small vectors, one number for a partition"):
                        sp.dma_start(rc_b1[:], a["rc_b1"].rearrange("(k p) -> p k", p=P)).then_inc(s_bias, 16)
                        sp.dma_start(sh_b1[:], a["sh_b1"].rearrange("(k p) -> p k", p=P)).then_inc(s_bias, 16)
                        sp.wait_ge(s_wz, 1)
                        for j in range(RC_TAPS):
                            sp.dma_start(rc_w2[:, :, 32 * j:32 * j + XE], a["rc_w2"][j].rearrange("(k p) o -> p k o", p=P)).then_inc(s_bias, 16)
                    sp.dma_start(rc_b2[:], a["rc_b2"].partition_broadcast(P)).then_inc(s_bias, 16)
                    sp.dma_start(out_bias[0:XE, :], a["e_b2"]).then_inc(s_bias, 16)
                    sp.dma_start(out_bias[XE:XE + 1, :], a["sh_b2"].partition_broadcast(1)).then_inc(s_bias, 16)
                    sp.dma_start(ln_g[:], a["ln_g"].partition_broadcast(P)).then_inc(s_bias, 16)
                    sp.dma_start(ln_b, a["ln_b"].partition_broadcast(P)).then_inc(s_bias, 16)
                    sp.dma_start(sh_w2[:], a["sh_w2"].rearrange("(k p) o -> p k o", p=P)).then_inc(s_bias, 16)
                    for n in range(2, NPOR):
                        sp.wait_ge(s_clo, n - 1)
                        portion(n)

                    def expert(b, e):
                        sp.dma_start(layer_view(w_f32[b], 0), a["e_w1"][bass.ds(e, 1), :, :].rearrange("e (k p) o -> p (e k) o", p=P)).then_inc(s_exp[b], 16)
                        sp.dma_start(layer_view(w_f32[b], 1), a["e_w2"][bass.ds(e, 1), :, :].rearrange("e (k p) o -> p (e k) o", p=P)).then_inc(s_exp[b], 16)
                        sp.dma_start(e_b1[b][:], a["e_b1_cols"][bass.ds(e, 1), :, :].rearrange("e p k -> p (e k)")).then_inc(s_exp[b], 16)

                    for b in range(2):
                        sp.wait_ge(s_clo, NPOR - 1 + b)
                        expert(b, b)
                    with sp.Fori(1, XE // 2) as u:
                        for b in range(2):
                            sp.wait_ge(s_elo[0], u * 2 + (b - 1))
                            sp.wait_ge(s_elo[1], u * 2 + (b - 1))
                            sp.wait_ge(s_h, u * (2 * EU) + (b - 1) * EU)
                            expert(b, u * 2 + b)
                    for t in range(NT):
                        sp.wait_ge(s_out, t + 1)
                        sp.dma_start(out[t * P:t * P + rows(t), :], yn[0:rows(t), t, :]).then_inc(s_st, 16)
                    sp.wait_ge(s_st, 16 * NT)

                @block.gpsimd
                def _(pool):
                    pool.memset(rc_w2[:], 0.0).then_inc(s_wz, 1)
                    pool.wait_ge(s_bias, 176)
                    for t in range(NT):
                        pool.wait_ge(s_yn, t + 1)
                        pool.tensor_tensor(x1[:, t, :], x1[:, t, :], ln_b, ALU.add).then_inc(s_xb, 1)
                    pool.iota(number_i[:], pattern=[[0, NT], [1, XE]], base=0, channel_multiplier=0).then_inc(s_iota, 1)
                    for t in range(NT):
                        pool.wait_ge(s_gn, t + 1)
                        pool.tensor_tensor(yn[:, t, :], yn[:, t, :], x1[:, t, :], ALU.add).then_inc(s_out, 1)

                @block.tensor
                def _(pe):
                    def split_product(bank, terms, start=True, stop=True):
                        passes = [(w[i], x[j]) for w, x in terms for i, j in ((0, 0), (0, 1), (1, 0))]
                        for n, (w, x) in enumerate(passes):
                            ins = pe.matmul(bank, w, x, start=start and n == 0, stop=stop and n == len(passes) - 1)
                        return ins

                    for t in range(NT):
                        pe.wait_ge(s_yn, t + 1)
                        if t >= 2:
                            pe.wait_ge(s_yt, t - 1)
                        for k in range(KT):
                            ins = pe.transpose(down[t % 2][:, k * P:(k + 1) * P], yn[:, t, k * P:(k + 1) * P], ident[:])
                        ins.then_inc(s_tr, 1)
                    pe.wait_ge(s_yt, NT)
                    pe.wait_ge(s_zero, 3)
                    unit = 0
                    for n, (name, m, tap) in enumerate(PORTIONS):
                        router = name == "rc_w1"
                        begin, end = tap == 0, router or tap == SH_TAPS - 3
                        output = m if router else KT + m
                        hi, lo = (conv_view(w) for w in w_split[n % 2])
                        pe.wait_ge(s_chi, n + 1)
                        pe.wait_ge(s_clo, n + 1)
                        for j, (at, width) in enumerate(SPANS):
                            if begin and output >= 2:
                                pe.wait_ge(s_act, 3 * (output - 2) + j + 1)
                            terms = []
                            for i in range(RC_TAPS):
                                col = at + PAD - (RC_TAPS if router else SH_TAPS) // 2 + tap + i
                                for k in range(KT):
                                    terms.append(((hi[:, i, k, :], lo[:, i, k, :]),
                                                  (yn_t[0][:, k, col:col + width], yn_t[1][:, k, col:col + width])))
                            ins = split_product(up[3 * (output % 2) + j][:, 0:width], terms, begin, end)
                            if end:
                                ins.then_inc(s_unit, 1)
                            elif j == 2:
                                ins.then_inc(s_part, 1)
                        if n == ROUTE_AFTER:
                            pe.wait_ge(s_act, KT * 3)
                            pe.wait_ge(s_bias, 176)
                            for j, (at, width) in enumerate(FULL_SPANS):
                                if j == 2:
                                    pe.wait_ge(s_tapc, 2 + RC_TAPS)
                                for k in range(KT):
                                    ins = pe.matmul(down[j % 2][0:RC_TAPS * 32, 0:width], rc_w2[:, k, :], rc_act[:, k, PAD + at:PAD + at + width],
                                                    start=(k == 0), stop=(k == KT - 1))
                                ins.then_inc(s_tap, 1)
                        if n == ROUTE_AFTER + 1:
                            pe.wait_ge(s_tapc, 2 + 3 * RC_TAPS)
                            for t in range(NT):
                                if t >= 2:
                                    pe.wait_ge(s_lgc, t - 1)
                                pe.matmul(down[t % 2][:, 0:XE], tap_out[:, PAD + t * P:PAD + (t + 1) * P], tap_sum,
                                          start=True, stop=True).then_inc(s_lg, 1)

                    def first_layer(b, e):
                        pe.wait_ge(s_ehi[0], e + 1)
                        pe.wait_ge(s_elo[0], e + 1)
                        hi, lo = (layer_view(w, 0) for w in w_split[b])
                        for i in range(EU):
                            m, (at, n) = i // 3, SPANS[i % 3]
                            if isinstance(e, int) and e == 0:
                                pe.wait_ge(s_act, CONV - EU + i + 1)
                            else:
                                pe.wait_ge(s_low, e * EU + (i + 1 - EU))
                            split_product(up[i][:, 0:n], [((hi[:, k, m * P:(m + 1) * P], lo[:, k, m * P:(m + 1) * P]),
                                                           (yn_t[0][:, k, PAD + at:PAD + at + n], yn_t[1][:, k, PAD + at:PAD + at + n]))
                                                          for k in range(KT)]).then_inc(s_unit, 1)

                    def second_layer(b, e):
                        pe.wait_ge(s_ehi[1], e + 1)
                        pe.wait_ge(s_elo[1], e + 1)
                        pe.wait_ge(s_hh, e * EU + EU)
                        pe.wait_ge(s_h, e * EU + EU)
                        hi, lo = (layer_view(w, 1) for w in w_split[b])
                        h_hi, h_lo = h_act[b]
                        for t in range(NT):
                            n = rows(t)
                            pe.wait_ge(s_add, e * NT + (NT + t - 1))
                            split_product(down[t % 2][0:n, :], [((h_hi[:, k, t * P:t * P + n], h_lo[:, k, t * P:t * P + n]),
                                                                 (hi[:, k, :], lo[:, k, :])) for k in range(HT)]).then_inc(s_dn, 1)

                    first_layer(0, 0)
                    pe.wait_ge(s_gate, 1)
                    for q in range(3):
                        if q == 2:
                            pe.wait_ge(s_gtc, 1)
                        for t in range(4 * q, min(4 * q + 4, NT)):
                            ins = pe.transpose(down[q % 2][0:XE + 1, (t % 4) * P:(t % 4 + 1) * P], gates[:, t, :], ident[:])
                        ins.then_inc(s_gt, 1)
                    pe.wait_ge(s_gtc, 3)
                    pe.wait_ge(s_act, CONV)
                    for t in range(NT):
                        if t >= 2:
                            pe.wait_ge(s_add, t - 1)
                        n = rows(t)
                        for k in range(HT):
                            pe.matmul(down[t % 2][0:n, :], sh_act[:, k, t * P:t * P + n], sh_w2[:, k, :], start=(k == 0), stop=False)
                        pe.matmul(down[t % 2][0:n, :], gates_t[:, t * P:t * P + n], out_bias[:], start=False, stop=True).then_inc(s_dn, 1)
                    with pe.Fori(0, XE // 2 - 1) as u:
                        first_layer(1, u * 2 + 1)
                        second_layer(0, u * 2)
                        first_layer(0, u * 2 + 2)
                        second_layer(1, u * 2 + 1)
                    first_layer(1, XE - 1)
                    second_layer(0, XE - 2)
                    second_layer(1, XE - 1)

                @block.scalar
                def _(act):
                    def portion_used(n):
                        last = [p[0] == "rc_w1" or p[2] == SH_TAPS - 3 for p in PORTIONS[:n + 1]]
                        if last[n]:
                            act.wait_ge(s_unit, 3 * sum(last))
                        else:
                            act.wait_ge(s_part, n + 1 - sum(last))

                    def split_conv(n):
                        act.wait_ge(s_cw[n % 2], 16 * (n // 2 + 1))
                        if n >= 2:
                            portion_used(n - 2)
                        act.copy(w_split[n % 2][0][:, 0:CW], w_f32[n % 2][:, 0:CW]).then_inc(s_chi, 1)

                    def split_expert(b, e, turn, j):
                        act.wait_ge(s_exp[b], turn * 48 + 48)
                        if isinstance(e, int) and e < 2:
                            portion_used(NPOR - 2 + e)
                        elif j == 0:
                            act.wait_ge(s_unit, e * EU + (CONV - EU))
                        else:
                            act.wait_ge(s_dn, e * NT)
                        act.copy(w_split[b][0][:, j * EW:(j + 1) * EW], w_f32[b][:, j * EW:(j + 1) * EW]).then_inc(s_ehi[j], 1)

                    act.activation(std[:], mv[:, :, 1], ACT.Sqrt, bias=eps_ln[:]).then_inc(s_std, 1)
                    split_conv(0)
                    split_conv(1)
                    act.wait_ge(s_zero, 3)
                    for t in range(NT):
                        n = rows(t)
                        act.wait_ge(s_tr, t + 1)
                        act.copy(yn_t[0][:, :, PAD + t * P:PAD + t * P + n],
                                 down[t % 2][:].rearrange("p (k n) -> p k n", k=KT)[:, :, 0:n]).then_inc(s_yh, 1)
                    act.wait_ge(s_bias, 176)
                    i = 0
                    for n, (name, m, tap) in enumerate(PORTIONS):
                        router = name == "rc_w1"
                        if router or tap == SH_TAPS - 3:
                            for j, (at, width) in enumerate(SPANS):
                                act.wait_ge(s_unit, i + 1)
                                bank = up[3 * ((m if router else KT + m) % 2) + j][:, 0:width]
                                if router:
                                    act.activation(rc_act[:, m, PAD + at:PAD + at + width], bank, ACT.Gelu,
                                                   bias=rc_b1[:, m:m + 1]).then_inc(s_act, 1)
                                else:
                                    act.activation(sh_act[:, m, at:at + width], bank, ACT.Silu,
                                                   bias=sh_b1[:, m:m + 1]).then_inc(s_act, 1)
                                i += 1
                        if n + 2 < NPOR:
                            split_conv(n + 2)
                        if n == GATES_AT:
                            act.wait_ge(s_gap, 1)
                            act.activation(share[:, 1, :], share[:, 0, :], ACT.Exp).then_inc(s_gx, 1)
                        if n == NPOR - 2:
                            split_expert(0, 0, 0, 0)
                            split_expert(0, 0, 0, 1)
                    split_expert(1, 1, 0, 0)

                    def hidden(b, e):
                        for i in range(EU + 2):
                            if i < EU:
                                m, n = i // 3, SPANS[i % 3][1]
                                need(act, s_h, e * EU + (i - 2))
                                act.wait_ge(s_unit, e * EU + (CONV + i + 1))
                                act.activation(hidden_f32[:, i % 3, 0:n], up[i][:, 0:n], ACT.Relu,
                                               bias=e_b1[b][:, m:m + 1]).then_inc(s_act, 1)
                            if 0 <= i - 1 < EU:
                                n = SPANS[(i - 1) % 3][1]
                                act.wait_ge(s_low, e * EU + i)
                                act.activation(negative[:, (i - 1) % 2, 0:n], negative[:, (i - 1) % 2, 0:n], ACT.Exp).then_inc(s_ex, 1)
                            if 0 <= i - 2 < EU:
                                m, (at, n) = (i - 2) // 3, SPANS[(i - 2) % 3]
                                if i == 2 and not (isinstance(e, int) and e < 2):
                                    act.wait_ge(s_dn, e * NT)
                                act.wait_ge(s_elu, e * EU + (i - 1))
                                act.copy(h_act[b][0][:, m, at:at + n], hidden_f32[:, (i - 2) % 3, 0:n]).then_inc(s_hh, 1)

                    hidden(0, 0)
                    split_expert(1, 1, 0, 1)
                    split_expert(0, 2, 1, 0)
                    hidden(1, 1)
                    split_expert(0, 2, 1, 1)
                    split_expert(1, 3, 1, 0)
                    with act.Fori(1, XE // 2 - 1) as u:
                        hidden(0, u * 2)
                        split_expert(1, u * 2 + 1, u, 1)
                        split_expert(0, u * 2 + 2, u + 1, 0)
                        hidden(1, u * 2 + 1)
                        split_expert(0, u * 2 + 2, u + 1, 1)
                        split_expert(1, u * 2 + 3, u + 1, 0)
                    hidden(0, XE - 2)
                    split_expert(1, XE - 1, XE // 2 - 1, 1)
                    hidden(1, XE - 1)
                    act.wait_ge(s_stat, 1)
                    act.activation(std[:], mv[:, :, 1], ACT.Sqrt, bias=eps_ln[:]).then_inc(s_std, 1)

                @block.vector
                def _(dve):
                    step = Steps(dve, s_d)

                    def split_conv(n):
                        dve.wait_ge(s_chi, n + 1)
                        dve.tensor_tensor(w_split[n % 2][1][:, 0:CW], w_f32[n % 2][:, 0:CW], w_split[n % 2][0][:, 0:CW],
                                          ALU.subtract).then_inc(s_clo, 1)

                    def split_expert(b, e, j):
                        cols = slice(j * EW, (j + 1) * EW)
                        dve.wait_ge(s_ehi[j], e + 1)
                        dve.tensor_tensor(w_split[b][1][:, cols], w_f32[b][:, cols], w_split[b][0][:, cols],
                                          ALU.subtract).then_inc(s_elo[j], 1)

                    dve.memset(rc_act[:], 0.0).then_inc(s_zero, 1)
                    dve.wait_ge(s_zero, 1)
                    for part in range(2):
                        dve.tensor_copy(yn_t[part][:], rc_act[:]).then_inc(s_zero, 1)
                    dve.wait_ge(s_std, 1)
                    step(dve.reciprocal(rstd[:], std[:]))
                    dve.wait_ge(s_zero, 3)

                    def to_columns(t):
                        n = rows(t)
                        dve.wait_ge(s_yh, t + 1)
                        cols = slice(PAD + t * P, PAD + t * P + n)
                        dve.tensor_tensor(yn_t[1][:, :, cols], down[t % 2][:].rearrange("p (k n) -> p k n", k=KT)[:, :, 0:n],
                                          yn_t[0][:, :, cols], ALU.subtract).then_inc(s_yt, 1)

                    for t in range(NT):
                        dve.tensor_scalar(yn[:, t, :], x1[:, t, :], mv[:, t, 0:1], rstd[:, t:t + 1],
                                          ALU.subtract, ALU.mult).then_inc(s_yn, 1)
                        if t >= 1:
                            to_columns(t - 1)
                    to_columns(NT - 1)
                    for n in range(GATES_AT + 2):
                        split_conv(n)
                    dve.wait_ge(s_xb, NT)
                    dve.memset(tap_out, 0.0).then_inc(s_tapc, 1)
                    dve.memset(tap_sum, 0.0).then_inc(s_tapc, 1)
                    dve.wait_ge(s_tapc, 2)
                    for j, (at, width) in enumerate(FULL_SPANS):
                        dve.wait_ge(s_tap, j + 1)
                        for i in range(RC_TAPS):
                            rows_i = slice(32 * i, 32 * i + XE)
                            col = PAD + at - (i - RC_TAPS // 2)
                            dve.tensor_copy(tap_out[rows_i, col:col + width], down[j % 2][rows_i, 0:width]).then_inc(s_tapc, 1)
                            if j == 0:
                                dve.tensor_copy(tap_sum[rows_i, :], ident[rows_i, rows_i])
                    split_conv(GATES_AT + 2)
                    dve.wait_ge(s_iota, 1)
                    step(dve.tensor_copy(number, number_i[:]))
                    for t in range(NT):
                        dve.wait_ge(s_lg, t + 1)
                        dve.tensor_tensor(logits[:, t, :], down[t % 2][:, 0:XE], rc_b2[:], ALU.add).then_inc(s_lgc, 1)
                    dve.wait_ge(s_lgc, NT)

                    def spread(v):
                        return v.unsqueeze(2).broadcast_to([P, NT, XE])

                    for r, hot in enumerate((first, second)):
                        step(dve.tensor_reduce(top[:, r, :], logits[:], AX.X, ALU.max))
                        step(dve.tensor_tensor(place, logits[:], spread(top[:, r, :]), ALU.not_equal))
                        step(dve.scalar_tensor_tensor(out=place, in0=place, scalar=float(XE), in1=number,
                                                      op0=ALU.mult, op1=ALU.add))
                        step(dve.tensor_reduce(which[:], place, AX.X, ALU.min))
                        step(dve.tensor_tensor(hot, number, spread(which[:]), ALU.is_equal))
                        if r == 0:
                            step(dve.scalar_tensor_tensor(out=logits[:], in0=hot, scalar=NEG, in1=logits[:],
                                                          op0=ALU.mult, op1=ALU.add))
                    dve.tensor_tensor(share[:, 0, :], top[:, 1, :], top[:, 0, :], ALU.subtract).then_inc(s_gap, 1)
                    dve.wait_ge(s_gx, 1)
                    step(dve.tensor_scalar(share[:, 0, :], share[:, 1, :], 1.0, None, ALU.add))
                    step(dve.reciprocal(share[:, 0, :], share[:, 0, :]))
                    step(dve.tensor_tensor(share[:, 1, :], share[:, 1, :], share[:, 0, :], ALU.mult))
                    step(dve.tensor_tensor(first, first, spread(share[:, 0, :]), ALU.mult))
                    step(dve.tensor_tensor(second, second, spread(share[:, 1, :]), ALU.mult))
                    step(dve.memset(gates[:, :, XE:XE + 1], 1.0))
                    dve.tensor_tensor(gates[:, :, 0:XE], first, second, ALU.add).then_inc(s_gate, 1)
                    for n in range(GATES_AT + 3, NPOR):
                        split_conv(n)
                    split_expert(0, 0, 0)
                    split_expert(0, 0, 1)
                    split_expert(1, 1, 0)

                    def hidden(b, e, before=None):
                        for i in range(EU + 2):
                            if i < EU:
                                m, n = i // 3, SPANS[i % 3][1]
                                need(dve, s_elu, e * EU + (i - 1))
                                dve.wait_ge(s_act, e * EU + (CONV + i + 1))
                                dve.tensor_scalar(negative[:, i % 2, 0:n], up[i][:, 0:n], e_b1[b][:, m:m + 1], 0.0,
                                                  ALU.add, ALU.min).then_inc(s_low, 1)
                            if before is not None and i >= EU - 1:
                                add(before, i - (EU - 1))
                            if 0 <= i - 2 < EU:
                                m, (at, n) = (i - 2) // 3, SPANS[(i - 2) % 3]
                                dve.wait_ge(s_hh, e * EU + (i - 1))
                                dve.tensor_tensor(h_act[b][1][:, m, at:at + n], hidden_f32[:, (i - 2) % 3, 0:n],
                                                  h_act[b][0][:, m, at:at + n], ALU.subtract).then_inc(s_h, 1)
                            if 0 <= i - 1 < EU:
                                n, r = SPANS[(i - 1) % 3][1], (i - 1) % 3
                                dve.wait_ge(s_ex, e * EU + i)
                                dve.scalar_tensor_tensor(out=hidden_f32[:, r, 0:n], in0=negative[:, (i - 1) % 2, 0:n], scalar=-1.0,
                                                         in1=hidden_f32[:, r, 0:n], op0=ALU.add, op1=ALU.add).then_inc(s_elu, 1)

                    def add(e, t):
                        n = rows(t)
                        dve.wait_ge(s_dn, e * NT + (NT + t + 1))
                        dve.wait_ge(s_add, e * NT + (t + 1))
                        dve.scalar_tensor_tensor(out=yn[0:n, t, :], in0=down[t % 2][0:n, :],
                                                 scalar=gates[0:n, t, bass.ds(e, 1)], in1=yn[0:n, t, :],
                                                 op0=ALU.mult, op1=ALU.add).then_inc(s_add, 1)

                    def hidden_and_add(b, e, before):
                        hidden(b, e, before)
                        for t in range(3, NT):
                            add(before, t)

                    hidden(0, 0)
                    for q in range(3):
                        n = SPANS[q][1]
                        dve.wait_ge(s_gt, q + 1)
                        dve.tensor_copy(gates_t[:, q * 512:q * 512 + n], down[q % 2][0:XE + 1, 0:n]).then_inc(s_gtc, 1)
                    for t in range(NT):
                        n = rows(t)
                        dve.wait_ge(s_dn, t + 1)
                        dve.tensor_tensor(yn[0:n, t, :], yn[0:n, t, :], down[t % 2][0:n, :], ALU.add).then_inc(s_add, 1)
                    split_expert(1, 1, 1)
                    split_expert(0, 2, 0)
                    hidden_and_add(1, 1, 0)
                    split_expert(0, 2, 1)
                    split_expert(1, 3, 0)
                    with dve.Fori(1, XE // 2 - 1) as u:
                        hidden_and_add(0, u * 2, u * 2 - 1)
                        split_expert(1, u * 2 + 1, 1)
                        split_expert(0, u * 2 + 2, 0)
                        hidden_and_add(1, u * 2 + 1, u * 2)
                        split_expert(0, u * 2 + 2, 1)
                        split_expert(1, u * 2 + 3, 0)
                    hidden_and_add(0, XE - 2, XE - 3)
                    split_expert(1, XE - 1, 1)
                    hidden_and_add(1, XE - 1, XE - 2)
                    for t in range(NT + 2):
                        if t < NT:
                            add(XE - 1, t)
                        if 0 <= t - 1 < NT:
                            dve.wait_ge(s_add, XE * NT + t)
                            dve.bn_stats(stats[:, t - 1, :], yn[:, t - 1, :]).then_inc(s_zs, 1)
                        if 0 <= t - 2 < NT:
                            dve.wait_ge(s_zs, t - 1)
                            ins = dve.bn_aggr(mv[:, t - 2, :], stats[:, t - 2, :])
                    ins.then_inc(s_stat, 1)
                    dve.wait_ge(s_std, 2)
                    step(dve.reciprocal(rstd[:], std[:]))
                    for t in range(NT + 1):
                        if t < NT:
                            dve.tensor_scalar(yn[:, t, :], yn[:, t, :], mv[:, t, 0:1], rstd[:, t:t + 1],
                                              ALU.subtract, ALU.mult).then_inc(s_norm, 1)
                        if t:
                            dve.wait_ge(s_norm, t)
                            dve.tensor_tensor(yn[:, t - 1, :], yn[:, t - 1, :], ln_g[:], ALU.mult).then_inc(s_gn, 1)


def lay_out(v):
    import numpy as np
    c = np.ascontiguousarray
    n_pad = EC * P - E
    loops = np.arange(NP, dtype=np.int32)
    tail = np.full(P, NP - 1, np.int32)
    src = np.concatenate([v["src"], np.full(n_pad, NP - 1, np.int32), loops, tail])
    dst = np.concatenate([v["dst"], np.full(n_pad, NP - 1, np.int32), loops, tail])
    attr = np.concatenate([v["edge_attr_4"], np.zeros((n_pad, 4), np.float32)])
    return {
        "x": v["x"],
        "edges": c(np.stack([src.reshape(CH, P).T, dst.reshape(CH, P).T], axis=2)), "dst_row": dst,
        "edge_attr": c(attr.reshape(EC, P, 4).transpose(1, 0, 2)),
        "gat_w": v["L0_gnn_W"], "gat_w_edge": v["L0_gnn_W_edge"], "att_src": v["L0_gnn_att_src"],
        "att_dst": v["L0_gnn_att_dst"], "att_edge": v["L0_gnn_att_edge"], "gat_bias": v["L0_gnn_bias"],
        "gamma": v["L0_gnn_gamma"], "beta": v["L0_gnn_beta"],
        "wq_t": c(v["L0_mix_Wq"].T), "wk_t": c(v["L0_mix_Wk"].T), "wv_t": c(v["L0_mix_Wv"].T), "wo_t": c(v["L0_mix_Wo"].T),
        "bq": v["L0_mix_bq"], "bk": v["L0_mix_bk"], "bv": v["L0_mix_bv"], "bo": v["L0_mix_bo"],
        "rc_w1": c(v["L0_ffn_rc_w1"].reshape(KT, P, D, RC_TAPS).transpose(0, 3, 2, 1)), "rc_b1": v["L0_ffn_rc_b1"],
        "rc_w2": c(v["L0_ffn_rc_w2"].transpose(2, 1, 0)), "rc_b2": v["L0_ffn_rc_b2"],
        "sh_w1": c(v["L0_ffn_sh_w1"].reshape(HT, P, D, SH_TAPS).transpose(0, 3, 2, 1)), "sh_b1": v["L0_ffn_sh_b1"],
        "sh_w2": c(v["L0_ffn_sh_w2"][:, :, 0].T), "sh_b2": v["L0_ffn_sh_b2"],
        "e_w1": v["L0_ffn_e_w1"], "e_b1_cols": c(v["L0_ffn_e_b1"].reshape(XE, HT, P).transpose(0, 2, 1)), "e_w2": v["L0_ffn_e_w2"], "e_b2": v["L0_ffn_e_b2"],
        "ln_g": v["L0_ffn_ln_g"], "ln_b": v["L0_ffn_ln_b"],
    }


def kernel(**inputs):
    import numpy as np
    import concourse.bacc as bacc
    from concourse.bass_utils import run_bass_kernel_spmd

    nc = bacc.Bacc("TRN2", target_bir_lowering=False, num_devices=1)
    laid = lay_out({name: np.asarray(v) for name, v in inputs.items()})
    arrays = {f"in_{name}": np.ascontiguousarray(v) for name, v in laid.items()}
    ins = {name: nc.dram_tensor(f"in_{name}", v.shape, mybir.dt.from_np(v.dtype), kind="ExternalInput").ap()
           for name, v in laid.items()}
    out = nc.dram_tensor("out_0_dram", (N, D), F32, kind="ExternalOutput").ap()
    layer(nc, ins, out)
    result = run_bass_kernel_spmd(nc, [arrays], core_ids=[0])
    return result.results[0]["out_0_dram"]
```
